# Optimizing a Trainium2 kernel written in Bass

```python
import numpy as np
import jax
import jax.numpy as jnp

def _softmax(x, axis=-1):
    return jax.nn.softmax(x, axis=axis)

def _gelu(x):
    return jax.nn.gelu(x, approximate=True)

def _silu(x):
    return jax.nn.silu(x)

def _sigmoid(x):
    return jax.nn.sigmoid(x)

def _layernorm(x, axis=-1, eps=1e-05):
    m = jnp.mean(x, axis=axis, keepdims=True)
    v = jnp.var(x, axis=axis, keepdims=True)
    return (x - m) / jnp.sqrt(v + eps)

def _scatter_add(tgt, idx, src, axis=0):
    return tgt.at[idx].add(src)

def _segment_sum(src, seg, n):
    return jax.ops.segment_sum(src, seg, n)
kernel_name = 'mk_lm_tower_d1_tok_ids256_r4_5f1f42'

def setup_inputs(seed: int=0):
    np.random.seed(seed)
    _w = jnp.asarray

    def _rec_inputs():
        import jax
        import jax.numpy as jnp
        _rk = jax.random.key(seed)
        x = jax.random.randint(jax.random.fold_in(_rk, 1), (32, 512), 0, 64, jnp.int32)
        return x
    x = _rec_inputs()

    def _L0_tok_setup():
        import jax, jax.numpy as jnp
        import numpy as np
        BATCH = 32
        SEQ = 1024
        HID = 64
        VOCAB = 8000
        NEXT_ID = 5
        EPS = 1e-05

        def _positions(state):
            eq = state == NEXT_ID
            starts = jnp.pad(eq[:, :-1], ((0, 0), (1, 0)))
            instr = jnp.cumsum(starts.astype(jnp.int32), axis=-1)
            pos = jnp.arange(state.shape[-1], dtype=jnp.int32)
            seg_start = jnp.where(starts, pos[None, :], 0)
            last_start = jax.lax.cummax(seg_start, axis=1)
            args = pos[None, :] - last_start
            return (instr, args)
        key = jax.random.key(seed)
        ks = jax.random.split(key, 6)
        state = jax.random.randint(ks[0], (BATCH, SEQ), 0, 64, dtype=jnp.int64)
        token_emb = jax.random.normal(ks[1], (VOCAB, HID), dtype=jnp.float32) * 0.02
        instr_emb = jax.random.normal(ks[2], (SEQ, HID), dtype=jnp.float32) * 0.02
        arg_emb = jax.random.normal(ks[3], (SEQ, HID), dtype=jnp.float32) * 0.02
        gamma = jnp.ones((HID,), dtype=jnp.float32)
        beta = jnp.zeros((HID,), dtype=jnp.float32)
        return {'state': state, 'token_emb': token_emb, 'instr_emb': instr_emb, 'arg_emb': arg_emb, 'gamma': gamma, 'beta': beta}
    _L0_tok_all = _L0_tok_setup()
    _L0_tok_in = {k: v for k, v in _L0_tok_all.items() if k in ('token_emb', 'instr_emb', 'arg_emb', 'gamma', 'beta')}
    del _L0_tok_all

    def _L0_attn_setup():
        import jax, jax.numpy as jnp
        import numpy as np
        D = 64
        L = 2
        B, S = (8, 1024)
        LR = 0.001
        WD = 0.01
        MAX_ALR = 0.1
        EPS = 1e-08

        def _lmm(Ws, bs, x):
            for i in range(L):
                x = x + jax.nn.silu(x @ Ws[i] + bs[i])
            return x

        def _reference_tuple_inner(x, Wk, Wq, Wv, Wlr, blr, Ws, bs):
            keys = x @ Wk
            queries = x @ Wq
            values = x @ Wv
            alr = (jax.nn.sigmoid(x @ Wlr + blr) * MAX_ALR).reshape(-1)

            def loss_fn(params):
                Ws_, bs_ = params
                preds = _lmm(Ws_, bs_, keys).reshape(-1, D)
                tgt = values.reshape(-1, D)
                per_tok = jnp.mean((preds - tgt) ** 2, axis=-1)
                return jnp.sum(per_tok * alr)
            gWs, gbs = jax.grad(loss_fn)((Ws, bs))

            def adamw_step(p, g):
                return p * (1.0 - LR * WD) - LR * g / (jnp.sqrt(g * g) + EPS)
            nWs = adamw_step(Ws, gWs)
            nbs = adamw_step(bs, gbs)
            retrieved = _lmm(nWs, nbs, queries)
            return (retrieved, -gWs, -gbs)
        key = jax.random.key(seed)
        ks = jax.random.split(key, 9)
        scale = 0.05
        return {'x': jax.random.normal(ks[0], (B, S, D), dtype=jnp.float32), 'Wk': jax.random.normal(ks[1], (D, D), dtype=jnp.float32) * scale, 'Wq': jax.random.normal(ks[2], (D, D), dtype=jnp.float32) * scale, 'Wv': jax.random.normal(ks[3], (D, D), dtype=jnp.float32) * scale, 'Wlr': jax.random.normal(ks[4], (D, 1), dtype=jnp.float32) * scale, 'blr': jnp.zeros((1,), dtype=jnp.float32), 'Ws': jax.random.normal(ks[5], (L, D, D), dtype=jnp.float32) * scale, 'bs': jnp.zeros((L, D), dtype=jnp.float32)}
    _L0_attn_all = _L0_attn_setup()
    _L0_attn_in = {k: v for k, v in _L0_attn_all.items() if k in ('Wk', 'Wq', 'Wv', 'Wlr', 'blr', 'Ws', 'bs')}
    del _L0_attn_all

    def _L0_ffn_setup():
        import jax, jax.numpy as jnp
        import numpy as np
        B, T, C = (64, 96, 64)
        NH, NKV = (4, 2)
        HD = C // NH
        NREP = NH // NKV
        NE, TOPK = (8, 2)
        HID = int(8 / 3 * C)
        EPS_RMS = 1e-06

        def _rope_tables(t_len):
            inv_freq = 1.0 / 10000.0 ** (np.arange(0, HD, 2, dtype=np.float32) / HD)
            t = np.arange(t_len, dtype=np.float32)
            freqs = np.outer(t, inv_freq)
            emb = np.concatenate([freqs, freqs], axis=-1)
            return (jnp.asarray(np.cos(emb)), jnp.asarray(np.sin(emb)))

        def _rotate_half(x):
            h = x.shape[-1] // 2
            return jnp.concatenate([-x[..., h:], x[..., :h]], axis=-1)

        def _rmsnorm(v, w):
            return v * jax.lax.rsqrt(jnp.mean(v * v, axis=-1, keepdims=True) + EPS_RMS) * w
        key = jax.random.key(seed)
        ks = jax.random.split(key, 10)
        s = lambda k, shape: jax.random.normal(k, shape, jnp.float32) * 0.02
        return {'x': jax.random.normal(ks[0], (B, T, C), jnp.float32), 'ln1_w': jnp.ones((C,), jnp.float32), 'ln2_w': jnp.ones((C,), jnp.float32), 'wq': s(ks[1], (NH * HD, C)), 'wk': s(ks[2], (NKV * HD, C)), 'wv': s(ks[3], (NKV * HD, C)), 'wo': s(ks[4], (C, C)), 'router_w': s(ks[5], (NE, C)), 'w1': s(ks[6], (NE, HID, C)), 'w2': s(ks[7], (NE, C, HID)), 'w3': s(ks[8], (NE, HID, C))}
    _L0_ffn_all = _L0_ffn_setup()
    _L0_ffn_in = {k: v for k, v in _L0_ffn_all.items() if k in ('ln1_w', 'ln2_w', 'wq', 'wk', 'wv', 'wo', 'router_w', 'w1', 'w2', 'w3')}
    del _L0_ffn_all
    return {'x': x, 'L0_tok_token_emb': _L0_tok_in['token_emb'], 'L0_tok_instr_emb': _L0_tok_in['instr_emb'], 'L0_tok_arg_emb': _L0_tok_in['arg_emb'], 'L0_tok_gamma': _L0_tok_in['gamma'], 'L0_tok_beta': _L0_tok_in['beta'], 'L0_attn_Wk': _L0_attn_in['Wk'], 'L0_attn_Wq': _L0_attn_in['Wq'], 'L0_attn_Wv': _L0_attn_in['Wv'], 'L0_attn_Wlr': _L0_attn_in['Wlr'], 'L0_attn_blr': _L0_attn_in['blr'], 'L0_attn_Ws': _L0_attn_in['Ws'], 'L0_attn_bs': _L0_attn_in['bs'], 'L0_ffn_ln1_w': _L0_ffn_in['ln1_w'], 'L0_ffn_ln2_w': _L0_ffn_in['ln2_w'], 'L0_ffn_wq': _L0_ffn_in['wq'], 'L0_ffn_wk': _L0_ffn_in['wk'], 'L0_ffn_wv': _L0_ffn_in['wv'], 'L0_ffn_wo': _L0_ffn_in['wo'], 'L0_ffn_router_w': _L0_ffn_in['router_w'], 'L0_ffn_w1': _L0_ffn_in['w1'], 'L0_ffn_w2': _L0_ffn_in['w2'], 'L0_ffn_w3': _L0_ffn_in['w3']}

def reference(x, L0_tok_token_emb, L0_tok_instr_emb, L0_tok_arg_emb, L0_tok_gamma, L0_tok_beta, L0_attn_Wk, L0_attn_Wq, L0_attn_Wv, L0_attn_Wlr, L0_attn_blr, L0_attn_Ws, L0_attn_bs, L0_ffn_ln1_w, L0_ffn_ln2_w, L0_ffn_wq, L0_ffn_wk, L0_ffn_wv, L0_ffn_wo, L0_ffn_router_w, L0_ffn_w1, L0_ffn_w2, L0_ffn_w3):
    import jax
    import jax.numpy as jnp

    def _L0_tok_ref(state, token_emb, instr_emb, arg_emb, gamma, beta):
        import jax, jax.numpy as jnp
        import numpy as np
        BATCH = 32
        SEQ = 1024
        HID = 64
        VOCAB = 8000
        NEXT_ID = 5
        EPS = 1e-05

        def _positions(state):
            eq = state == NEXT_ID
            starts = jnp.pad(eq[:, :-1], ((0, 0), (1, 0)))
            instr = jnp.cumsum(starts.astype(jnp.int32), axis=-1)
            pos = jnp.arange(state.shape[-1], dtype=jnp.int32)
            seg_start = jnp.where(starts, pos[None, :], 0)
            last_start = jax.lax.cummax(seg_start, axis=1)
            args = pos[None, :] - last_start
            return (instr, args)
        instr, args = _positions(state)
        embedded = token_emb[state] + instr_emb[instr] + arg_emb[args]
        mean = jnp.mean(embedded, axis=-1, keepdims=True)
        var = jnp.mean(jnp.square(embedded - mean), axis=-1, keepdims=True)
        normed = (embedded - mean) * jax.lax.rsqrt(var + EPS)
        return normed * gamma + beta

    def _L0_attn_ref(x, Wk, Wq, Wv, Wlr, blr, Ws, bs):
        import jax, jax.numpy as jnp
        import numpy as np
        D = 64
        L = 2
        B, S = (8, 1024)
        LR = 0.001
        WD = 0.01
        MAX_ALR = 0.1
        EPS = 1e-08

        def _lmm(Ws, bs, x):
            for i in range(L):
                x = x + jax.nn.silu(x @ Ws[i] + bs[i])
            return x

        def _reference_tuple_inner(x, Wk, Wq, Wv, Wlr, blr, Ws, bs):
            keys = x @ Wk
            queries = x @ Wq
            values = x @ Wv
            alr = (jax.nn.sigmoid(x @ Wlr + blr) * MAX_ALR).reshape(-1)

            def loss_fn(params):
                Ws_, bs_ = params
                preds = _lmm(Ws_, bs_, keys).reshape(-1, D)
                tgt = values.reshape(-1, D)
                per_tok = jnp.mean((preds - tgt) ** 2, axis=-1)
                return jnp.sum(per_tok * alr)
            gWs, gbs = jax.grad(loss_fn)((Ws, bs))

            def adamw_step(p, g):
                return p * (1.0 - LR * WD) - LR * g / (jnp.sqrt(g * g) + EPS)
            nWs = adamw_step(Ws, gWs)
            nbs = adamw_step(bs, gbs)
            retrieved = _lmm(nWs, nbs, queries)
            return (retrieved, -gWs, -gbs)
        return _reference_tuple_inner(x, Wk, Wq, Wv, Wlr, blr, Ws, bs)[0]

    def _L0_ffn_ref(x, ln1_w, ln2_w, wq, wk, wv, wo, router_w, w1, w2, w3):
        import jax, jax.numpy as jnp
        import numpy as np
        B, T, C = (64, 96, 64)
        NH, NKV = (4, 2)
        HD = C // NH
        NREP = NH // NKV
        NE, TOPK = (8, 2)
        HID = int(8 / 3 * C)
        EPS_RMS = 1e-06

        def _rope_tables(t_len):
            inv_freq = 1.0 / 10000.0 ** (np.arange(0, HD, 2, dtype=np.float32) / HD)
            t = np.arange(t_len, dtype=np.float32)
            freqs = np.outer(t, inv_freq)
            emb = np.concatenate([freqs, freqs], axis=-1)
            return (jnp.asarray(np.cos(emb)), jnp.asarray(np.sin(emb)))

        def _rotate_half(x):
            h = x.shape[-1] // 2
            return jnp.concatenate([-x[..., h:], x[..., :h]], axis=-1)

        def _rmsnorm(v, w):
            return v * jax.lax.rsqrt(jnp.mean(v * v, axis=-1, keepdims=True) + EPS_RMS) * w
        Bx, Tx, Cx = x.shape
        h = _rmsnorm(x, ln1_w)
        q = (h @ wq.T).reshape(Bx, Tx, NH, HD).transpose(0, 2, 1, 3)
        k = (h @ wk.T).reshape(Bx, Tx, NKV, HD).transpose(0, 2, 1, 3)
        v = (h @ wv.T).reshape(Bx, Tx, NKV, HD).transpose(0, 2, 1, 3)
        cos, sin = _rope_tables(Tx)
        cos, sin = (cos[None, None], sin[None, None])
        q = q * cos + _rotate_half(q) * sin
        k = k * cos + _rotate_half(k) * sin
        k = jnp.repeat(k, NREP, axis=1)
        v = jnp.repeat(v, NREP, axis=1)
        scores = jnp.einsum('bhtd,bhsd->bhts', q, k) / jnp.sqrt(jnp.float32(HD))
        causal = jnp.tril(jnp.ones((Tx, Tx), dtype=bool))
        scores = jnp.where(causal[None, None], scores, jnp.float32(-1e+30))
        att = jax.nn.softmax(scores, axis=-1)
        y = jnp.einsum('bhts,bhsd->bhtd', att, v).transpose(0, 2, 1, 3).reshape(Bx, Tx, Cx)
        x = x + y @ wo.T
        flat = _rmsnorm(x, ln2_w).reshape(-1, Cx)
        probs = jax.nn.softmax(flat @ router_w.T, axis=-1)
        tp, ti = jax.lax.top_k(probs, TOPK)
        tp = tp / (jnp.sum(tp, axis=-1, keepdims=True) + 1e-09)
        weights = jnp.sum(tp[..., None] * jax.nn.one_hot(ti, NE, dtype=flat.dtype), axis=1)
        out = jnp.zeros_like(flat)
        for e in range(NE):
            hh = jax.nn.silu(flat @ w1[e].T) * (flat @ w3[e].T)
            out = out + weights[:, e:e + 1] * (hh @ w2[e].T)
        return x + out.reshape(Bx, Tx, Cx)
    h = _L0_tok_ref(x, L0_tok_token_emb, L0_tok_instr_emb, L0_tok_arg_emb, L0_tok_gamma, L0_tok_beta)
    h = h + _L0_attn_ref(_layernorm(h, axis=-1), L0_attn_Wk, L0_attn_Wq, L0_attn_Wv, L0_attn_Wlr, L0_attn_blr, L0_attn_Ws, L0_attn_bs)
    h = h + _L0_ffn_ref(_layernorm(h, axis=-1), L0_ffn_ln1_w, L0_ffn_ln2_w, L0_ffn_wq, L0_ffn_wk, L0_ffn_wv, L0_ffn_wo, L0_ffn_router_w, L0_ffn_w1, L0_ffn_w2, L0_ffn_w3)
    return h

_drawn_inputs = setup_inputs


def setup_inputs(seed=0):
    import zlib

    import numpy as np

    out = dict(_drawn_inputs(seed))
    spreads = {'L0_tok_gamma': (1.0, 0.2),
     'L0_tok_beta': (0.0, 0.1),
     'L0_attn_bs': (0.0, 0.1),
     'L0_ffn_ln1_w': (1.0, 0.6),
     'L0_ffn_ln2_w': (1.0, 0.6)}
    factors = {'L0_attn_Wk': 8.0,
     'L0_attn_Wv': 8.0,
     'L0_attn_Wlr': 8.0,
     'L0_ffn_wq': 8.0,
     'L0_ffn_wk': 8.0,
     'L0_ffn_wv': 8.0,
     'L0_ffn_wo': 8.0,
     'L0_ffn_router_w': 8.0,
     'L0_ffn_w1': 8.0,
     'L0_ffn_w2': 8.0,
     'L0_ffn_w3': 8.0}
    for name, (base, spread) in spreads.items():
        noise = np.random.default_rng([zlib.crc32(name.encode()), seed]).standard_normal(out[name].shape)
        drawn = base * np.exp(spread * noise) if base else spread * noise
        out[name] = jnp.asarray(drawn.astype(out[name].dtype))
    for name, factor in factors.items():
        out[name] = (out[name] * factor).astype(out[name].dtype)
    return out
```

```python
from contextlib import ExitStack

import numpy as np
import concourse.bass as bass
from concourse import mybir

F32 = mybir.dt.float32
F16 = mybir.dt.float16
BF16 = mybir.dt.bfloat16
I32 = mybir.dt.int32
ALU = mybir.AluOpType
ACT = mybir.ActivationFunctionType
AX_X = mybir.AxisListType.X

P = 128
ROWS, SEQ, D = 32, 512, 64
PAIRS = ROWS // 2
BLK = SEQ // P
NEXT_ID = 5
EPS_LN, EPS_RMS = 1e-5, 1e-6
LR, WD, MAX_ALR, EPS_ADAM = 0.001, 0.01, 0.1, 1e-8
HEADS, KV, HD = 4, 2, 16
EXPERTS, HID = 8, 170
NEG = -1e30

WIDTH = [SEQ - P * c for c in range(BLK)]
START = [sum(WIDTH[:c]) for c in range(BLK)]
TRAP = sum(WIDTH)

C_ID, C_CENTRE, C_MEAN, C_FOLD, C_DEN = (P * j for j in range(5))
C_IOTA = 5 * P
C_EPS_LN, C_EPS_RMS = C_IOTA + BLK, C_IOTA + BLK + 1
C_RANK = C_EPS_RMS + 1
C_COLS = C_RANK + EXPERTS


def shape_constants():
    p = np.arange(P)
    same_half = (p[:, None] // D == p[None, :] // D).astype(np.float32)
    c = np.zeros((P, C_COLS), np.float32)
    c[:, C_ID:C_ID + P] = np.eye(P)
    c[:, C_CENTRE:C_CENTRE + P] = np.eye(P) - same_half / D
    c[:, C_MEAN:C_MEAN + P] = same_half / D
    c[:, C_FOLD:C_FOLD + P] = p[:, None] % D == p[None, :] % D
    c[:, C_DEN:C_DEN + P] = (p[:, None] // 32 == p[None, :] // 32) & (p[:, None] % 32 == HD)
    c[:, C_IOTA:C_IOTA + BLK] = p[:, None] + P * np.arange(BLK)[None, :]
    c[:, C_EPS_LN] = EPS_LN
    c[:, C_EPS_RMS] = EPS_RMS
    c[:, C_RANK:C_RANK + EXPERTS] = EXPERTS - np.arange(EXPERTS)
    position = np.tile(np.arange(SEQ, dtype=np.float32), (ROWS, 1))
    inv_freq = 1.0 / 10000.0 ** (np.arange(0, HD, 2, dtype=np.float32) / HD)
    angle = np.outer(np.arange(SEQ, dtype=np.float32), inv_freq)
    angle = np.concatenate([angle, angle], axis=-1)
    sign = np.where(np.arange(HD) < HD // 2, -1.0, 1.0).astype(np.float32)
    cos, sin = np.cos(angle).T, np.sin(angle).T * sign[:, None]
    scale = np.float32(HD ** -0.5)
    turn = np.stack([cos * scale, sin * scale, cos, sin], axis=1)
    turn = np.tile(turn, (P // HD, 1, 1)).astype(np.float32)
    causal = np.where(p[:, None] <= p[None, :], 0.0, NEG).astype(np.float32)
    return {"consts": c, "position": position, "turn": np.ascontiguousarray(turn), "causal": causal}


def wait(eng, sem, count):
    if isinstance(count, int) and count <= 0:
        return
    eng.wait_ge(sem, count)


def live(n, stage, tiles):
    return not isinstance(n, int) or 0 <= n - stage < tiles


def pipeline(eng, tiles, stages, ring=2, first=0):
    first = first or (stages + ring) // ring * ring
    for n in range(first):
        yield n, n % ring, n // ring
    with eng.Fori(first // ring, tiles // ring) as i:
        for u in range(ring):
            yield ring * i + u, u, i
    for n in range(tiles, tiles + stages - 1):
        yield n, n % ring, n // ring


def turns(i, u, stage=0, ring=2):
    return i + (u - stage) // ring + 1



(W_K, W_Q, W_V, W_LR, W_0, W_1, W_1T, W_FQ, W_FQR) = (P * j for j in range(9))
W_01 = 9 * P
W_FK, W_FKR, W_FV, W_O = (W_01 + P + D * j for j in range(4))
W_ROUTE = W_O + D
V_GAMMA, V_BETA, V_B0, V_B1, V_BLR, V_LN1, V_LN2 = (W_ROUTE + 2 * EXPERTS + j for j in range(7))
W_COLS = V_LN2 + 1


def diagonal(w):
    k, m = w.shape
    out = np.zeros((2 * k, 2 * m), np.float32)
    out[:k, :m] = w
    out[k:, m:] = w
    return out


def twice(w):
    return np.concatenate([w, w], axis=0)


def pack_weights(a):
    ws, bs = a["L0_attn_Ws"], a["L0_attn_bs"]
    swap = np.arange(D).reshape(-1, 2, HD // 2)[:, ::-1].reshape(-1)
    fq, fk, fv = a["L0_ffn_wq"].T, a["L0_ffn_wk"].T, a["L0_ffn_wv"].T
    wo = np.zeros((P, D), np.float32)
    for h in range(HEADS):
        wo[32 * h:32 * h + HD] = a["L0_ffn_wo"].T[HD * h:HD * (h + 1)]
    vectors = [a["L0_tok_gamma"], a["L0_tok_beta"], bs[0], bs[1], np.repeat(a["L0_attn_blr"], D),
               a["L0_ffn_ln1_w"], a["L0_ffn_ln2_w"]]
    parts = [diagonal(w) for w in (a["L0_attn_Wk"], a["L0_attn_Wq"], a["L0_attn_Wv"],
                                   np.repeat(a["L0_attn_Wlr"], D, axis=1), ws[0], ws[1], ws[1].T,
                                   fq, fq[:, swap])]
    parts += [twice(ws[0]), twice(ws[1])]
    parts += [diagonal(w) for w in (fk, fk[:, swap[:KV * HD]], fv)]
    parts += [wo, diagonal(a["L0_ffn_router_w"].T)]
    parts += [twice(v[:, None]) for v in vectors]
    return np.ascontiguousarray(np.concatenate(parts, axis=1))


def tower(nc, ids, token_emb, place_emb, weights, w13, w2, consts, position, turn, causal, out):
    ctx = ExitStack()
    with ctx:
        def sb(name, shape, dt=F32):
            return ctx.enter_context(nc.sbuf_tensor(name, shape, dt))

        sems = []

        def sem(name):
            sems.append(nc.alloc_semaphore(name=name))
            return sems[-1]

        def recycle():
            nc.all_engine_barrier()
            nc.clear_and_free_semaphores(sems)
            sems.clear()
            nc.all_engine_barrier()

        banks = [ctx.enter_context(nc.psum_tensor(f"bank{j}", [P, SEQ], F32)) for j in range(8)]

        H = sb("H", [P, PAIRS, SEQ])
        XN = sb("XN", [P, PAIRS, SEQ])
        CST = sb("CST", [P, C_COLS])
        W = sb("W", [P, W_COLS])

        def wcols(at, cols=P):
            return W[:, at:at + cols]

        def vec(at):
            return W[:, at:at + 1]

        ident = CST[:, C_ID:C_ID + P]
        centre = CST[:, C_CENTRE:C_CENTRE + P]
        mean = CST[:, C_MEAN:C_MEAN + P]
        fold = CST[:, C_FOLD:C_FOLD + P]
        eps_ln = CST[:, C_EPS_LN:C_EPS_LN + 1]
        eps_rms = CST[:, C_EPS_RMS:C_EPS_RMS + 1]

        embed(nc, sb, sem, banks, ids, token_emb, place_emb, weights, consts, position,
              H, XN, CST, W, ident, centre, mean, eps_ln, vec)
        with ExitStack() as inner:
            NW, NB = learn(nc, inner, sem, banks, XN, W, wcols, vec, ident, fold)
            retrieve(nc, inner, sem, banks, XN, H, W, wcols, NW, NB)
        recycle()
        with ExitStack() as inner:
            VT = inner.enter_context(nc.sbuf_tensor("VT", [P, PAIRS, BLK * 2 * KV * HD], F32))
            q_parts = nc.dram_tensor("q_parts", [3, PAIRS, P, SEQ], BF16, kind="Internal").ap()
            k_parts = nc.dram_tensor("k_parts", [3, PAIRS, 2 * KV * HD, SEQ], BF16, kind="Internal").ap()
            project(nc, sem, banks, H, XN, W, VT, q_parts, k_parts, turn, centre, mean, eps_ln, eps_rms, vec)
            attend(nc, sem, banks, H, XN, W, CST, VT, q_parts, k_parts, causal, ident)
        recycle()
        with ExitStack() as inner:
            FS = inner.enter_context(nc.sbuf_tensor("FS", [P, ROWS, SEQ], F16))
            gates = nc.dram_tensor("gates", [PAIRS, 2, EXPERTS, SEQ], F32, kind="Internal").ap()
            route(nc, sem, banks, XN, W, CST, FS, gates, ident, mean, eps_rms, vec)
            experts(nc, sem, banks, H, W, FS, gates, w13, w2, out, ident, vec)


def embed(nc, sb_, sem, banks, ids, token_emb, place_emb, weights, consts, position,
          H, XN, CST, W, ident, centre, mean, eps_ln, vec):
    ids16 = nc.dram_tensor("ids16", [2, ROWS, SEQ], F16, kind="Internal").ap()
    with ExitStack() as ctx:
        def sb(name, shape, dt=F32):
            return ctx.enter_context(nc.sbuf_tensor(name, shape, dt))

        pos = sb("pos", [ROWS, SEQ])
        xi = sb("xi", [ROWS, SEQ], I32)
        xf = sb("xf", [ROWS, SEQ])
        starts = sb("starts", [ROWS, SEQ])
        ones = sb("ones", [ROWS, SEQ])
        seg = sb("seg", [ROWS, SEQ])
        last = sb("last", [ROWS, SEQ])
        place16 = sb("place16", [ROWS, 2, SEQ], F16)
        tokid = sb("tokid", [P, PAIRS, BLK * 2], I32)
        pemb = sb("pemb", [P, 2 * BLK, D])
        prest = sb("prest", [P, 2 * BLK, D])
        table = sb("table", [P, 3, 2 * BLK, D], BF16)
        tokcol = sb("tokcol", [P, 2, BLK * 2], I32)
        tok = sb("tok", [P, 2, BLK, 2, D])
        where = sb("where", [P, 2, 2, 2, SEQ], F16)
        onehot = sb("onehot", [P, 2, 2, 2 * TRAP], BF16)
        x = sb("x", [P, 2, SEQ])
        sq1, sq2, ln1, ln2, r1, r2 = (sb(n, [P, SEQ]) for n in ("sq1", "sq2", "ln1", "ln2", "r1", "r2"))
        normed = sb("normed", [P, SEQ])

        loaded, xloaded, ploaded = sem("loaded"), sem("xloaded"), sem("ploaded")
        step, ids_turned, tok_ready, places_stored = sem("step"), sem("ids_turned"), sem("tok_ready"), sem("places_stored")
        places_ready, table_ready, table_step = sem("places_ready"), sem("table_ready"), sem("table_step")
        col_ready, col_seen, gathered = sem("col_ready"), sem("col_seen"), [sem(f"gathered{u}") for u in range(2)]
        where_loaded, onehot_ready, embedded, x_ready = [sem(f"where_loaded{u}") for u in range(2)], sem("onehot_ready"), sem("embedded"), sem("x_ready")
        c1_done, sq1_done, v1_done, ln1_done, r1_done, n1_done, h_done = (sem(f"{n}_a") for n in ("c", "sq", "v", "ln", "r", "n", "h"))
        c2_done, sq2_done, v2_done, ln2_done, r2_done, xn_done = (sem(f"{n}_b") for n in ("c", "sq", "v", "ln", "r", "xn"))

        ps_x, ps_c1, ps_c2, ps_v1, ps_v2 = banks[0], banks[1:3], banks[3:5], banks[5], banks[6]
        ids_turn = banks[7]
        STAGES = 4

        with nc.Block() as block:
            @block.sync
            def _(sp):
                sp.dma_start(xi[:, :], ids).then_inc(xloaded, 16)
                sp.dma_start(pos[:, :], position).then_inc(xloaded, 16)
                sp.dma_start(CST[:, :], consts).then_inc(loaded, 16)
                sp.dma_start(pemb[:, :, :], place_emb).then_inc(ploaded, 16)
                sp.dma_start(W[:, :], weights).then_inc(loaded, 16)
                sp.wait_ge(places_ready, 2)
                sp.dma_start(ids16.rearrange("t r s -> r t s"), place16[:, :, :]).then_inc(places_stored, 16)
                sp.wait_ge(places_stored, 16)
                for n, u, i in pipeline(sp, PAIRS, STAGES):
                    if live(n, 0, PAIRS):
                        wait(sp, onehot_ready, n - 1)
                        sp.dma_start(where[:, u], ids16[:, bass.ds(2 * n, 2), :].partition_broadcast(P)).then_inc(where_loaded[u], 16)

            @block.gpsimd
            def _(pool):
                pool.wait_ge(tok_ready, 1)
                for n, u, i in pipeline(pool, PAIRS, STAGES):
                    if live(n, 0, PAIRS):
                        wait(pool, embedded, n - 1)
                        pool.sem_inc(col_seen, 1)
                        pool.tensor_copy(tokcol[:, u, :], tokid[:, bass.ds(n, 1), :].rearrange("p a b -> p (a b)")).then_inc(col_ready, 1)
                        wait(pool, col_ready, n + 1)
                        pool.sem_inc(col_seen, 1)
                        for q in range(BLK):
                            for a in range(2):
                                pool.indirect_dma_start(
                                    out=tok[:, u, q, a, :], out_offset=None, in_=token_emb,
                                    in_offset=bass.IndirectOffsetOnAxis(ap=tokcol[:, u, 2 * q + a:2 * q + a + 1], axis=0),
                                ).then_inc(gathered[u], 16)

            @block.vector
            def _(dve):
                count = [0]

                def then(ins):
                    count[0] += 1
                    ins.then_inc(step, 1)
                    dve.wait_ge(step, count[0])

                then(dve.memset(ones[:, :], 1.0))
                then(dve.memset(starts[:, :], 0.0))
                dve.wait_ge(xloaded, 32)
                then(dve.tensor_copy(xf[:, :], xi[:, :]))
                then(dve.tensor_scalar(starts[:, 1:SEQ], xf[:, 0:SEQ - 1], float(NEXT_ID), None, ALU.is_equal))
                dve.tensor_tensor_scan(place16[:, 0, :], ones[:, :], starts[:, :], 0.0, ALU.mult, ALU.add).then_inc(places_ready, 1)
                then(dve.tensor_tensor(seg[:, :], starts[:, :], pos[:, :], ALU.mult))
                then(dve.tensor_tensor_scan(last[:, :], seg[:, :], seg[:, :], 0.0, ALU.max, ALU.max))
                dve.tensor_tensor(place16[:, 1, :], pos[:, :], last[:, :], ALU.subtract).then_inc(places_ready, 1)
                dve.wait_ge(ids_turned, BLK)
                dve.tensor_copy(tokid[:, :, :].rearrange("p m (q a) -> p q m a", a=2),
                                ids_turn[:, 0:BLK * ROWS].rearrange("p (q m a) -> p q m a", q=BLK, a=2)).then_inc(tok_ready, 1)
                dve.wait_ge(ploaded, 16)
                then(dve.tensor_copy(table[:, 0], pemb[:, :, :]))
                then(dve.tensor_tensor(prest[:, :, :], pemb[:, :, :], table[:, 0], ALU.subtract))
                then(dve.tensor_copy(table[:, 1], prest[:, :, :]))
                dve.tensor_tensor(table[:, 2], prest[:, :, :], table[:, 1], ALU.subtract).then_inc(table_ready, 1)
                dve.wait_ge(loaded, 32)
                for n, u, i in pipeline(dve, PAIRS, STAGES):
                    if live(n, 0, PAIRS):
                        dve.wait_ge(where_loaded[u], turns(i, u) * 16)
                        wait(dve, embedded, n - 1)
                        for t in range(2):
                            for c in range(BLK):
                                at, w = 2 * START[c], WIDTH[c]
                                mark = dve.tensor_scalar(
                                    onehot[:, u, t, at:at + 2 * w].rearrange("p (a s) -> p a s", a=2),
                                    where[:, u, t, :, SEQ - w:], CST[:, C_IOTA + c:C_IOTA + c + 1], None, ALU.is_equal)
                        mark.then_inc(onehot_ready, 1)
                    if live(n, 2, PAIRS):
                        m = n - 2
                        dve.wait_ge(r1_done, m + 1)
                        wait(dve, h_done, m)
                        dve.tensor_tensor(normed[:, :], ps_c1[u][:, :], r1[:, :], ALU.mult).then_inc(n1_done, 1)
                        dve.wait_ge(n1_done, m + 1)
                        dve.tensor_scalar(H[:, bass.ds(m, 1), :].rearrange("p a s -> p (a s)"), normed[:, :], vec(V_GAMMA), vec(V_BETA), ALU.mult, ALU.add).then_inc(h_done, 1)
                    if live(n, 3, PAIRS):
                        m, v = n - 3, 1 - u
                        dve.wait_ge(r2_done, m + 1)
                        dve.tensor_tensor(XN[:, bass.ds(m, 1), :].rearrange("p a s -> p (a s)"), ps_c2[v][:, :], r2[:, :], ALU.mult).then_inc(xn_done, 1)

            @block.tensor
            def _(pe):
                pe.wait_ge(loaded, 32)
                pe.wait_ge(step, 3)
                for q in range(BLK):
                    pe.transpose(ids_turn[:, q * ROWS:(q + 1) * ROWS], xf[:, q * P:(q + 1) * P], ident[0:ROWS, 0:ROWS]).then_inc(ids_turned, 1)
                pe.wait_ge(table_ready, 1)
                for n, u, i in pipeline(pe, PAIRS, STAGES):
                    if live(n, 2, PAIRS):
                        m = n - 2
                        pe.wait_ge(x_ready, m + 1)
                        wait(pe, n1_done, m - 1)
                        pe.matmul(ps_c1[u][:, :], centre, x[:, u, :], start=True, stop=True).then_inc(c1_done, 1)
                    if live(n, 3, PAIRS):
                        m, v = n - 3, 1 - u
                        pe.wait_ge(h_done, m + 1)
                        wait(pe, xn_done, m - 1)
                        pe.matmul(ps_c2[v][:, :], centre, H[:, bass.ds(m, 1), :].rearrange("p a s -> p (a s)"), start=True, stop=True).then_inc(c2_done, 1)
                    if live(n, 1, PAIRS):
                        m, v = n - 1, 1 - u
                        pe.wait_ge(gathered[v], turns(i, u, 1) * 2 * BLK * 16)
                        wait(pe, x_ready, m)
                        for q in range(BLK):
                            pe.matmul(ps_x[:, q * P:(q + 1) * P], tok[:, v, q].rearrange("p a f -> p (a f)"), ident,
                                      start=(q == 0), stop=False, skip_group_check=True)
                        pe.wait_ge(onehot_ready, m + 1)
                        for t in range(2):
                            for part in range(3):
                                for c in range(BLK):
                                    w = WIDTH[c]
                                    for a in range(2):
                                        at = 2 * START[c] + a * w
                                        mm = pe.matmul(ps_x[a * D:(a + 1) * D, SEQ - w:], table[:, part, t * BLK + c, :],
                                                       onehot[:, v, t, at:at + w], start=False, stop=False, skip_group_check=True)
                        mm.then_inc(embedded, 1)
                    if live(n, 2, PAIRS):
                        m = n - 2
                        pe.wait_ge(sq1_done, m + 1)
                        wait(pe, ln1_done, m)
                        pe.matmul(ps_v1[:, :], mean, sq1[:, :], start=True, stop=True).then_inc(v1_done, 1)
                    if live(n, 3, PAIRS):
                        m = n - 3
                        pe.wait_ge(sq2_done, m + 1)
                        wait(pe, ln2_done, m)
                        pe.matmul(ps_v2[:, :], mean, sq2[:, :], start=True, stop=True).then_inc(v2_done, 1)

            @block.scalar
            def _(act):
                act.preload_act_table_set("natural_log_exp_and_others")
                act.wait_ge(loaded, 32)
                for n, u, i in pipeline(act, PAIRS, STAGES):
                    if live(n, 2, PAIRS):
                        m = n - 2
                        act.wait_ge(c1_done, m + 1)
                        wait(act, v1_done, m)
                        act.activation(sq1[:, :], ps_c1[u][:, :], ACT.Square).then_inc(sq1_done, 1)
                    if live(n, 3, PAIRS):
                        m, v = n - 3, 1 - u
                        act.wait_ge(c2_done, m + 1)
                        wait(act, v2_done, m)
                        act.activation(sq2[:, :], ps_c2[v][:, :], ACT.Square).then_inc(sq2_done, 1)
                    if live(n, 1, PAIRS):
                        m, v = n - 1, 1 - u
                        act.wait_ge(embedded, m + 1)
                        wait(act, c1_done, m - 1)
                        act.activation(x[:, v, :], ps_x[:, :], ACT.Identity).then_inc(x_ready, 1)
                    if live(n, 2, PAIRS):
                        m = n - 2
                        act.wait_ge(v1_done, m + 1)
                        act.activation(ln1[:, :], ps_v1[:, :], ACT.Ln, bias=eps_ln).then_inc(ln1_done, 1)
                        act.wait_ge(ln1_done, m + 1)
                        wait(act, n1_done, m)
                        act.activation(r1[:, :], ln1[:, :], ACT.Exp, scale=-0.5).then_inc(r1_done, 1)
                    if live(n, 3, PAIRS):
                        m = n - 3
                        act.wait_ge(v2_done, m + 1)
                        act.activation(ln2[:, :], ps_v2[:, :], ACT.Ln, bias=eps_ln).then_inc(ln2_done, 1)
                        act.wait_ge(ln2_done, m + 1)
                        wait(act, xn_done, m)
                        act.activation(r2[:, :], ln2[:, :], ACT.Exp, scale=-0.5).then_inc(r2_done, 1)



def tile_of(big, m):
    return big[:, bass.ds(m, 1), :].rearrange("p a s -> p (a s)")


def learn(nc, outer, sem, banks, XN, W, wcols, vec, ident, fold):
    NW = outer.enter_context(nc.sbuf_tensor("NW", [P, 2, P], F32))
    NB = outer.enter_context(nc.sbuf_tensor("NB", [P, 2], F32))
    with ExitStack() as ctx:
        def sb(name, shape, dt=F32):
            return ctx.enter_context(nc.sbuf_tensor(name, shape, dt))

        k, tlr, s0, x1, w0, s1, t1 = (sb(f"m_{n}", [P, 2, SEQ]) for n in ("k", "tlr", "s0", "x1", "w0", "s1", "t1"))
        t0, u0, x2, e, g, u1, w1, dz1, dx1, dz0, kT, x1T, dz1T, dz0T = (
            sb(f"m_{n}", [P, SEQ]) for n in ("t0", "u0", "x2", "e", "g", "u1", "w1", "dz1", "dx1", "dz0", "kT", "x1T", "dz1T", "dz0T"))
        gbs = sb("gbs", [P, 2, PAIRS])
        half_b = sb("half_b", [P, 3])
        names = ("K", "L", "k", "tlr", "Z0", "s0", "t0", "x1", "u0", "w0", "Z1", "V", "s1", "t1", "x2", "e", "g", "u1", "w1",
                 "dz1", "B", "dx1", "dz0", "Tk", "Tx1", "Tdz1", "Tdz0", "kT", "x1T", "dz1T", "dz0T", "grads")
        done = {n: sem(f"learn_{n}") for n in names}
        half_ready, updated = sem("half_ready"), sem("updated")
        bk_z0, bk_z1, bk_v, bk_b, bk_t0, bk_t1, bk_t2, bk_grad = banks
        STAGES = 2

        with nc.Block() as block:
            @block.tensor
            def _(pe):
                def turn(bank, source, name):
                    for q in range(BLK):
                        mm = pe.transpose(bank[:, q * P:(q + 1) * P], source[:, q * P:(q + 1) * P], ident)
                    mm.then_inc(done[name], 1)

                for n, u, i in pipeline(pe, PAIRS, STAGES):
                    v, m = 1 - u, n - 1
                    front, back = live(n, 0, PAIRS), live(n, 1, PAIRS)
                    if front:
                        wait(pe, done["s0"], n)
                        wait(pe, done["t0"], n)
                        pe.matmul(bk_z0[:, :], wcols(W_K), tile_of(XN, n), start=True, stop=True).then_inc(done["K"], 1)
                        wait(pe, done["s1"], n)
                        wait(pe, done["t1"], n)
                        pe.matmul(bk_z1[:, :], wcols(W_LR), tile_of(XN, n), start=True, stop=True).then_inc(done["L"], 1)
                    if back:
                        wait(pe, done["dz0T"], m)
                        turn(bk_t0, k[:, v, :], "Tk")
                        wait(pe, done["x1T"], m)
                        turn(bk_t1, x1[:, v, :], "Tx1")
                    if front:
                        wait(pe, done["k"], n + 1)
                        pe.matmul(bk_z0[:, :], wcols(W_0), k[:, u, :], start=True, stop=True).then_inc(done["Z0"], 1)
                    if back:
                        wait(pe, done["dz1"], m + 1)
                        wait(pe, done["dx1"], m)
                        pe.matmul(bk_b[:, :], wcols(W_1T), dz1[:, :], start=True, stop=True).then_inc(done["B"], 1)
                        wait(pe, done["dz1T"], m)
                        turn(bk_t2, dz1, "Tdz1")
                    if front:
                        wait(pe, done["x1"], n + 1)
                        wait(pe, done["tlr"], n + 1)
                        pe.matmul(bk_z1[:, :], wcols(W_1), x1[:, u, :], start=True, stop=True).then_inc(done["Z1"], 1)
                        wait(pe, done["e"], n)
                        pe.matmul(bk_v[:, :], wcols(W_V), tile_of(XN, n), start=True, stop=True).then_inc(done["V"], 1)
                    if back:
                        wait(pe, done["dz0"], m + 1)
                        wait(pe, done["kT"], m + 1)
                        turn(bk_t0, dz0, "Tdz0")
                        wait(pe, done["x1T"], m + 1)
                        wait(pe, done["dz1T"], m + 1)
                        for q in range(BLK):
                            pe.matmul(bk_grad[:, P:2 * P], x1T[:, q * P:(q + 1) * P], dz1T[:, q * P:(q + 1) * P],
                                      start=isinstance(n, int) and m == 0 and q == 0, stop=False, skip_group_check=True)
                        wait(pe, done["dz0T"], m + 1)
                        for q in range(BLK):
                            mm = pe.matmul(bk_grad[:, 0:P], kT[:, q * P:(q + 1) * P], dz0T[:, q * P:(q + 1) * P],
                                           start=False, stop=False, skip_group_check=True)
                        mm.then_inc(done["grads"], 1)

            @block.scalar
            def _(act):
                act.preload_act_table_set("silu_and_others")
                act.wait_ge(half_ready, 1)

                def run(name, to, source, func, **more):
                    act.activation(to, source, func, **more).then_inc(done[name], 1)

                for n, u, i in pipeline(act, PAIRS, STAGES):
                    m = n - 1
                    front, back = live(n, 0, PAIRS), live(n, 1, PAIRS)
                    if front:
                        wait(act, done["K"], n + 1)
                        wait(act, done["Tk"], n - 1)
                        run("k", k[:, u, :], bk_z0[:, :], ACT.Identity)
                        wait(act, done["L"], n + 1)
                        wait(act, done["g"], n - 1)
                        run("tlr", tlr[:, u, :], bk_z1[:, :], ACT.Tanh, bias=half_b[:, 2:3], scale=0.5)
                    if back:
                        wait(act, done["grads"], m)
                        wait(act, done["Tk"], m + 1)
                        run("kT", kT[:, :], bk_t0[:, :], ACT.Identity)
                        wait(act, done["Tx1"], m + 1)
                        run("x1T", x1T[:, :], bk_t1[:, :], ACT.Identity)
                    if front:
                        wait(act, done["Z0"], n + 1)
                        wait(act, done["w0"], n - 1)
                        run("s0", s0[:, u, :], bk_z0[:, :], ACT.Silu, bias=vec(V_B0))
                        wait(act, done["u0"], n)
                        run("t0", t0[:, :], bk_z0[:, :], ACT.Tanh, bias=half_b[:, 0:1], scale=0.5)
                        wait(act, done["Z1"], n + 1)
                        wait(act, done["x2"], n - 1)
                        wait(act, done["w1"], n - 1)
                        run("s1", s1[:, u, :], bk_z1[:, :], ACT.Silu, bias=vec(V_B1))
                        run("t1", t1[:, u, :], bk_z1[:, :], ACT.Tanh, bias=half_b[:, 1:2], scale=0.5)
                    if back:
                        wait(act, done["Tdz0"], m + 1)
                        run("dz0T", dz0T[:, :], bk_t0[:, :], ACT.Identity)

            @block.gpsimd
            def _(pool):
                for n, u, i in pipeline(pool, PAIRS, STAGES):
                    if live(n, 1, PAIRS):
                        m, v = n - 1, 1 - u
                        wait(pool, done["s1"], m + 1)
                        wait(pool, done["e"], m)
                        pool.tensor_tensor(x2[:, :], x1[:, v, :], s1[:, v, :], ALU.add).then_inc(done["x2"], 1)

            @block.vector
            def _(dve):
                dve.tensor_scalar(half_b[:, 0:2], W[:, V_B0:V_B1 + 1], 0.5, None, ALU.mult)
                dve.tensor_scalar(half_b[:, 2:3], vec(V_BLR), 0.5, None, ALU.mult).then_inc(half_ready, 1)
                for n, u, i in pipeline(dve, PAIRS, STAGES):
                    v, m = 1 - u, n - 1
                    front, back = live(n, 0, PAIRS), live(n, 1, PAIRS)
                    if back:
                        wait(dve, done["x2"], m + 1)
                        wait(dve, done["V"], m + 1)
                        dve.tensor_tensor(e[:, :], x2[:, :], bk_v[:, :], ALU.subtract).then_inc(done["e"], 1)
                        wait(dve, done["t1"], m + 1)
                        dve.tensor_scalar(u1[:, :], t1[:, v, :], 1.0, None, ALU.subtract).then_inc(done["u1"], 1)
                        wait(dve, done["e"], m + 1)
                        dve.scalar_tensor_tensor(g[:, :], tlr[:, v, :], 1.0, e[:, :], ALU.add, ALU.mult).then_inc(done["g"], 1)
                        wait(dve, done["u1"], m + 1)
                        dve.scalar_tensor_tensor(w1[:, :], s1[:, v, :], 1.0, u1[:, :], ALU.subtract, ALU.mult).then_inc(done["w1"], 1)
                        wait(dve, done["w1"], m + 1)
                        wait(dve, done["Tdz1"], m)
                        dve.scalar_tensor_tensor(dz1[:, :], w1[:, :], 2.0, g[:, :], ALU.subtract, ALU.mult,
                                                 accum_out=gbs[:, 1, bass.ds(m, 1)]).then_inc(done["dz1"], 1)
                    if front:
                        wait(dve, done["s0"], n + 1)
                        wait(dve, done["Tx1"], n - 1)
                        dve.tensor_tensor(x1[:, u, :], k[:, u, :], s0[:, u, :], ALU.add).then_inc(done["x1"], 1)
                        wait(dve, done["t0"], n + 1)
                        dve.tensor_scalar(u0[:, :], t0[:, :], 1.0, None, ALU.subtract).then_inc(done["u0"], 1)
                        wait(dve, done["u0"], n + 1)
                        dve.scalar_tensor_tensor(w0[:, u, :], s0[:, u, :], 1.0, u0[:, :], ALU.subtract, ALU.mult).then_inc(done["w0"], 1)
                    if back:
                        wait(dve, done["B"], m + 1)
                        dve.scalar_tensor_tensor(dx1[:, :], bk_b[:, :], -0.5, g[:, :], ALU.mult, ALU.add).then_inc(done["dx1"], 1)
                        wait(dve, done["dx1"], m + 1)
                        wait(dve, done["Tdz0"], m)
                        dve.scalar_tensor_tensor(dz0[:, :], w0[:, v, :], 2.0, dx1[:, :], ALU.subtract, ALU.mult,
                                                 accum_out=gbs[:, 0, bass.ds(m, 1)]).then_inc(done["dz0"], 1)
                        wait(dve, done["grads"], m)
                        wait(dve, done["Tdz1"], m + 1)
                        dve.tensor_copy(dz1T[:, :], bk_t2[:, :]).then_inc(done["dz1T"], 1)

        gd = sb("gd", [P, 2, D])
        gb = sb("gb", [P, 2])
        grad = sb("grad", [P, 2 * D + 2])
        size = sb("size", [P, 2 * D + 2])
        param = sb("param", [P, 2 * D + 2])
        folded, gathered_g, chain = sem("folded"), sem("gathered_g"), sem("chain")
        with nc.Block() as block:
            @block.vector
            def _(dve):
                count = [0]

                def then(ins):
                    count[0] += 1
                    ins.then_inc(chain, 1)
                    dve.wait_ge(chain, count[0])

                dve.tensor_reduce(gb[:, :], gbs[:, :, :], AX_X, ALU.add).then_inc(gathered_g, 1)
                dve.memset(NW[:, :, :], 0.0).then_inc(gathered_g, 1)
                dve.tensor_copy(param[:, 2 * D:], W[:, V_B0:V_B1 + 1])
                for layer in range(2):
                    for a in range(2):
                        half = slice(a * D, (a + 1) * D)
                        dve.tensor_copy(gd[half, layer, :], bk_grad[half, layer * P + a * D:layer * P + (a + 1) * D]).then_inc(gathered_g, 1)
                then(dve.tensor_copy(param[:, 0:2 * D], W[:, W_01:W_01 + 2 * D]))
                dve.wait_ge(folded, 2)
                then(dve.tensor_scalar(grad[:, :], bk_v[:, 0:2 * D + 2], -0.5 * 2.0 / D * MAX_ALR * 0.5, None, ALU.mult))
                then(dve.scalar_tensor_tensor(size[:, :], grad[:, :], -1.0, grad[:, :], ALU.mult, ALU.max))
                then(dve.tensor_scalar(size[:, :], size[:, :], EPS_ADAM, None, ALU.add))
                then(dve.reciprocal(size[:, :], size[:, :]))
                then(dve.scalar_tensor_tensor(grad[:, :], grad[:, :], -LR, size[:, :], ALU.mult, ALU.mult))
                then(dve.scalar_tensor_tensor(param[:, :], param[:, :], 1.0 - LR * WD, grad[:, :], ALU.mult, ALU.add))
                for layer in range(2):
                    for a in range(2):
                        half = slice(a * D, (a + 1) * D)
                        then(dve.tensor_copy(NW[half, layer, a * D:(a + 1) * D], param[half, layer * D:(layer + 1) * D]))
                then(dve.tensor_copy(NB[:, :], param[:, 2 * D:]))

            @block.tensor
            def _(pe):
                pe.wait_ge(gathered_g, 6)
                pe.matmul(bk_v[:, 0:2 * D], fold, gd[:, :, :].rearrange("p l d -> p (l d)"), start=True, stop=True).then_inc(folded, 1)
                pe.matmul(bk_v[:, 2 * D:2 * D + 2], fold, gb[:, :], start=False, stop=True, skip_group_check=True).then_inc(folded, 1)
    return NW, NB


def retrieve(nc, ctx, sem, banks, XN, H, W, wcols, NW, NB):
    q, s0, x1, s1 = (ctx.enter_context(nc.sbuf_tensor(f"r_{n}", [P, 2, SEQ], F32)) for n in ("q", "s0", "x1", "s1"))
    done = {n: sem(f"read_{n}") for n in ("Q", "q", "Z0", "s0", "x1", "Z1", "s1", "x2", "h")}
    STAGES = 3
    with nc.Block() as block:
        @block.tensor
        def _(pe):
            for n, u, i in pipeline(pe, PAIRS, STAGES):
                if live(n, 2, PAIRS):
                    wait(pe, done["x1"], n - 1)
                    wait(pe, done["s1"], n - 3)
                    pe.matmul(banks[4 + u][:, :], NW[:, 1, :], x1[:, u, :], start=True, stop=True).then_inc(done["Z1"], 1)
                if live(n, 1, PAIRS):
                    wait(pe, done["q"], n)
                    wait(pe, done["s0"], n - 2)
                    pe.matmul(banks[3 - u][:, :], NW[:, 0, :], q[:, 1 - u, :], start=True, stop=True).then_inc(done["Z0"], 1)
                if live(n, 0, PAIRS):
                    wait(pe, done["q"], n - 1)
                    pe.matmul(banks[u][:, :], wcols(W_Q), tile_of(XN, n), start=True, stop=True).then_inc(done["Q"], 1)

        @block.scalar
        def _(act):
            for n, u, i in pipeline(act, PAIRS, STAGES):
                if live(n, 2, PAIRS):
                    wait(act, done["Z1"], n - 1)
                    wait(act, done["h"], n - 3)
                    act.activation(s1[:, u, :], banks[4 + u][:, :], ACT.Silu, bias=NB[:, 1:2]).then_inc(done["s1"], 1)
                if live(n, 1, PAIRS):
                    wait(act, done["Z0"], n)
                    wait(act, done["x1"], n - 2)
                    act.activation(s0[:, 1 - u, :], banks[3 - u][:, :], ACT.Silu, bias=NB[:, 0:1]).then_inc(done["s0"], 1)
                if live(n, 0, PAIRS):
                    wait(act, done["Q"], n + 1)
                    wait(act, done["x1"], n - 1)
                    act.activation(q[:, u, :], banks[u][:, :], ACT.Identity).then_inc(done["q"], 1)

        @block.vector
        def _(dve):
            for n, u, i in pipeline(dve, PAIRS, STAGES):
                if live(n, 1, PAIRS):
                    wait(dve, done["s0"], n)
                    wait(dve, done["x2"], n - 2)
                    wait(dve, done["Z1"], n - 2)
                    dve.tensor_tensor(x1[:, 1 - u, :], q[:, 1 - u, :], s0[:, 1 - u, :], ALU.add).then_inc(done["x1"], 1)
                if live(n, 2, PAIRS):
                    wait(dve, done["s1"], n - 1)
                    dve.tensor_tensor(s1[:, u, :], x1[:, u, :], s1[:, u, :], ALU.add).then_inc(done["x2"], 1)
                    wait(dve, done["x2"], n - 1)
                    dve.tensor_tensor(tile_of(H, n - 2), tile_of(H, n - 2), s1[:, u, :], ALU.add).then_inc(done["h"], 1)


def project(nc, sem, banks, H, XN, W, VT, q_parts, k_parts, turn, centre, mean, eps_ln, eps_rms, vec):
    KR = 2 * KV * HD
    with ExitStack() as ctx:
        def sb(name, shape, dt=F32):
            return ctx.enter_context(nc.sbuf_tensor(name, shape, dt))

        TURN = sb("TURN", [P, 4, SEQ])
        sq, lnv, r, sq2, lnv2, r2 = (sb(f"j_{n}", [P, SEQ]) for n in ("sq", "ln", "r", "sq2", "ln2", "r2"))
        hn = sb("j_hn", [P, 2, SEQ])
        rows = {"q": P, "k": KR}
        cosd = {x: sb(f"j_{x}cos", [rows[x], SEQ]) for x in "qk"}
        sind = {x: sb(f"j_{x}sin", [rows[x], SEQ]) for x in "qk"}
        full = {x: sb(f"j_{x}", [rows[x], 2, SEQ]) for x in "qk"}
        rest = {x: sb(f"j_{x}rest", [rows[x], SEQ]) for x in "qk"}
        part = {x: sb(f"j_{x}part", [rows[x], 2, 3, SEQ], BF16) for x in "qk"}
        names = ["turn", "ln1w", "c", "sq", "v", "ln", "r", "xn", "sq2", "v2", "ln2", "r2", "hn", "V", "VT"]
        names += [f"{x}{n}" for x in "qk" for n in ("P", "R", "cos", "sin", "full", "hi", "rest", "mid", "lo")]
        done = {n: sem(f"proj_{n}") for n in names}
        stored = {x: [sem(f"stored_{x}{u}") for u in range(2)] for x in "qk"}
        bk_c, bk_v, bk_v2, bk_vt = banks[0], banks[1], banks[2], banks[3]
        bk = {"q": (banks[4], banks[5]), "k": (banks[6], banks[7])}
        wq = {"q": (W_FQ, W_FQR, P), "k": (W_FK, W_FKR, KR)}
        parts = {"q": q_parts, "k": k_parts}
        STAGES = 4

        with nc.Block() as block:
            @block.sync
            def _(sp):
                sp.dma_start(TURN[:, :, :], turn).then_inc(done["turn"], 16)
                for n, u, i in pipeline(sp, PAIRS, STAGES):
                    if live(n, 3, PAIRS):
                        m, v = n - 3, 1 - u
                        for x in "qk":
                            wait(sp, done[f"{x}lo"], m + 1)
                            sp.dma_start(parts[x][:, bass.ds(m, 1)].rearrange("t a p s -> p (t a) s"),
                                         part[x][:, v]).then_inc(stored[x][v], 16)
                for x in "qk":
                    for u in range(2):
                        sp.wait_ge(stored[x][u], PAIRS // 2 * 16)

            @block.tensor
            def _(pe):
                pe.wait_ge(done["ln1w"], 2)
                for n, u, i in pipeline(pe, PAIRS, STAGES):
                    if live(n, 0, PAIRS):
                        wait(pe, done["xn"], n)
                        pe.matmul(bk_c[:, :], centre, tile_of(H, n), start=True, stop=True).then_inc(done["c"], 1)
                    if live(n, 1, PAIRS):
                        m = n - 1
                        wait(pe, done["sq2"], m + 1)
                        wait(pe, done["ln2"], m)
                        pe.matmul(bk_v2[:, :], mean, sq2[:, :], start=True, stop=True).then_inc(done["v2"], 1)
                    if live(n, 2, PAIRS):
                        m = n - 2
                        wait(pe, done["hn"], m + 1)
                        for x in "qk":
                            wait(pe, done[f"{x}cos"], m)
                            pe.matmul(bk[x][0][0:rows[x], :], W[:, wq[x][0]:wq[x][0] + wq[x][2]], hn[:, u, :], start=True, stop=True).then_inc(done[f"{x}P"], 1)
                            wait(pe, done[f"{x}sin"], m)
                            pe.matmul(bk[x][1][0:rows[x], :], W[:, wq[x][1]:wq[x][1] + wq[x][2]], hn[:, u, :], start=True, stop=True).then_inc(done[f"{x}R"], 1)
                            if x == "q" and live(n, 0, PAIRS):
                                wait(pe, done["sq"], n + 1)
                                wait(pe, done["ln"], n)
                                pe.matmul(bk_v[:, :], mean, sq[:, :], start=True, stop=True).then_inc(done["v"], 1)
                        wait(pe, done["VT"], m)
                        for q in range(BLK):
                            mm = pe.matmul(bk_vt[:, q * KR:(q + 1) * KR], hn[:, u, q * P:(q + 1) * P], W[:, W_FV:W_FV + KR],
                                           start=q == 0, stop=False, skip_group_check=True)
                        mm.then_inc(done["V"], 1)
                    elif live(n, 0, PAIRS):
                        wait(pe, done["sq"], n + 1)
                        wait(pe, done["ln"], n)
                        pe.matmul(bk_v[:, :], mean, sq[:, :], start=True, stop=True).then_inc(done["v"], 1)

            @block.scalar
            def _(act):
                act.preload_act_table_set("natural_log_exp_and_others")

                def run(name, to, source, func, **more):
                    act.activation(to, source, func, **more).then_inc(done[name], 1)

                for n, u, i in pipeline(act, PAIRS, STAGES):
                    if live(n, 1, PAIRS):
                        m = n - 1
                        wait(act, done["xn"], m + 1)
                        wait(act, done["v2"], m)
                        run("sq2", sq2[:, :], tile_of(XN, m), ACT.Square)
                    if live(n, 0, PAIRS):
                        wait(act, done["c"], n + 1)
                        wait(act, done["v"], n)
                        run("sq", sq[:, :], bk_c[:, :], ACT.Square)
                    if live(n, 3, PAIRS):
                        m, v = n - 3, 1 - u
                        for x in "qk":
                            wait(act, done[f"{x}full"], m + 1)
                            if live(n, 5, PAIRS):
                                wait(act, stored[x][v], turns(i, u, 5) * 16)
                            run(f"{x}hi", part[x][:, v, 0, :], full[x][:, v, :], ACT.Identity)
                    if live(n, 1, PAIRS):
                        m = n - 1
                        wait(act, done["v2"], m + 1)
                        run("ln2", lnv2[:, :], bk_v2[:, :], ACT.Ln, bias=eps_rms)
                        wait(act, done["ln2"], m + 1)
                        wait(act, done["hn"], m)
                        run("r2", r2[:, :], lnv2[:, :], ACT.Exp, scale=-0.5)
                    if live(n, 0, PAIRS):
                        wait(act, done["v"], n + 1)
                        run("ln", lnv[:, :], bk_v[:, :], ACT.Ln, bias=eps_ln)
                        wait(act, done["ln"], n + 1)
                        run("r", r[:, :], lnv[:, :], ACT.Exp, scale=-0.5)
                    if live(n, 3, PAIRS):
                        m, v = n - 3, 1 - u
                        for x in "qk":
                            wait(act, done[f"{x}rest"], m + 1)
                            run(f"{x}mid", part[x][:, v, 1, :], rest[x][:, :], ACT.Identity)
                    if live(n, 2, PAIRS):
                        m = n - 2
                        wait(act, done["V"], m + 1)
                        run("VT", tile_of(VT, m), bk_vt[:, 0:BLK * KR], ACT.Identity)

            @block.gpsimd
            def _(pool):
                for n, u, i in pipeline(pool, PAIRS, STAGES):
                    if live(n, 2, PAIRS):
                        m = n - 2
                        for x in "qk":
                            wait(pool, done[f"{x}sin"], m + 1)
                            wait(pool, done[f"{x}cos"], m + 1)
                            wait(pool, done[f"{x}rest"], m - 1)
                            pool.tensor_tensor(full[x][:, u, :], cosd[x][:, :], sind[x][:, :], ALU.add).then_inc(done[f"{x}full"], 1)

            @block.vector
            def _(dve):
                dve.tensor_scalar(W[:, W_FQ:W_01], W[:, W_FQ:W_01], vec(V_LN1), None, ALU.mult).then_inc(done["ln1w"], 1)
                dve.tensor_scalar(W[:, W_FK:W_O], W[:, W_FK:W_O], vec(V_LN1), None, ALU.mult).then_inc(done["ln1w"], 1)
                dve.wait_ge(done["turn"], 16)
                for n, u, i in pipeline(dve, PAIRS, STAGES):
                    if live(n, 3, PAIRS):
                        m, v = n - 3, 1 - u
                        for x in "qk":
                            wait(dve, done[f"{x}lo"], m)
                            wait(dve, done[f"{x}hi"], m + 1)
                            dve.tensor_tensor(rest[x][:, :], full[x][:, v, :], part[x][:, v, 0, :], ALU.subtract).then_inc(done[f"{x}rest"], 1)
                    if live(n, 1, PAIRS):
                        m, v = n - 1, 1 - u
                        wait(dve, done["r2"], m + 1)
                        wait(dve, done["V"], m - 1)
                        dve.tensor_tensor(hn[:, v, :], tile_of(XN, m), r2[:, :], ALU.mult).then_inc(done["hn"], 1)
                    if live(n, 2, PAIRS):
                        m = n - 2
                        for j, x in enumerate("qk"):
                            wait(dve, done[f"{x}full"], m)
                            wait(dve, done[f"{x}P"], m + 1)
                            dve.tensor_tensor(cosd[x][:, :], bk[x][0][0:rows[x], :], TURN[0:rows[x], 2 * j, :], ALU.mult).then_inc(done[f"{x}cos"], 1)
                            wait(dve, done[f"{x}R"], m + 1)
                            dve.tensor_tensor(sind[x][:, :], bk[x][1][0:rows[x], :], TURN[0:rows[x], 2 * j + 1, :], ALU.mult).then_inc(done[f"{x}sin"], 1)
                    if live(n, 3, PAIRS):
                        m, v = n - 3, 1 - u
                        for x in "qk":
                            wait(dve, done[f"{x}mid"], m + 1)
                            dve.tensor_tensor(part[x][:, v, 2, :], rest[x][:, :], part[x][:, v, 1, :], ALU.subtract).then_inc(done[f"{x}lo"], 1)
                    if live(n, 0, PAIRS):
                        wait(dve, done["r"], n + 1)
                        dve.tensor_tensor(tile_of(XN, n), bk_c[:, :], r[:, :], ALU.mult).then_inc(done["xn"], 1)


def score_units(order):
    units = []
    for b in order:
        w = SEQ - P * b
        heads = min(HEADS, SEQ // w)
        units += [(b, h, heads, w) for h in range(0, HEADS, heads)]
    return units


def attend(nc, sem, banks, H, XN, W, CST, VT, q_parts, k_parts, causal, ident):
    RING = 4
    UNITS = score_units(range(BLK))
    NU = len(UNITS)
    SROWS, TROWS = 6 * HD, 6 * HD + 3
    STAGES = 5
    with ExitStack() as ctx:
        def sb(name, shape, dt=F32):
            return ctx.enter_context(nc.sbuf_tensor(name, shape, dt))

        Q = sb("t_q", [TROWS, RING, HEADS, SEQ], BF16)
        K = sb("t_k", [TROWS, RING, KV, SEQ], BF16)
        V = sb("t_v", [P, 2, BLK, KV, 32])
        negmax = sb("negmax", [P, 2, HEADS * BLK])
        nm = sb("nm", [HEADS * BLK, 2, 3, P], BF16)
        nrest = sb("nrest", [HEADS * BLK, P])
        E = sb("t_e", [P, HEADS * TRAP])
        Y = sb("t_y", [P, SEQ])
        lnd = sb("lnd", [P, SEQ])
        rd = sb("rd", [P, SEQ])
        yn = sb("yn", [P, SEQ])
        causal32 = sb("causal32", [P, P])
        mask = sb("mask", [P, P], BF16)
        eye = sb("eye", [P, P], BF16)
        names = ("mask_loaded", "mask", "ones", "S", "max", "turned", "nhi", "nrest", "nmid", "nlo", "T", "exp", "V",
                 "av", "Y", "D", "lnd", "rd", "yn", "wo", "xn", "h")
        done = {n: sem(f"att_{n}") for n in names}
        q_loaded = [sem(f"q_loaded{u}") for u in range(RING)]
        nm_loaded = [sem(f"nm_loaded{u}") for u in range(RING)]
        bk_s, bk_t, bk_av, bk_d, bk_o = banks[0:2], banks[2:5], banks[5], banks[6], banks[7]
        KSLOTS = [(0, 0, 3), (1, 3, 2), (2, 5, 1)]
        QSLOTS = [(0, 0), (1, 1), (2, 2), (0, 3), (1, 4), (0, 5)]
        LOADS = len(QSLOTS) + sum(n for _, _, n in KSLOTS)

        def e_cols(b, h):
            at = HEADS * START[b] + h * WIDTH[b]
            return E[:, at:at + WIDTH[b]]

        with nc.Block() as block:
            @block.sync
            def _(sp):
                sp.dma_start(causal32[:, :], causal).then_inc(done["mask_loaded"], 16)
                for n, u, i in pipeline(sp, ROWS, STAGES, RING):
                    if live(n, 0, ROWS):
                        wait(sp, done["T"], (n - RING + 1) * NU)
                        pair = RING // 2 * i + u // 2
                        a = u % 2
                        for part, slot in QSLOTS:
                            src = q_parts[part, bass.ds(pair, 1), a * D:(a + 1) * D].rearrange("o (h d) s -> (o d) h s", d=HD)
                            sp.dma_start(Q[slot * HD:(slot + 1) * HD, u], src).then_inc(q_loaded[u], 16)
                        for part, slot, copies in KSLOTS:
                            for c in range(copies):
                                src = k_parts[part, bass.ds(pair, 1), a * KV * HD:(a + 1) * KV * HD].rearrange("o (h d) s -> (o d) h s", d=HD)
                                sp.dma_start(K[(slot + c) * HD:(slot + c + 1) * HD, u], src).then_inc(q_loaded[u], 16)
                    if live(n, 2, ROWS):
                        m, g = n - 2, (u - 2) % RING
                        wait(sp, done["nlo"], m + 1)
                        for part in range(3):
                            sp.dma_start(Q[SROWS + part:SROWS + part + 1, g].rearrange("o h s -> o (h s)"),
                                         nm[:, u % 2, part, :]).then_inc(nm_loaded[g], 16)

            @block.gpsimd
            def _(pool):
                for n, u, i in pipeline(pool, ROWS, STAGES, RING):
                    if live(n, 3, ROWS):
                        m, a = n - 3, (u - 3) % 2
                        pair = RING // 2 * i + (u - 3) // 2
                        wait(pool, done["av"], (m - 1) * BLK)
                        wait(pool, done["ones"], 3)
                        pool.sem_inc(done["ones"], 1)
                        src = tile_of(VT, pair).rearrange("p (q a k d) -> p q a k d", q=BLK, a=2, k=KV)[:, :, a]
                        pool.tensor_copy(V[:, a, :, :, 0:HD], src).then_inc(done["V"], 1)
                    if live(n, 4, ROWS):
                        m, a = n - 4, u % 2
                        wait(pool, done["rd"], m + 1)
                        wait(pool, done["wo"], m)
                        pool.tensor_tensor(yn[:, :], Y[:, :], rd[:, :], ALU.mult).then_inc(done["yn"], 1)

            @block.vector
            def _(dve):
                dve.memset(V[:, :, :, :, :], 0.0).then_inc(done["ones"], 1)
                dve.wait_ge(done["ones"], 1)
                dve.memset(V[:, :, :, :, HD:HD + 1], 1.0).then_inc(done["ones"], 1)
                dve.memset(K[SROWS:TROWS, :, :, :], 1.0).then_inc(done["ones"], 1)
                dve.wait_ge(done["mask_loaded"], 16)
                dve.tensor_copy(mask[:, :], causal32[:, :]).then_inc(done["mask"], 1)
                dve.tensor_copy(eye[:, :], ident).then_inc(done["mask"], 1)

                def fold(n, u):
                    m = n - 2
                    wait(dve, done["turned"], m + 1)
                    if live(n, 4, ROWS):
                        g = (u - 4) % RING
                        dve.wait_ge(nm_loaded[g], turns(i, u, 4, RING) * 48)
                    dve.tensor_copy(nm[:, u % 2, 0, :], bk_d[0:HEADS * BLK, 0:P]).then_inc(done["nhi"], 1)
                    wait(dve, done["nhi"], m + 1)
                    dve.tensor_tensor(nrest[:, :], bk_d[0:HEADS * BLK, 0:P], nm[:, u % 2, 0, :], ALU.subtract).then_inc(done["nrest"], 1)
                    wait(dve, done["nrest"], m + 1)
                    dve.tensor_copy(nm[:, u % 2, 1, :], nrest[:, :]).then_inc(done["nmid"], 1)
                    wait(dve, done["nmid"], m + 1)
                    dve.tensor_tensor(nm[:, u % 2, 2, :], nrest[:, :], nm[:, u % 2, 1, :], ALU.subtract).then_inc(done["nlo"], 1)

                for n, u, i in pipeline(dve, ROWS, STAGES, RING):
                    if live(n, 2, ROWS):
                        fold(n, u)
                    if live(n, 1, ROWS):
                        m = n - 1
                        wait(dve, done["turned"], m - 1)
                        for t, (c, h, heads, w) in enumerate(UNITS):
                            wait(dve, done["S"], m * NU + t + 1)
                            j = BLK - 1 - c
                            to = negmax[:, (u - 1) % 2, :].rearrange("p (h j) -> p h j", j=BLK)[:, h:h + heads, j]
                            dve.tensor_reduce(to, bk_s[t % 2][:, 0:heads * w].rearrange("p (h s) -> p h s", h=heads),
                                              AX_X, ALU.max, negate=True).then_inc(done["max"], 1)
                    if live(n, 4, ROWS) and u % 2 == 1:
                        pair = RING // 2 * i + (u - 4) // 2
                        wait(dve, done["wo"], n - 4 + 1)
                        dve.tensor_tensor(tile_of(XN, pair), tile_of(XN, pair), bk_o[:, :], ALU.add).then_inc(done["xn"], 1)
                        wait(dve, done["xn"], pair + 1)
                        dve.tensor_tensor(tile_of(H, pair), tile_of(H, pair), tile_of(XN, pair), ALU.add).then_inc(done["h"], 1)

            @block.tensor
            def _(pe):
                pe.wait_ge(done["mask"], 2)
                pe.wait_ge(done["ones"], 3)

                def s_unit(m, g, t):
                    c, h, heads, w = UNITS[t]
                    j = BLK - 1 - c
                    wait(pe, done["max"], m * NU + max(t - 1, 0))
                    for x in range(heads):
                        pe.matmul(bk_s[t % 2][:, x * w:(x + 1) * w], Q[0:SROWS, g, h + x, j * P:(j + 1) * P],
                                  K[0:SROWS, g, (h + x) // KV, 0:w], start=x == 0, stop=False, skip_group_check=True)
                        mm = pe.matmul(bk_s[t % 2][:, (x + 1) * w - P:(x + 1) * w], mask[:, :], eye[:, :],
                                       start=False, stop=False, skip_group_check=True)
                    mm.then_inc(done["S"], 1)

                def t_unit(m, g, t):
                    c, h, heads, w = UNITS[t]
                    wait(pe, done["exp"], m * NU + (t - 2 if t > 2 else -1 if t == 0 else 0))
                    for x in range(heads):
                        pe.matmul(bk_t[t % 3][:, x * w:(x + 1) * w], K[:, g, (h + x) // KV, c * P:(c + 1) * P],
                                  Q[:, g, h + x, c * P:], start=x == 0, stop=False, skip_group_check=True)
                        mm = pe.matmul(bk_t[t % 3][:, x * w:x * w + P], eye[:, :], mask[:, :],
                                       start=False, stop=False, skip_group_check=True)
                    mm.then_inc(done["T"], 1)

                def values(m, a, c):
                    wait(pe, done["exp"], m * NU + sum(b <= c for b, *_ in UNITS))
                    if c == 0:
                        wait(pe, done["V"], m + 1)
                        wait(pe, done["Y"], m)
                    for h in range(HEADS):
                        mm = pe.matmul(bk_av[32 * h:32 * h + 32, c * P:], V[:, a, c, h // KV, :], e_cols(c, h),
                                       start=c == 0, stop=False, skip_group_check=True)
                    mm.then_inc(done["av"], 1)

                for n, u, i in pipeline(pe, ROWS, STAGES, RING):
                    s_live, t_live, f_live = live(n, 1, ROWS), live(n, 3, ROWS), live(n, 4, ROWS)
                    if s_live:
                        g = (u - 1) % RING
                        pe.wait_ge(q_loaded[g], turns(i, u, 1, RING) * LOADS * 16)
                    if t_live:
                        g = (u - 3) % RING
                        pe.wait_ge(nm_loaded[g], turns(i, u, 3, RING) * 48)
                    for t in range(NU):
                        if s_live:
                            s_unit(n - 1, (u - 1) % RING, t)
                        if t_live:
                            t_unit(n - 3, (u - 3) % RING, t)
                        if t == 0 and live(n, 2, ROWS):
                            m = n - 2
                            wait(pe, done["max"], (m + 1) * NU)
                            wait(pe, done["lnd"], n - 5 + 1)
                            pe.transpose(bk_d[0:HEADS * BLK, 0:P], negmax[:, u % 2, :], ident).then_inc(done["turned"], 1)
                        if f_live:
                            m, a = n - 4, u % 2
                            if t == 1:
                                values(m, a, 2)
                                values(m, a, 3)
                            if t == 4:
                                wait(pe, done["Y"], m + 1)
                                wait(pe, done["nrest"], min(n - 1, ROWS) if isinstance(n, int) else n - 1)
                                pe.matmul(bk_d[:, :], CST[:, C_DEN:C_DEN + P], Y[:, :], start=True, stop=True).then_inc(done["D"], 1)
                            if t == 9:
                                wait(pe, done["yn"], m + 1)
                                if a == 0:
                                    wait(pe, done["xn"], (n - 4 + 1) // 2 if isinstance(n, int) else RING // 2 * i + (u - 4) // 2)
                                pe.matmul(bk_o[a * D:(a + 1) * D, :], W[:, W_O:W_O + D], yn[:, :],
                                          start=True, stop=False, skip_group_check=True).then_inc(done["wo"], 1)
                        if t_live:
                            m, a = n - 3, (u - 3) % 2
                            if t == 6:
                                values(m, a, 0)
                            if t == 10:
                                values(m, a, 1)

            @block.scalar
            def _(act):
                def run(name, to, source, func, **more):
                    act.activation(to, source, func, **more).then_inc(done[name], 1)

                for n, u, i in pipeline(act, ROWS, STAGES, RING):
                    for t, (c, h, heads, w) in enumerate(UNITS):
                        if live(n, 3, ROWS):
                            m = n - 3
                            wait(act, done["T"], m * NU + t + 1)
                            wait(act, done["av"], (m - 1) * BLK + c + 1)
                            at = HEADS * START[c] + h * w
                            run("exp", E[:, at:at + heads * w], bk_t[t % 3][:, 0:heads * w], ACT.Exp)
                        if live(n, 4, ROWS):
                            m = n - 4
                            if t == 2:
                                wait(act, done["av"], (m + 1) * BLK)
                                wait(act, done["yn"], m)
                                run("Y", Y[:, :], bk_av[:, :], ACT.Identity)
                            if t == 6:
                                wait(act, done["D"], m + 1)
                                run("lnd", lnd[:, :], bk_d[:, :], ACT.Ln)
                                wait(act, done["lnd"], m + 1)
                                wait(act, done["yn"], m)
                                run("rd", rd[:, :], lnd[:, :], ACT.Exp, scale=-1.0)


X_SCALE, W_SCALE = 256.0, 64.0


def route(nc, sem, banks, XN, W, CST, FS, gates, ident, mean, eps_rms, vec):
    GROUPS = PAIRS * BLK * 2
    with ExitStack() as ctx:
        def sb(name, shape, dt=F32):
            return ctx.enter_context(nc.sbuf_tensor(name, shape, dt))

        sq, lnv, r = (sb(f"g_{n}", [P, SEQ]) for n in ("sq", "ln", "r"))
        flat = sb("g_flat", [P, 2, SEQ])
        hi, lo = sb("g_hi", [P, 2, SEQ], F16), sb("g_lo", [P, 2, SEQ], F16)
        LG = sb("g_logits", [P, PAIRS, BLK * 2 * EXPERTS])
        done = {n: sem(f"route_{n}") for n in ("ln2w", "sq", "v", "ln", "r", "flat", "L", "logits", "hi", "lo")}
        stacked = [sem(f"stacked{u}") for u in range(2)]
        bk_v, bk_l = banks[0], banks[1]
        G8 = 2 * EXPERTS
        STAGES = 3

        with nc.Block() as block:
            @block.sync
            def _(sp):
                for n, u, i in pipeline(sp, PAIRS, STAGES):
                    if live(n, 2, PAIRS):
                        m = n - 2
                        wait(sp, done["hi"], m + 1)
                        wait(sp, done["lo"], m + 1)
                        for a in range(2):
                            for j, part in enumerate((hi, lo)):
                                sp.dma_start(FS[j * D:(j + 1) * D, bass.ds(2 * m + a, 1), :].rearrange("p a s -> p (a s)"),
                                             part[a * D:(a + 1) * D, u, :]).then_inc(stacked[u], 16)
                for u in range(2):
                    sp.wait_ge(stacked[u], PAIRS // 2 * 64)

            @block.tensor
            def _(pe):
                pe.wait_ge(done["ln2w"], 1)
                for n, u, i in pipeline(pe, PAIRS, STAGES):
                    if live(n, 0, PAIRS):
                        wait(pe, done["sq"], n + 1)
                        wait(pe, done["ln"], n)
                        pe.matmul(bk_v[:, :], mean, sq[:, :], start=True, stop=True).then_inc(done["v"], 1)
                    if live(n, 1, PAIRS):
                        m, v = n - 1, 1 - u
                        wait(pe, done["flat"], m + 1)
                        wait(pe, done["logits"], m)
                        for q in range(BLK):
                            mm = pe.matmul(bk_l[:, q * G8:(q + 1) * G8], flat[:, v, q * P:(q + 1) * P], W[:, W_ROUTE:W_ROUTE + G8],
                                           start=q == 0, stop=False, skip_group_check=True)
                        mm.then_inc(done["L"], 1)

            @block.scalar
            def _(act):
                def run(name, to, source, func, **more):
                    act.activation(to, source, func, **more).then_inc(done[name], 1)

                for n, u, i in pipeline(act, PAIRS, STAGES):
                    if live(n, 0, PAIRS):
                        wait(act, done["v"], n)
                        run("sq", sq[:, :], tile_of(XN, n), ACT.Square)
                    if live(n, 1, PAIRS):
                        m, v = n - 1, 1 - u
                        wait(act, done["flat"], m + 1)
                        if live(n, 3, PAIRS):
                            wait(act, stacked[v], turns(i, u, 3) * 64)
                        run("hi", hi[:, v, :], flat[:, v, :], ACT.Identity, scale=X_SCALE)
                        wait(act, done["L"], m + 1)
                        run("logits", tile_of(LG, m), bk_l[:, 0:BLK * G8], ACT.Identity)
                    if live(n, 0, PAIRS):
                        wait(act, done["v"], n + 1)
                        run("ln", lnv[:, :], bk_v[:, :], ACT.Ln, bias=eps_rms)
                        wait(act, done["ln"], n + 1)
                        wait(act, done["flat"], n)
                        run("r", r[:, :], lnv[:, :], ACT.Exp, scale=-0.5)

            @block.vector
            def _(dve):
                dve.tensor_scalar(W[:, W_ROUTE:W_ROUTE + G8], W[:, W_ROUTE:W_ROUTE + G8], vec(V_LN2), None, ALU.mult).then_inc(done["ln2w"], 1)
                for n, u, i in pipeline(dve, PAIRS, STAGES):
                    if live(n, 1, PAIRS):
                        m, v = n - 1, 1 - u
                        wait(dve, done["hi"], m + 1)
                        if live(n, 3, PAIRS):
                            wait(dve, stacked[v], turns(i, u, 3) * 64)
                        dve.scalar_tensor_tensor(lo[:, v, :], flat[:, v, :], X_SCALE, hi[:, v, :], ALU.mult, ALU.subtract).then_inc(done["lo"], 1)
                    if live(n, 0, PAIRS):
                        wait(dve, done["r"], n + 1)
                        wait(dve, done["L"], n - 1)
                        wait(dve, done["lo"], n - 1)
                        dve.tensor_tensor(flat[:, u, :], tile_of(XN, n), r[:, :], ALU.mult).then_inc(done["flat"], 1)

        prob, first, second, spare = (sb(f"g_{n}", [P, GROUPS, EXPERTS]) for n in ("prob", "first", "second", "spare"))
        most, total, top1, top2 = (sb(f"g_{n}", [P, GROUPS]) for n in ("most", "total", "top1", "top2"))
        gate = sb("g_gate", [P, PAIRS, 2, EXPERTS, BLK])
        gateT = sb("g_gateT", [P, 2, BLK, P])
        chain, less_ready, exp_ready, gate_ready = sem("chain_g"), sem("less_ready"), sem("exp_ready"), sem("gate_ready")
        gate_turned, gateT_ready, gates_stored = sem("gate_turned"), sem("gateT_ready"), sem("gates_stored")
        logits = LG[:, :, :].rearrange("p m (g e) -> p (m g) e", e=EXPERTS)

        def each(t):
            return t[:, :].unsqueeze(2).to_broadcast([P, GROUPS, EXPERTS])

        with nc.Block() as block:
            @block.vector
            def _(dve):
                count = [0]

                def then(ins):
                    count[0] += 1
                    ins.then_inc(chain, 1)
                    dve.wait_ge(chain, count[0])

                rank = CST[:, C_RANK:C_RANK + EXPERTS].unsqueeze(1).to_broadcast([P, GROUPS, EXPERTS])

                def pick(chosen, source, best):
                    then(dve.tensor_reduce(best[:, :], source[:, :, :], AX_X, ALU.max))
                    then(dve.tensor_tensor(chosen[:, :, :], source[:, :, :], each(best), ALU.is_equal))
                    then(dve.tensor_tensor(chosen[:, :, :], chosen[:, :, :], rank, ALU.mult))
                    then(dve.tensor_reduce(most[:, :], chosen[:, :, :], AX_X, ALU.max))
                    then(dve.tensor_tensor(chosen[:, :, :], chosen[:, :, :], each(most), ALU.is_equal))

                then(dve.tensor_reduce(most[:, :], logits, AX_X, ALU.max))
                dve.tensor_tensor(prob[:, :, :], logits, each(most), ALU.subtract).then_inc(less_ready, 1)
                dve.wait_ge(exp_ready, 1)
                then(dve.tensor_reduce(total[:, :], prob[:, :, :], AX_X, ALU.add))
                then(dve.reciprocal(total[:, :], total[:, :]))
                then(dve.tensor_tensor(prob[:, :, :], prob[:, :, :], each(total), ALU.mult))
                pick(first, prob, top1)
                then(dve.scalar_tensor_tensor(spare[:, :, :], first[:, :, :], -2.0, prob[:, :, :], ALU.mult, ALU.add))
                pick(second, spare, top2)
                then(dve.tensor_tensor(first[:, :, :], first[:, :, :], second[:, :, :], ALU.add))
                then(dve.tensor_tensor(first[:, :, :], first[:, :, :], prob[:, :, :], ALU.mult))
                then(dve.tensor_tensor(total[:, :], top1[:, :], top2[:, :], ALU.add))
                then(dve.tensor_scalar(total[:, :], total[:, :], 1e-9, None, ALU.add))
                then(dve.reciprocal(total[:, :], total[:, :]))
                for q in range(BLK):
                    chosen = first[:, :, :].rearrange("p (m q a) e -> p q m a e", q=BLK, a=2)[:, q]
                    by = each(total).rearrange("p (m q a) e -> p q m a e", q=BLK, a=2)[:, q]
                    for a in range(2):
                        dve.tensor_tensor(gate[:, :, a, :, q], chosen[:, :, a], by[:, :, a], ALU.mult).then_inc(gate_ready, 1)
                for half in range(2):
                    dve.wait_ge(gate_turned, (half + 1) * BLK)
                    dve.tensor_copy(gateT[:, half].rearrange("p b t -> p (b t)"), banks[half][:, :]).then_inc(gateT_ready, 1)

            @block.scalar
            def _(act):
                act.wait_ge(less_ready, 1)
                act.activation(prob[:, :, :], prob[:, :, :], ACT.Exp).then_inc(exp_ready, 1)

            @block.tensor
            def _(pe):
                pe.wait_ge(gate_ready, 2 * BLK)
                cols = gate[:, :, :, :, :].rearrange("p m a e q -> p (m a e q)")
                for b in range(2 * BLK):
                    pe.transpose(banks[b // BLK][:, b % BLK * P:(b % BLK + 1) * P], cols[:, b * P:(b + 1) * P], ident).then_inc(gate_turned, 1)

            @block.sync
            def _(sp):
                sp.wait_ge(gateT_ready, 2)
                flat_gates = gates.rearrange("m a e (q t) -> (m a e q) t", t=P)
                sp.dma_start(flat_gates.rearrange("(b r) t -> r b t", r=P), gateT[:, :, :, :].rearrange("p h b t -> p (h b) t")).then_inc(gates_stored, 16)
                sp.wait_ge(gates_stored, 16)


DUO = 2 * HID
CHUNKS = [(c, min(P, DUO - c)) for c in range(0, DUO, P)]


def experts(nc, sem, banks, H, W, FS, gates, w13, w2, out, ident, vec):
    DUOS = EXPERTS // 2
    RING = DUOS
    UNITS = PAIRS * DUOS
    NC_ = 2 * len(CHUNKS)
    COLS = 2 * EXPERTS * HID
    DOWN = 1.0 / (X_SCALE * W_SCALE)
    with ExitStack() as ctx:
        def sb(name, shape, dt=F32):
            return ctx.enter_context(nc.sbuf_tensor(name, shape, dt))

        whi, wlo = sb("whi", [P, COLS], F16), sb("wlo", [P, COLS], F16)
        W2 = sb("w2", [P, 2 * EXPERTS, D])
        gate = sb("x_gate", [P, RING, 2, SEQ])
        s = sb("x_s", [P, 2, SEQ])
        hh = sb("x_hh", [P, 2, NC_, SEQ])
        part = sb("x_part", [P, 2, SEQ])
        acc = sb("x_acc", [P, SEQ])
        outsb = sb("outsb", [P, SEQ])
        wraw = hh[:, :, :, :].rearrange("p a c s -> p (a c s)")[:, 0:COLS]
        names = ("w13", "w2", "scaled", "whi", "wlo", "H1", "H3", "s", "hh", "O", "part", "acc", "turned", "out")
        done = {n: sem(f"moe_{n}") for n in names}
        gate_loaded = [sem(f"gate_loaded{u}") for u in range(RING)]
        stored = sem("stored")
        bk_h1, bk_h3, bk_o, bk_t = banks[0:2], banks[2:4], banks[4:6], banks[6]
        out_v = out.rearrange("r (q p) f -> r p q f", p=P)
        STAGES = 3

        with nc.Block() as block:
            @block.sync
            def _(sp):
                for a in range(2):
                    sp.dma_start(wraw[a * D:(a + 1) * D, :], w13.rearrange("d j h -> d (j h)")).then_inc(done["w13"], 16)
                sp.dma_start(W2[:, :, :], w2).then_inc(done["w2"], 16)
                for n, u, i in pipeline(sp, UNITS, STAGES, RING, 2 * RING):
                    if live(n, 0, UNITS):
                        wait(sp, done["part"], (n - RING + 1) * 2)
                        for a in range(2):
                            src = gates[bass.ds(i, 1), a, 2 * u:2 * u + 2, :].rearrange("o e s -> (o e) s").partition_broadcast(D)
                            sp.dma_start(gate[a * D:(a + 1) * D, u], src).then_inc(gate_loaded[u], 16)
                    if live(n, 2, UNITS) and u == 1:
                        pair = i - 1
                        wait(sp, done["out"], pair + 1)
                        for a in range(2):
                            sp.dma_start(out_v[bass.ds(2 * pair + a, 1)].rearrange("o p q f -> (o p) q f"),
                                         outsb[:, :].rearrange("p (q a f) -> p q a f", q=BLK, a=2)[:, :, a]).then_inc(stored, 16)
                sp.wait_ge(stored, ROWS * 16)

            @block.tensor
            def _(pe):
                pe.wait_ge(done["w2"], 16)
                pe.wait_ge(done["wlo"], 1)

                def hidden(n, u, i, t):
                    c, a = t // 2, t % 2
                    at, rows = CHUNKS[c]
                    for bank, name, layer, reader in ((bk_h1, "H1", 0, "s"), (bk_h3, "H3", 1, "hh")):
                        wait(pe, done[reader], n * NC_ + t - 1)
                        cols = slice(layer * EXPERTS * HID + u * DUO + at, layer * EXPERTS * HID + u * DUO + at + rows)
                        x = tile_of(FS, 2 * i + a)
                        pe.matmul(bank[t % 2][0:rows, :], whi[:, cols], x, start=True, stop=False)
                        pe.matmul(bank[t % 2][0:rows, :], wlo[:, cols], x, start=False, stop=True).then_inc(done[name], 1)

                def output(m, u, e):
                    wait(pe, done["hh"], m * NC_ + (4 if e == 0 else 6))
                    wait(pe, done["part"], m * 2 + e - 1)
                    for j, c in enumerate((0, 1) if e == 0 else (1, 2)):
                        rows = CHUNKS[c][1]
                        for a in range(2):
                            mm = pe.matmul(bk_o[e][a * D:(a + 1) * D, :], W2[0:rows, 4 * ((u - 1) % RING) + 2 * e + j, :],
                                           hh[0:rows, (u - 1) % 2, 2 * c + a, :], start=j == 0, stop=j == 1, skip_group_check=True)
                    mm.then_inc(done["O"], 1)

                for n, u, i in pipeline(pe, UNITS, STAGES, RING, 2 * RING):
                    for t in range(NC_):
                        if live(n, 0, UNITS):
                            hidden(n, u, i, t)
                        if live(n, 1, UNITS) and t == 1:
                            output(n - 1, u, 0)
                        if live(n, 1, UNITS) and t == 2:
                            output(n - 1, u, 1)
                        if live(n, 2, UNITS) and u == 1 and t == 1:
                            pair = i - 1
                            wait(pe, done["acc"], (pair + 1) * EXPERTS)
                            wait(pe, done["out"], pair)
                            for q in range(BLK):
                                mm = pe.transpose(bk_t[:, q * P:(q + 1) * P], acc[:, q * P:(q + 1) * P], ident)
                            mm.then_inc(done["turned"], 1)

            @block.scalar
            def _(act):
                act.preload_act_table_set("silu_and_others")
                act.wait_ge(done["scaled"], 1)
                act.activation(whi[:, :], wraw, ACT.Identity).then_inc(done["whi"], 1)
                for n, u, i in pipeline(act, UNITS, STAGES, RING, 2 * RING):
                    for t in range(NC_):
                        if live(n, 0, UNITS):
                            rows = CHUNKS[t // 2][1]
                            wait(act, done["H1"], n * NC_ + t + 1)
                            wait(act, done["hh"], n * NC_ + t - 1)
                            act.activation(s[0:rows, t % 2, :], bk_h1[t % 2][0:rows, :], ACT.Silu, scale=DOWN).then_inc(done["s"], 1)
                    if live(n, 2, UNITS) and u == 1:
                        pair = i - 1
                        wait(act, done["turned"], pair + 1)
                        wait(act, stored, pair * 32)
                        act.activation(outsb[:, :], bk_t[:, :], ACT.Identity).then_inc(done["out"], 1)

            @block.gpsimd
            def _(pool):
                for n, u, i in pipeline(pool, UNITS, STAGES, RING, 2 * RING):
                    if live(n, 1, UNITS):
                        m, x = n - 1, (u - 1) % RING
                        pair = i + (u - 1) // RING
                        for e in range(2):
                            k = m * 2 + e
                            wait(pool, done["part"], k + 1)
                            if x == 0 and e == 0:
                                wait(pool, done["turned"], pair)
                                pool.tensor_tensor(acc[:, :], part[:, e, :], tile_of(H, pair), ALU.add).then_inc(done["acc"], 1)
                            else:
                                wait(pool, done["acc"], k)
                                pool.tensor_tensor(acc[:, :], acc[:, :], part[:, e, :], ALU.add).then_inc(done["acc"], 1)

            @block.vector
            def _(dve):
                dve.wait_ge(done["w13"], 32)
                dve.tensor_scalar(wraw, wraw, vec(V_LN2), W_SCALE, ALU.mult, ALU.mult).then_inc(done["scaled"], 1)
                dve.wait_ge(done["whi"], 1)
                dve.tensor_tensor(wlo[:, :], wraw, whi[:, :], ALU.subtract).then_inc(done["wlo"], 1)
                dve.wait_ge(done["wlo"], 1)

                def gating(n, u, i, e):
                    m, x = n - 1, (u - 1) % RING
                    dve.wait_ge(gate_loaded[x], turns(i, u, 1, RING) * 32)
                    wait(dve, done["O"], m * 2 + e + 1)
                    wait(dve, done["acc"], m * 2 + e - 1)
                    dve.tensor_tensor(part[:, e, :], bk_o[e][:, :], gate[:, x, e, :], ALU.mult).then_inc(done["part"], 1)

                for n, u, i in pipeline(dve, UNITS, STAGES, RING, 2 * RING):
                    for t in range(NC_):
                        if live(n, 0, UNITS):
                            rows = CHUNKS[t // 2][1]
                            wait(dve, done["s"], n * NC_ + t + 1)
                            wait(dve, done["H3"], n * NC_ + t + 1)
                            wait(dve, done["O"], (n - 1) * 2)
                            dve.scalar_tensor_tensor(hh[0:rows, u % 2, t, :], bk_h3[t % 2][0:rows, :], DOWN, s[0:rows, t % 2, :],
                                                     ALU.mult, ALU.mult).then_inc(done["hh"], 1)
                        if live(n, 1, UNITS) and t in (2, 3):
                            gating(n, u, i, t - 2)


def lay_out(a):
    fixed = shape_constants()
    places = np.stack([a["L0_tok_instr_emb"][:SEQ], a["L0_tok_arg_emb"][:SEQ]])
    places = places.reshape(2 * BLK, P, D).transpose(1, 0, 2)
    w13 = np.stack([a["L0_ffn_w1"], a["L0_ffn_w3"]]).transpose(3, 0, 1, 2).reshape(D, 2, EXPERTS * HID)
    w2 = np.zeros((P, 2 * EXPERTS, D), np.float32)
    for e in range(EXPERTS):
        w, at = a["L0_ffn_w2"][e].T, e % 2 * HID
        for j, (c, rows) in enumerate(CHUNKS[e % 2:e % 2 + 2]):
            low, high = max(c, at), min(c + rows, at + HID)
            w2[low - c:high - c, 2 * e + j] = w[low - at:high - at]
    return {"ids": a["x"], "token_emb": a["L0_tok_token_emb"], "place_emb": np.ascontiguousarray(places),
            "weights": pack_weights(a), "w13": np.ascontiguousarray(w13), "w2": w2, **fixed}


def kernel(**inputs):
    import concourse.bacc as bacc
    from concourse.bass_utils import run_bass_kernel_spmd

    nc = bacc.Bacc("TRN2", target_bir_lowering=False, num_devices=1)
    arrays, args = {}, []
    for name, a in lay_out({k: np.asarray(v) for k, v in inputs.items()}).items():
        arrays[f"in_{name}"] = a = np.ascontiguousarray(a)
        args.append(nc.dram_tensor(f"in_{name}", a.shape, mybir.dt.from_np(a.dtype), kind="ExternalInput").ap())
    out = nc.dram_tensor("out_0", [ROWS, SEQ, D], F32, kind="ExternalOutput").ap()
    tower(nc, *args, out)
    return run_bass_kernel_spmd(nc, [arrays], core_ids=[0]).results[0]["out_0"]
```

```python
from contextlib import ExitStack

import numpy as np
import concourse.bass as bass
from concourse import mybir

F32 = mybir.dt.float32
F16 = mybir.dt.float16
BF16 = mybir.dt.bfloat16
I32 = mybir.dt.int32
ALU = mybir.AluOpType
ACT = mybir.ActivationFunctionType
AX_X = mybir.AxisListType.X

P = 128
ROWS, SEQ, D = 32, 512, 64
PAIRS = ROWS // 2
BLK = SEQ // P
NEXT_ID = 5
EPS_LN, EPS_RMS = 1e-5, 1e-6
LR, WD, MAX_ALR, EPS_ADAM = 0.001, 0.01, 0.1, 1e-8
HEADS, KV, HD = 4, 2, 16
EXPERTS, HID = 8, 170
NEG = -1e30

WIDTH = [SEQ - P * c for c in range(BLK)]
START = [sum(WIDTH[:c]) for c in range(BLK)]
TRAP = sum(WIDTH)

C_ID, C_CENTRE, C_MEAN, C_FOLD, C_DEN = (P * j for j in range(5))
C_IOTA = 5 * P
C_EPS_LN, C_EPS_RMS = C_IOTA + BLK, C_IOTA + BLK + 1
C_RANK = C_EPS_RMS + 1
C_COLS = C_RANK + EXPERTS


def shape_constants():
    p = np.arange(P)
    same_half = (p[:, None] // D == p[None, :] // D).astype(np.float32)
    c = np.zeros((P, C_COLS), np.float32)
    c[:, C_ID:C_ID + P] = np.eye(P)
    c[:, C_CENTRE:C_CENTRE + P] = np.eye(P) - same_half / D
    c[:, C_MEAN:C_MEAN + P] = same_half / D
    c[:, C_FOLD:C_FOLD + P] = p[:, None] % D == p[None, :] % D
    c[:, C_DEN:C_DEN + P] = (p[:, None] // 32 == p[None, :] // 32) & (p[:, None] % 32 == HD)
    c[:, C_IOTA:C_IOTA + BLK] = p[:, None] + P * np.arange(BLK)[None, :]
    c[:, C_EPS_LN] = EPS_LN
    c[:, C_EPS_RMS] = EPS_RMS
    c[:, C_RANK:C_RANK + EXPERTS] = EXPERTS - np.arange(EXPERTS)
    position = np.tile(np.arange(SEQ, dtype=np.float32), (ROWS, 1))
    inv_freq = 1.0 / 10000.0 ** (np.arange(0, HD, 2, dtype=np.float32) / HD)
    angle = np.outer(np.arange(SEQ, dtype=np.float32), inv_freq)
    angle = np.concatenate([angle, angle], axis=-1)
    sign = np.where(np.arange(HD) < HD // 2, -1.0, 1.0).astype(np.float32)
    cos, sin = np.cos(angle).T, np.sin(angle).T * sign[:, None]
    scale = np.float32(HD ** -0.5)
    turn = [np.tile(np.repeat(t, heads, axis=0), (P // (HD * heads), 1))
            for t, heads in ((cos * scale, HEADS), (sin * scale, HEADS), (cos, KV), (sin, KV))]
    turn = np.stack(turn, axis=1).astype(np.float32)
    causal = np.where(p[:, None] <= p[None, :], 0.0, NEG).astype(np.float32)
    return {"consts": c, "position": position, "turn": np.ascontiguousarray(turn), "causal": causal}


def wait(eng, sem, count):
    if isinstance(count, int) and count <= 0:
        return
    eng.wait_ge(sem, count)


def live(n, stage, tiles):
    return not isinstance(n, int) or 0 <= n - stage < tiles


def pipeline(eng, tiles, stages, ring=2, first=0):
    first = first or (stages + ring) // ring * ring
    for n in range(first):
        yield n, n % ring, n // ring
    with eng.Fori(first // ring, tiles // ring) as i:
        for u in range(ring):
            yield ring * i + u, u, i
    for n in range(tiles, tiles + stages - 1):
        yield n, n % ring, n // ring


def turns(i, u, stage=0, ring=2):
    return i + (u - stage) // ring + 1



(W_K, W_Q, W_V, W_LR, W_0, W_1, W_1T, W_FQ, W_FQR) = (P * j for j in range(9))
W_01 = 9 * P
W_FK, W_FKR, W_FV, W_O = (W_01 + P + D * j for j in range(4))
W_ROUTE = W_O + D
V_GAMMA, V_BETA, V_B0, V_B1, V_BLR, V_LN1, V_LN2 = (W_ROUTE + 2 * EXPERTS + j for j in range(7))
W_COLS = V_LN2 + 1


def diagonal(w):
    k, m = w.shape
    out = np.zeros((2 * k, 2 * m), np.float32)
    out[:k, :m] = w
    out[k:, m:] = w
    return out


def twice(w):
    return np.concatenate([w, w], axis=0)


def pack_weights(a):
    ws, bs = a["L0_attn_Ws"], a["L0_attn_bs"]
    swap = np.arange(D).reshape(-1, 2, HD // 2)[:, ::-1].reshape(-1)
    by_dim = {n: np.arange(n * HD).reshape(n, HD).T.reshape(-1) for n in (HEADS, KV)}
    fq, fk, fv = a["L0_ffn_wq"].T, a["L0_ffn_wk"].T, a["L0_ffn_wv"].T
    wo = np.zeros((P, D), np.float32)
    for h in range(HEADS):
        wo[32 * h:32 * h + HD] = a["L0_ffn_wo"].T[HD * h:HD * (h + 1)]
    vectors = [a["L0_tok_gamma"], a["L0_tok_beta"], bs[0], bs[1], np.repeat(a["L0_attn_blr"], D),
               a["L0_ffn_ln1_w"], a["L0_ffn_ln2_w"]]
    parts = [diagonal(w) for w in (a["L0_attn_Wk"], a["L0_attn_Wq"], a["L0_attn_Wv"],
                                   np.repeat(a["L0_attn_Wlr"], D, axis=1), ws[0], ws[1], ws[1].T,
                                   fq[:, by_dim[HEADS]], fq[:, swap[by_dim[HEADS]]])]
    parts += [twice(ws[0]), twice(ws[1])]
    parts += [diagonal(w) for w in (fk[:, by_dim[KV]], fk[:, swap[by_dim[KV]]], fv)]
    parts += [wo, diagonal(a["L0_ffn_router_w"].T)]
    parts += [twice(v[:, None]) for v in vectors]
    return np.ascontiguousarray(np.concatenate(parts, axis=1))


def tower(nc, ids, token_emb, place_emb, weights, w13, w2, consts, position, turn, causal, out):
    ctx = ExitStack()
    with ctx:
        def sb(name, shape, dt=F32):
            return ctx.enter_context(nc.sbuf_tensor(name, shape, dt))

        sems = []

        def sem(name):
            sems.append(nc.alloc_semaphore(name=name))
            return sems[-1]

        def recycle():
            nc.all_engine_barrier()
            nc.clear_and_free_semaphores(sems)
            sems.clear()
            nc.all_engine_barrier()

        banks = [ctx.enter_context(nc.psum_tensor(f"bank{j}", [P, SEQ], F32)) for j in range(8)]

        H = sb("H", [P, PAIRS, SEQ])
        XN = sb("XN", [P, PAIRS, SEQ])
        CST = sb("CST", [P, C_COLS])
        W = sb("W", [P, W_COLS])

        def wcols(at, cols=P):
            return W[:, at:at + cols]

        def vec(at):
            return W[:, at:at + 1]

        ident = CST[:, C_ID:C_ID + P]
        centre = CST[:, C_CENTRE:C_CENTRE + P]
        mean = CST[:, C_MEAN:C_MEAN + P]
        fold = CST[:, C_FOLD:C_FOLD + P]
        eps_ln = CST[:, C_EPS_LN:C_EPS_LN + 1]
        eps_rms = CST[:, C_EPS_RMS:C_EPS_RMS + 1]

        embed(nc, sb, sem, banks, ids, token_emb, place_emb, weights, consts, position,
              H, XN, CST, W, ident, centre, mean, eps_ln, vec)
        with ExitStack() as inner:
            NW, NB = learn(nc, inner, sem, banks, XN, W, wcols, vec, ident, fold)
            retrieve(nc, inner, sem, banks, XN, H, W, wcols, NW, NB)
        recycle()
        with ExitStack() as inner:
            VT = inner.enter_context(nc.sbuf_tensor("VT", [P, PAIRS, BLK * 2 * KV * HD], F32))
            q_parts = nc.dram_tensor("q_parts", [PAIRS, 3, 2, HD, HEADS, SEQ], BF16, kind="Internal").ap()
            k_parts = nc.dram_tensor("k_parts", [PAIRS, 3, 2, HD, KV, SEQ], BF16, kind="Internal").ap()
            parts_stored = [sem(f"parts_stored{u}") for u in range(2)]
            K = inner.enter_context(nc.sbuf_tensor("t_k", [KEY_ROWS, KEY_RING, KV, SEQ], BF16))
            V = inner.enter_context(nc.sbuf_tensor("t_v", [P, 2, BLK, KV, 32], F32))
            mask, eye = (inner.enter_context(nc.sbuf_tensor(n, [P, P], BF16)) for n in ("mask", "eye"))
            project(nc, sem, banks, H, XN, W, VT, q_parts, k_parts, parts_stored, turn, causal, K, V, mask, eye,
                    ident, centre, mean, eps_ln, eps_rms, vec)
            attend(nc, sem, banks, H, XN, W, VT, q_parts, k_parts, parts_stored, K, V, mask, eye, ident)
        recycle()
        with ExitStack() as inner:
            FS = inner.enter_context(nc.sbuf_tensor("FS", [P, ROWS, SEQ], F16))
            gates = nc.dram_tensor("gates", [PAIRS, 2, EXPERTS, SEQ], F32, kind="Internal").ap()
            whi, wlo = (inner.enter_context(nc.sbuf_tensor(n, [P, 2 * EXPERTS * HID], F16)) for n in ("whi", "wlo"))
            v2hi, v2lo = (inner.enter_context(nc.sbuf_tensor(n, [P, 2 * EXPERTS, D], F16)) for n in ("v2hi", "v2lo"))
            route(nc, sem, banks, XN, W, CST, FS, gates, w13, w2, whi, wlo, v2hi, v2lo, ident, mean, eps_rms, vec)
            experts(nc, sem, banks, H, XN, FS, gates, whi, wlo, v2hi, v2lo, out, ident)


def embed(nc, sb_, sem, banks, ids, token_emb, place_emb, weights, consts, position,
          H, XN, CST, W, ident, centre, mean, eps_ln, vec):
    ids16 = nc.dram_tensor("ids16", [2, ROWS, SEQ], F16, kind="Internal").ap()
    with ExitStack() as ctx:
        def sb(name, shape, dt=F32):
            return ctx.enter_context(nc.sbuf_tensor(name, shape, dt))

        pos = sb("pos", [ROWS, SEQ])
        xi = sb("xi", [ROWS, SEQ], I32)
        xf = sb("xf", [ROWS, SEQ])
        starts = sb("starts", [ROWS, SEQ])
        ones = sb("ones", [ROWS, SEQ])
        seg = sb("seg", [ROWS, SEQ])
        last = sb("last", [ROWS, SEQ])
        place16 = sb("place16", [ROWS, 2, SEQ], F16)
        tokid = sb("tokid", [P, PAIRS, BLK * 2], I32)
        pemb = sb("pemb", [P, 2 * BLK, D])
        prest = sb("prest", [P, 2 * BLK, D])
        table = sb("table", [P, 3, 2 * BLK, D], BF16)
        tokcol = sb("tokcol", [P, 2, BLK * 2], I32)
        tok = sb("tok", [P, 2, BLK, 2, D])
        where = sb("where", [P, 2, 2, 2, SEQ], F16)
        onehot = sb("onehot", [P, 2, 2, 2 * TRAP], BF16)
        x = sb("x", [P, 2, SEQ])
        sq1, sq2, ln1, ln2, r1, r2 = (sb(n, [P, SEQ]) for n in ("sq1", "sq2", "ln1", "ln2", "r1", "r2"))
        normed = sb("normed", [P, SEQ])

        loaded, xloaded, ploaded = sem("loaded"), sem("xloaded"), sem("ploaded")
        step, ids_turned, tok_ready, places_stored = sem("step"), sem("ids_turned"), sem("tok_ready"), sem("places_stored")
        places_ready, table_ready, table_step = sem("places_ready"), sem("table_ready"), sem("table_step")
        col_ready, col_seen, gathered = sem("col_ready"), sem("col_seen"), [sem(f"gathered{u}") for u in range(2)]
        where_loaded, onehot_ready, embedded, x_ready = [sem(f"where_loaded{u}") for u in range(2)], sem("onehot_ready"), sem("embedded"), sem("x_ready")
        c1_done, sq1_done, v1_done, ln1_done, r1_done, n1_done, h_done = (sem(f"{n}_a") for n in ("c", "sq", "v", "ln", "r", "n", "h"))
        c2_done, sq2_done, v2_done, ln2_done, r2_done, xn_done = (sem(f"{n}_b") for n in ("c", "sq", "v", "ln", "r", "xn"))

        ps_x, ps_c1, ps_c2, ps_v1, ps_v2 = banks[0], banks[1:3], banks[3:5], banks[5], banks[6]
        ids_turn = banks[7]
        STAGES = 4

        with nc.Block() as block:
            @block.sync
            def _(sp):
                sp.dma_start(xi[:, :], ids).then_inc(xloaded, 16)
                sp.dma_start(pos[:, :], position).then_inc(xloaded, 16)
                sp.dma_start(CST[:, :], consts).then_inc(loaded, 16)
                sp.dma_start(pemb[:, :, :], place_emb).then_inc(ploaded, 16)
                sp.dma_start(W[:, :], weights).then_inc(loaded, 16)
                sp.wait_ge(places_ready, 2)
                sp.dma_start(ids16.rearrange("t r s -> r t s"), place16[:, :, :]).then_inc(places_stored, 16)
                sp.wait_ge(places_stored, 16)
                for n, u, i in pipeline(sp, PAIRS, STAGES):
                    if live(n, 0, PAIRS):
                        wait(sp, onehot_ready, n - 1)
                        sp.dma_start(where[:, u], ids16[:, bass.ds(2 * n, 2), :].partition_broadcast(P)).then_inc(where_loaded[u], 16)

            @block.gpsimd
            def _(pool):
                pool.wait_ge(tok_ready, 1)
                for n, u, i in pipeline(pool, PAIRS, STAGES):
                    if live(n, 0, PAIRS):
                        wait(pool, embedded, n - 1)
                        pool.sem_inc(col_seen, 1)
                        pool.tensor_copy(tokcol[:, u, :], tokid[:, bass.ds(n, 1), :].rearrange("p a b -> p (a b)")).then_inc(col_ready, 1)
                        wait(pool, col_ready, n + 1)
                        pool.sem_inc(col_seen, 1)
                        for q in range(BLK):
                            for a in range(2):
                                pool.indirect_dma_start(
                                    out=tok[:, u, q, a, :], out_offset=None, in_=token_emb,
                                    in_offset=bass.IndirectOffsetOnAxis(ap=tokcol[:, u, 2 * q + a:2 * q + a + 1], axis=0),
                                ).then_inc(gathered[u], 16)

            @block.vector
            def _(dve):
                count = [0]

                def then(ins):
                    count[0] += 1
                    ins.then_inc(step, 1)
                    dve.wait_ge(step, count[0])

                then(dve.memset(ones[:, :], 1.0))
                then(dve.memset(starts[:, :], 0.0))
                dve.wait_ge(xloaded, 32)
                then(dve.tensor_copy(xf[:, :], xi[:, :]))
                then(dve.tensor_scalar(starts[:, 1:SEQ], xf[:, 0:SEQ - 1], float(NEXT_ID), None, ALU.is_equal))
                dve.tensor_tensor_scan(place16[:, 0, :], ones[:, :], starts[:, :], 0.0, ALU.mult, ALU.add).then_inc(places_ready, 1)
                then(dve.tensor_tensor(seg[:, :], starts[:, :], pos[:, :], ALU.mult))
                then(dve.tensor_tensor_scan(last[:, :], seg[:, :], seg[:, :], 0.0, ALU.max, ALU.max))
                dve.tensor_tensor(place16[:, 1, :], pos[:, :], last[:, :], ALU.subtract).then_inc(places_ready, 1)
                dve.wait_ge(ids_turned, BLK)
                dve.tensor_copy(tokid[:, :, :].rearrange("p m (q a) -> p q m a", a=2),
                                ids_turn[:, 0:BLK * ROWS].rearrange("p (q m a) -> p q m a", q=BLK, a=2)).then_inc(tok_ready, 1)
                dve.wait_ge(ploaded, 16)
                then(dve.tensor_copy(table[:, 0], pemb[:, :, :]))
                then(dve.tensor_tensor(prest[:, :, :], pemb[:, :, :], table[:, 0], ALU.subtract))
                then(dve.tensor_copy(table[:, 1], prest[:, :, :]))
                dve.tensor_tensor(table[:, 2], prest[:, :, :], table[:, 1], ALU.subtract).then_inc(table_ready, 1)
                dve.wait_ge(loaded, 32)
                for n, u, i in pipeline(dve, PAIRS, STAGES):
                    if live(n, 0, PAIRS):
                        dve.wait_ge(where_loaded[u], turns(i, u) * 16)
                        wait(dve, embedded, n - 1)
                        for t in range(2):
                            for c in range(BLK):
                                at, w = 2 * START[c], WIDTH[c]
                                mark = dve.tensor_scalar(
                                    onehot[:, u, t, at:at + 2 * w].rearrange("p (a s) -> p a s", a=2),
                                    where[:, u, t, :, SEQ - w:], CST[:, C_IOTA + c:C_IOTA + c + 1], None, ALU.is_equal)
                        mark.then_inc(onehot_ready, 1)
                    if live(n, 2, PAIRS):
                        m = n - 2
                        dve.wait_ge(r1_done, m + 1)
                        wait(dve, h_done, m)
                        dve.tensor_tensor(normed[:, :], ps_c1[u][:, :], r1[:, :], ALU.mult).then_inc(n1_done, 1)
                        dve.wait_ge(n1_done, m + 1)
                        dve.tensor_scalar(H[:, bass.ds(m, 1), :].rearrange("p a s -> p (a s)"), normed[:, :], vec(V_GAMMA), vec(V_BETA), ALU.mult, ALU.add).then_inc(h_done, 1)
                    if live(n, 3, PAIRS):
                        m, v = n - 3, 1 - u
                        dve.wait_ge(r2_done, m + 1)
                        dve.tensor_tensor(XN[:, bass.ds(m, 1), :].rearrange("p a s -> p (a s)"), ps_c2[v][:, :], r2[:, :], ALU.mult).then_inc(xn_done, 1)

            @block.tensor
            def _(pe):
                pe.wait_ge(loaded, 32)
                pe.wait_ge(step, 3)
                for q in range(BLK):
                    pe.transpose(ids_turn[:, q * ROWS:(q + 1) * ROWS], xf[:, q * P:(q + 1) * P], ident[0:ROWS, 0:ROWS]).then_inc(ids_turned, 1)
                pe.wait_ge(table_ready, 1)
                for n, u, i in pipeline(pe, PAIRS, STAGES):
                    if live(n, 2, PAIRS):
                        m = n - 2
                        pe.wait_ge(x_ready, m + 1)
                        wait(pe, n1_done, m - 1)
                        pe.matmul(ps_c1[u][:, :], centre, x[:, u, :], start=True, stop=True).then_inc(c1_done, 1)
                    if live(n, 3, PAIRS):
                        m, v = n - 3, 1 - u
                        pe.wait_ge(h_done, m + 1)
                        wait(pe, xn_done, m - 1)
                        pe.matmul(ps_c2[v][:, :], centre, H[:, bass.ds(m, 1), :].rearrange("p a s -> p (a s)"), start=True, stop=True).then_inc(c2_done, 1)
                    if live(n, 1, PAIRS):
                        m, v = n - 1, 1 - u
                        pe.wait_ge(gathered[v], turns(i, u, 1) * 2 * BLK * 16)
                        wait(pe, x_ready, m)
                        for q in range(BLK):
                            pe.matmul(ps_x[:, q * P:(q + 1) * P], tok[:, v, q].rearrange("p a f -> p (a f)"), ident,
                                      start=(q == 0), stop=False, skip_group_check=True)
                        pe.wait_ge(onehot_ready, m + 1)
                        for t in range(2):
                            for part in range(3):
                                for c in range(BLK):
                                    w = WIDTH[c]
                                    for a in range(2):
                                        at = 2 * START[c] + a * w
                                        mm = pe.matmul(ps_x[a * D:(a + 1) * D, SEQ - w:], table[:, part, t * BLK + c, :],
                                                       onehot[:, v, t, at:at + w], start=False, stop=False, skip_group_check=True)
                        mm.then_inc(embedded, 1)
                    if live(n, 2, PAIRS):
                        m = n - 2
                        pe.wait_ge(sq1_done, m + 1)
                        wait(pe, ln1_done, m)
                        pe.matmul(ps_v1[:, :], mean, sq1[:, :], start=True, stop=True).then_inc(v1_done, 1)
                    if live(n, 3, PAIRS):
                        m = n - 3
                        pe.wait_ge(sq2_done, m + 1)
                        wait(pe, ln2_done, m)
                        pe.matmul(ps_v2[:, :], mean, sq2[:, :], start=True, stop=True).then_inc(v2_done, 1)

            @block.scalar
            def _(act):
                act.preload_act_table_set("natural_log_exp_and_others")
                act.wait_ge(loaded, 32)
                for n, u, i in pipeline(act, PAIRS, STAGES):
                    if live(n, 2, PAIRS):
                        m = n - 2
                        act.wait_ge(c1_done, m + 1)
                        wait(act, v1_done, m)
                        act.activation(sq1[:, :], ps_c1[u][:, :], ACT.Square).then_inc(sq1_done, 1)
                    if live(n, 3, PAIRS):
                        m, v = n - 3, 1 - u
                        act.wait_ge(c2_done, m + 1)
                        wait(act, v2_done, m)
                        act.activation(sq2[:, :], ps_c2[v][:, :], ACT.Square).then_inc(sq2_done, 1)
                    if live(n, 1, PAIRS):
                        m, v = n - 1, 1 - u
                        act.wait_ge(embedded, m + 1)
                        wait(act, c1_done, m - 1)
                        act.activation(x[:, v, :], ps_x[:, :], ACT.Identity).then_inc(x_ready, 1)
                    if live(n, 2, PAIRS):
                        m = n - 2
                        act.wait_ge(v1_done, m + 1)
                        act.activation(ln1[:, :], ps_v1[:, :], ACT.Ln, bias=eps_ln).then_inc(ln1_done, 1)
                        act.wait_ge(ln1_done, m + 1)
                        wait(act, n1_done, m)
                        act.activation(r1[:, :], ln1[:, :], ACT.Exp, scale=-0.5).then_inc(r1_done, 1)
                    if live(n, 3, PAIRS):
                        m = n - 3
                        act.wait_ge(v2_done, m + 1)
                        act.activation(ln2[:, :], ps_v2[:, :], ACT.Ln, bias=eps_ln).then_inc(ln2_done, 1)
                        act.wait_ge(ln2_done, m + 1)
                        wait(act, xn_done, m)
                        act.activation(r2[:, :], ln2[:, :], ACT.Exp, scale=-0.5).then_inc(r2_done, 1)



def tile_of(big, m):
    return big[:, bass.ds(m, 1), :].rearrange("p a s -> p (a s)")


def learn(nc, outer, sem, banks, XN, W, wcols, vec, ident, fold):
    NW = outer.enter_context(nc.sbuf_tensor("NW", [P, 2, P], F32))
    NB = outer.enter_context(nc.sbuf_tensor("NB", [P, 2], F32))
    with ExitStack() as ctx:
        def sb(name, shape, dt=F32):
            return ctx.enter_context(nc.sbuf_tensor(name, shape, dt))

        k, tlr, s0, x1, w0, s1, t1 = (sb(f"m_{n}", [P, 2, SEQ]) for n in ("k", "tlr", "s0", "x1", "w0", "s1", "t1"))
        t0, u0, x2, e, g, u1, w1, dz1, dx1, dz0, kT, x1T, dz1T, dz0T = (
            sb(f"m_{n}", [P, SEQ]) for n in ("t0", "u0", "x2", "e", "g", "u1", "w1", "dz1", "dx1", "dz0", "kT", "x1T", "dz1T", "dz0T"))
        gbs = sb("gbs", [P, 2, PAIRS])
        half_b = sb("half_b", [P, 3])
        names = ("K", "L", "k", "tlr", "Z0", "s0", "t0", "x1", "u0", "w0", "Z1", "V", "s1", "t1", "x2", "e", "g", "u1", "w1",
                 "dz1", "B", "dx1", "dz0", "Tk", "Tx1", "Tdz1", "Tdz0", "kT", "x1T", "dz1T", "dz0T", "grads")
        done = {n: sem(f"learn_{n}") for n in names}
        half_ready, updated = sem("half_ready"), sem("updated")
        bk_z0, bk_z1, bk_v, bk_b, bk_t0, bk_t1, bk_t2, bk_grad = banks
        STAGES = 2

        with nc.Block() as block:
            @block.tensor
            def _(pe):
                def turn(bank, source, name):
                    for q in range(BLK):
                        mm = pe.transpose(bank[:, q * P:(q + 1) * P], source[:, q * P:(q + 1) * P], ident)
                    mm.then_inc(done[name], 1)

                for n, u, i in pipeline(pe, PAIRS, STAGES):
                    v, m = 1 - u, n - 1
                    front, back = live(n, 0, PAIRS), live(n, 1, PAIRS)
                    if front:
                        wait(pe, done["s0"], n)
                        wait(pe, done["t0"], n)
                        pe.matmul(bk_z0[:, :], wcols(W_K), tile_of(XN, n), start=True, stop=True).then_inc(done["K"], 1)
                        wait(pe, done["s1"], n)
                        wait(pe, done["t1"], n)
                        pe.matmul(bk_z1[:, :], wcols(W_LR), tile_of(XN, n), start=True, stop=True).then_inc(done["L"], 1)
                    if back:
                        wait(pe, done["dz0T"], m)
                        turn(bk_t0, k[:, v, :], "Tk")
                        wait(pe, done["x1T"], m)
                        turn(bk_t1, x1[:, v, :], "Tx1")
                    if front:
                        wait(pe, done["k"], n + 1)
                        pe.matmul(bk_z0[:, :], wcols(W_0), k[:, u, :], start=True, stop=True).then_inc(done["Z0"], 1)
                    if back:
                        wait(pe, done["dz1"], m + 1)
                        wait(pe, done["dx1"], m)
                        pe.matmul(bk_b[:, :], wcols(W_1T), dz1[:, :], start=True, stop=True).then_inc(done["B"], 1)
                        wait(pe, done["dz1T"], m)
                        turn(bk_t2, dz1, "Tdz1")
                    if front:
                        wait(pe, done["x1"], n + 1)
                        wait(pe, done["tlr"], n + 1)
                        pe.matmul(bk_z1[:, :], wcols(W_1), x1[:, u, :], start=True, stop=True).then_inc(done["Z1"], 1)
                        wait(pe, done["e"], n)
                        pe.matmul(bk_v[:, :], wcols(W_V), tile_of(XN, n), start=True, stop=True).then_inc(done["V"], 1)
                    if back:
                        wait(pe, done["dz0"], m + 1)
                        wait(pe, done["kT"], m + 1)
                        turn(bk_t0, dz0, "Tdz0")
                        wait(pe, done["x1T"], m + 1)
                        wait(pe, done["dz1T"], m + 1)
                        for q in range(BLK):
                            pe.matmul(bk_grad[:, P:2 * P], x1T[:, q * P:(q + 1) * P], dz1T[:, q * P:(q + 1) * P],
                                      start=isinstance(n, int) and m == 0 and q == 0, stop=False, skip_group_check=True)
                        wait(pe, done["dz0T"], m + 1)
                        for q in range(BLK):
                            mm = pe.matmul(bk_grad[:, 0:P], kT[:, q * P:(q + 1) * P], dz0T[:, q * P:(q + 1) * P],
                                           start=False, stop=False, skip_group_check=True)
                        mm.then_inc(done["grads"], 1)

            @block.scalar
            def _(act):
                act.preload_act_table_set("silu_and_others")
                act.wait_ge(half_ready, 1)

                def run(name, to, source, func, **more):
                    act.activation(to, source, func, **more).then_inc(done[name], 1)

                for n, u, i in pipeline(act, PAIRS, STAGES):
                    m = n - 1
                    front, back = live(n, 0, PAIRS), live(n, 1, PAIRS)
                    if front:
                        wait(act, done["K"], n + 1)
                        wait(act, done["Tk"], n - 1)
                        run("k", k[:, u, :], bk_z0[:, :], ACT.Identity)
                        wait(act, done["L"], n + 1)
                        wait(act, done["g"], n - 1)
                        run("tlr", tlr[:, u, :], bk_z1[:, :], ACT.Tanh, bias=half_b[:, 2:3], scale=0.5)
                    if back:
                        wait(act, done["grads"], m)
                        wait(act, done["Tk"], m + 1)
                        run("kT", kT[:, :], bk_t0[:, :], ACT.Identity)
                        wait(act, done["Tx1"], m + 1)
                        run("x1T", x1T[:, :], bk_t1[:, :], ACT.Identity)
                    if front:
                        wait(act, done["Z0"], n + 1)
                        wait(act, done["w0"], n - 1)
                        run("s0", s0[:, u, :], bk_z0[:, :], ACT.Silu, bias=vec(V_B0))
                        wait(act, done["u0"], n)
                        run("t0", t0[:, :], bk_z0[:, :], ACT.Tanh, bias=half_b[:, 0:1], scale=0.5)
                        wait(act, done["Z1"], n + 1)
                        wait(act, done["x2"], n - 1)
                        wait(act, done["w1"], n - 1)
                        run("s1", s1[:, u, :], bk_z1[:, :], ACT.Silu, bias=vec(V_B1))
                        run("t1", t1[:, u, :], bk_z1[:, :], ACT.Tanh, bias=half_b[:, 1:2], scale=0.5)
                    if back:
                        wait(act, done["Tdz0"], m + 1)
                        run("dz0T", dz0T[:, :], bk_t0[:, :], ACT.Identity)

            @block.gpsimd
            def _(pool):
                for n, u, i in pipeline(pool, PAIRS, STAGES):
                    if live(n, 1, PAIRS):
                        m, v = n - 1, 1 - u
                        wait(pool, done["s1"], m + 1)
                        wait(pool, done["e"], m)
                        pool.tensor_tensor(x2[:, :], x1[:, v, :], s1[:, v, :], ALU.add).then_inc(done["x2"], 1)

            @block.vector
            def _(dve):
                dve.tensor_scalar(half_b[:, 0:2], W[:, V_B0:V_B1 + 1], 0.5, None, ALU.mult)
                dve.tensor_scalar(half_b[:, 2:3], vec(V_BLR), 0.5, None, ALU.mult).then_inc(half_ready, 1)
                for n, u, i in pipeline(dve, PAIRS, STAGES):
                    v, m = 1 - u, n - 1
                    front, back = live(n, 0, PAIRS), live(n, 1, PAIRS)
                    if back:
                        wait(dve, done["x2"], m + 1)
                        wait(dve, done["V"], m + 1)
                        dve.tensor_tensor(e[:, :], x2[:, :], bk_v[:, :], ALU.subtract).then_inc(done["e"], 1)
                        wait(dve, done["t1"], m + 1)
                        dve.tensor_scalar(u1[:, :], t1[:, v, :], 1.0, None, ALU.subtract).then_inc(done["u1"], 1)
                        wait(dve, done["e"], m + 1)
                        dve.scalar_tensor_tensor(g[:, :], tlr[:, v, :], 1.0, e[:, :], ALU.add, ALU.mult).then_inc(done["g"], 1)
                        wait(dve, done["u1"], m + 1)
                        dve.scalar_tensor_tensor(w1[:, :], s1[:, v, :], 1.0, u1[:, :], ALU.subtract, ALU.mult).then_inc(done["w1"], 1)
                        wait(dve, done["w1"], m + 1)
                        wait(dve, done["Tdz1"], m)
                        dve.scalar_tensor_tensor(dz1[:, :], w1[:, :], 2.0, g[:, :], ALU.subtract, ALU.mult,
                                                 accum_out=gbs[:, 1, bass.ds(m, 1)]).then_inc(done["dz1"], 1)
                    if front:
                        wait(dve, done["s0"], n + 1)
                        wait(dve, done["Tx1"], n - 1)
                        dve.tensor_tensor(x1[:, u, :], k[:, u, :], s0[:, u, :], ALU.add).then_inc(done["x1"], 1)
                        wait(dve, done["t0"], n + 1)
                        dve.tensor_scalar(u0[:, :], t0[:, :], 1.0, None, ALU.subtract).then_inc(done["u0"], 1)
                        wait(dve, done["u0"], n + 1)
                        dve.scalar_tensor_tensor(w0[:, u, :], s0[:, u, :], 1.0, u0[:, :], ALU.subtract, ALU.mult).then_inc(done["w0"], 1)
                    if back:
                        wait(dve, done["B"], m + 1)
                        dve.scalar_tensor_tensor(dx1[:, :], bk_b[:, :], -0.5, g[:, :], ALU.mult, ALU.add).then_inc(done["dx1"], 1)
                        wait(dve, done["dx1"], m + 1)
                        wait(dve, done["Tdz0"], m)
                        dve.scalar_tensor_tensor(dz0[:, :], w0[:, v, :], 2.0, dx1[:, :], ALU.subtract, ALU.mult,
                                                 accum_out=gbs[:, 0, bass.ds(m, 1)]).then_inc(done["dz0"], 1)
                        wait(dve, done["grads"], m)
                        wait(dve, done["Tdz1"], m + 1)
                        dve.tensor_copy(dz1T[:, :], bk_t2[:, :]).then_inc(done["dz1T"], 1)

        gd = sb("gd", [P, 2, D])
        gb = sb("gb", [P, 2])
        grad = sb("grad", [P, 2 * D + 2])
        size = sb("size", [P, 2 * D + 2])
        param = sb("param", [P, 2 * D + 2])
        folded, gathered_g, chain = sem("folded"), sem("gathered_g"), sem("chain")
        with nc.Block() as block:
            @block.vector
            def _(dve):
                count = [0]

                def then(ins):
                    count[0] += 1
                    ins.then_inc(chain, 1)
                    dve.wait_ge(chain, count[0])

                dve.tensor_reduce(gb[:, :], gbs[:, :, :], AX_X, ALU.add).then_inc(gathered_g, 1)
                dve.memset(NW[:, :, :], 0.0).then_inc(gathered_g, 1)
                dve.tensor_copy(param[:, 2 * D:], W[:, V_B0:V_B1 + 1])
                for layer in range(2):
                    for a in range(2):
                        half = slice(a * D, (a + 1) * D)
                        dve.tensor_copy(gd[half, layer, :], bk_grad[half, layer * P + a * D:layer * P + (a + 1) * D]).then_inc(gathered_g, 1)
                then(dve.tensor_copy(param[:, 0:2 * D], W[:, W_01:W_01 + 2 * D]))
                dve.wait_ge(folded, 2)
                then(dve.tensor_scalar(grad[:, :], bk_v[:, 0:2 * D + 2], -0.5 * 2.0 / D * MAX_ALR * 0.5, None, ALU.mult))
                then(dve.scalar_tensor_tensor(size[:, :], grad[:, :], -1.0, grad[:, :], ALU.mult, ALU.max))
                then(dve.tensor_scalar(size[:, :], size[:, :], EPS_ADAM, None, ALU.add))
                then(dve.reciprocal(size[:, :], size[:, :]))
                then(dve.scalar_tensor_tensor(grad[:, :], grad[:, :], -LR, size[:, :], ALU.mult, ALU.mult))
                then(dve.scalar_tensor_tensor(param[:, :], param[:, :], 1.0 - LR * WD, grad[:, :], ALU.mult, ALU.add))
                for layer in range(2):
                    for a in range(2):
                        half = slice(a * D, (a + 1) * D)
                        then(dve.tensor_copy(NW[half, layer, a * D:(a + 1) * D], param[half, layer * D:(layer + 1) * D]))
                then(dve.tensor_copy(NB[:, :], param[:, 2 * D:]))

            @block.tensor
            def _(pe):
                pe.wait_ge(gathered_g, 6)
                pe.matmul(bk_v[:, 0:2 * D], fold, gd[:, :, :].rearrange("p l d -> p (l d)"), start=True, stop=True).then_inc(folded, 1)
                pe.matmul(bk_v[:, 2 * D:2 * D + 2], fold, gb[:, :], start=False, stop=True, skip_group_check=True).then_inc(folded, 1)
    return NW, NB


def retrieve(nc, ctx, sem, banks, XN, H, W, wcols, NW, NB):
    q, s0, x1, s1 = (ctx.enter_context(nc.sbuf_tensor(f"r_{n}", [P, 2, SEQ], F32)) for n in ("q", "s0", "x1", "s1"))
    done = {n: sem(f"read_{n}") for n in ("Q", "q", "Z0", "s0", "x1", "Z1", "s1", "x2", "h")}
    STAGES = 3
    with nc.Block() as block:
        @block.tensor
        def _(pe):
            for n, u, i in pipeline(pe, PAIRS, STAGES):
                if live(n, 0, PAIRS):
                    wait(pe, done["q"], n - 1)
                    pe.matmul(banks[u][:, :], wcols(W_Q), tile_of(XN, n), start=True, stop=True).then_inc(done["Q"], 1)
                if live(n, 1, PAIRS):
                    wait(pe, done["q"], n)
                    wait(pe, done["s0"], n - 2)
                    pe.matmul(banks[3 - u][:, :], NW[:, 0, :], q[:, 1 - u, :], start=True, stop=True).then_inc(done["Z0"], 1)
                if live(n, 2, PAIRS):
                    wait(pe, done["x1"], n - 1)
                    wait(pe, done["s1"], n - 3)
                    pe.matmul(banks[4 + u][:, :], NW[:, 1, :], x1[:, u, :], start=True, stop=True).then_inc(done["Z1"], 1)

        @block.scalar
        def _(act):
            for n, u, i in pipeline(act, PAIRS, STAGES):
                if live(n, 0, PAIRS):
                    wait(act, done["Q"], n + 1)
                    wait(act, done["x1"], n - 1)
                    act.activation(q[:, u, :], banks[u][:, :], ACT.Identity).then_inc(done["q"], 1)
                if live(n, 1, PAIRS):
                    wait(act, done["Z0"], n)
                    wait(act, done["x1"], n - 2)
                    act.activation(s0[:, 1 - u, :], banks[3 - u][:, :], ACT.Silu, bias=NB[:, 0:1]).then_inc(done["s0"], 1)
                if live(n, 2, PAIRS):
                    wait(act, done["Z1"], n - 1)
                    wait(act, done["h"], n - 3)
                    act.activation(s1[:, u, :], banks[4 + u][:, :], ACT.Silu, bias=NB[:, 1:2]).then_inc(done["s1"], 1)

        @block.vector
        def _(dve):
            for n, u, i in pipeline(dve, PAIRS, STAGES):
                if live(n, 1, PAIRS):
                    wait(dve, done["s0"], n)
                    wait(dve, done["x2"], n - 2)
                    wait(dve, done["Z1"], n - 2)
                    dve.tensor_tensor(x1[:, 1 - u, :], q[:, 1 - u, :], s0[:, 1 - u, :], ALU.add).then_inc(done["x1"], 1)
                if live(n, 2, PAIRS):
                    wait(dve, done["s1"], n - 1)
                    dve.tensor_tensor(s1[:, u, :], x1[:, u, :], s1[:, u, :], ALU.add).then_inc(done["x2"], 1)
                    wait(dve, done["x2"], n - 1)
                    dve.tensor_tensor(tile_of(H, n - 2), tile_of(H, n - 2), s1[:, u, :], ALU.add).then_inc(done["h"], 1)


KEY_ROWS, KEY_RING = 6 * HD + 3, 4
PART_STORES = 2
AV_AT = [7, 11, 13, 14]
A_Y, A_RD = 4, 7
D_DEN, D_XN = 5, 4
P_WO = 2
POOL_ORDER = ["V", "split", 0, "H", 1, "yn", 2, 3]


def project(nc, sem, banks, H, XN, W, VT, q_parts, k_parts, parts_stored, turn, causal, K, V, mask, eye, ident, centre, mean, eps_ln, eps_rms, vec):
    KR = 2 * KV * HD
    with ExitStack() as ctx:
        def sb(name, shape, dt=F32):
            return ctx.enter_context(nc.sbuf_tensor(name, shape, dt))

        TURN = sb("TURN", [P, 4, SEQ])
        sq, sq2, hn = (sb(f"j_{n}", [P, 2, SEQ]) for n in ("sq", "sq2", "hn"))
        lnv, r, lnv2, r2 = (sb(f"j_{n}", [P, SEQ]) for n in ("ln", "r", "ln2", "r2"))
        rows = {"q": P, "k": KR}
        cosd = {x: sb(f"j_{x}cos", [rows[x], SEQ]) for x in "qk"}
        sind = {x: sb(f"j_{x}sin", [rows[x], SEQ]) for x in "qk"}
        full = {x: sb(f"j_{x}", [rows[x], 2, SEQ]) for x in "qk"}
        rest = {x: sb(f"j_{x}rest", [rows[x], SEQ]) for x in "qk"}
        part = {x: sb(f"j_{x}part", [rows[x], 2, 3, SEQ], BF16) for x in "qk"}
        names = ["turn", "causal", "setup", "ln1w", "c", "sq", "v", "ln", "r", "xn", "sq2", "v2", "ln2", "r2", "hn", "V", "VT", "qP", "qR", "kPR"]
        names += [f"{x}{n}" for x in "qk" for n in ("cos", "sin", "full", "hi", "rest", "mid", "lo")]
        done = {n: sem(f"proj_{n}") for n in names}
        causal32 = sb("causal32", [P, P])
        bk_c, bk_v, bk_v2, bk_vt, bk_q, bk_qr, bk_k = banks[0:2], banks[2], banks[3], banks[4], banks[5], banks[6], banks[7]
        terms = {"q": ((bk_q[:, :], "qP", TURN[:, 0, :]), (bk_qr[:, :], "qR", TURN[:, 1, :])),
                 "k": ((bk_k[0:KR, :], "kPR", TURN[0:KR, 2, :]), (bk_k[KR:2 * KR, :], "kPR", TURN[KR:2 * KR, 3, :]))}
        parts = {"q": q_parts, "k": k_parts}
        STAGES = 5

        with nc.Block() as block:
            @block.sync
            def _(sp):
                sp.dma_start(TURN[:, :, :], turn).then_inc(done["turn"], 16)
                sp.dma_start(causal32[:, :], causal).then_inc(done["causal"], 16)
                for n, u, i in pipeline(sp, PAIRS, STAGES):
                    if live(n, 4, PAIRS):
                        m = n - 4
                        for x in "qk":
                            to = parts[x]
                            wait(sp, done[f"{x}lo"], m + 1)
                            sp.dma_start(to[bass.ds(m, 1)].rearrange("o t a d h s -> (o a d h) t s"),
                                         part[x][:, u]).then_inc(parts_stored[u], 16)

            @block.tensor
            def _(pe):
                pe.wait_ge(done["ln1w"], 2)
                for n, u, i in pipeline(pe, PAIRS, STAGES):
                    if live(n, 0, PAIRS):
                        wait(pe, done["xn"], n - 1)
                        pe.matmul(bk_c[u][:, :], centre, tile_of(H, n), start=True, stop=True).then_inc(done["c"], 1)
                    if live(n, 1, PAIRS):
                        m = n - 1
                        wait(pe, done["sq"], m + 1)
                        wait(pe, done["ln"], m)
                        pe.matmul(bk_v[:, :], mean, sq[:, 1 - u, :], start=True, stop=True).then_inc(done["v"], 1)
                    if live(n, 3, PAIRS):
                        m, v = n - 3, 1 - u
                        wait(pe, done["hn"], m + 1)
                        wait(pe, done["qcos"], m)
                        pe.matmul(bk_q[:, :], W[:, W_FQ:W_FQ + P], hn[:, v, :], start=True, stop=True).then_inc(done["qP"], 1)
                        wait(pe, done["qsin"], m)
                        pe.matmul(bk_qr[:, :], W[:, W_FQR:W_FQR + P], hn[:, v, :], start=True, stop=True).then_inc(done["qR"], 1)
                        wait(pe, done["ksin"], m)
                        pe.matmul(bk_k[:, :], W[:, W_FK:W_FK + 2 * KR], hn[:, v, :], start=True, stop=True).then_inc(done["kPR"], 1)
                    if live(n, 2, PAIRS):
                        m = n - 2
                        wait(pe, done["sq2"], m + 1)
                        wait(pe, done["ln2"], m)
                        pe.matmul(bk_v2[:, :], mean, sq2[:, u, :], start=True, stop=True).then_inc(done["v2"], 1)
                    if live(n, 3, PAIRS):
                        m, v = n - 3, 1 - u
                        wait(pe, done["VT"], m)
                        for q in range(BLK):
                            mm = pe.matmul(bk_vt[:, q * KR:(q + 1) * KR], hn[:, v, q * P:(q + 1) * P], W[:, W_FV:W_FV + KR],
                                           start=q == 0, stop=False, skip_group_check=True)
                        mm.then_inc(done["V"], 1)

            @block.scalar
            def _(act):
                act.preload_act_table_set("natural_log_exp_and_others")

                def run(name, to, source, func, **more):
                    act.activation(to, source, func, **more).then_inc(done[name], 1)

                for n, u, i in pipeline(act, PAIRS, STAGES):
                    if live(n, 2, PAIRS):
                        m = n - 2
                        wait(act, done["xn"], m + 1)
                        wait(act, done["v2"], m - 1)
                        run("sq2", sq2[:, u, :], tile_of(XN, m), ACT.Square)
                    if live(n, 0, PAIRS):
                        wait(act, done["c"], n + 1)
                        wait(act, done["v"], n - 1)
                        run("sq", sq[:, u, :], bk_c[u][:, :], ACT.Square)
                    if live(n, 4, PAIRS):
                        m = n - 4
                        for x in "qk":
                            wait(act, done[f"{x}full"], m + 1)
                            if live(n, 6, PAIRS):
                                wait(act, parts_stored[u], turns(i, u, 6) * PART_STORES * 16)
                            run(f"{x}hi", part[x][:, u, 0, :], full[x][:, u, :], ACT.Identity)
                    if live(n, 1, PAIRS):
                        m = n - 1
                        wait(act, done["v"], m + 1)
                        run("ln", lnv[:, :], bk_v[:, :], ACT.Ln, bias=eps_ln)
                        wait(act, done["ln"], m + 1)
                        wait(act, done["xn"], m)
                        run("r", r[:, :], lnv[:, :], ACT.Exp, scale=-0.5)
                    if live(n, 4, PAIRS):
                        m = n - 4
                        for x in "qk":
                            wait(act, done[f"{x}rest"], m + 1)
                            run(f"{x}mid", part[x][:, u, 1, :], rest[x][:, :], ACT.Identity)
                    if live(n, 2, PAIRS):
                        m = n - 2
                        wait(act, done["v2"], m + 1)
                        run("ln2", lnv2[:, :], bk_v2[:, :], ACT.Ln, bias=eps_rms)
                        wait(act, done["ln2"], m + 1)
                        wait(act, done["hn"], m)
                        run("r2", r2[:, :], lnv2[:, :], ACT.Exp, scale=-0.5)
                    if live(n, 3, PAIRS):
                        m = n - 3
                        wait(act, done["V"], m + 1)
                        run("VT", tile_of(VT, m), bk_vt[:, 0:BLK * KR], ACT.Identity)

            @block.gpsimd
            def _(pool):
                pool.memset(V[:, :, :, :, :], 0.0).then_inc(done["setup"], 1)
                pool.wait_ge(done["setup"], 1)
                pool.memset(K[KEY_ROWS - 3:KEY_ROWS, :, :, :], 1.0).then_inc(done["setup"], 1)
                pool.wait_ge(done["setup"], 2)
                pool.memset(V[:, :, :, :, HD:HD + 1], 1.0).then_inc(done["setup"], 1)
                pool.tensor_copy(eye[:, :], ident).then_inc(done["setup"], 1)
                pool.wait_ge(done["causal"], 16)
                pool.tensor_copy(mask[:, :], causal32[:, :]).then_inc(done["setup"], 1)
                for n, u, i in pipeline(pool, PAIRS, STAGES):
                    if live(n, 3, PAIRS):
                        m, v = n - 3, 1 - u
                        for x in "qk":
                            wait(pool, done[f"{x}sin"], m + 1)
                            wait(pool, done[f"{x}cos"], m + 1)
                            wait(pool, done[f"{x}rest"], m - 1)
                            pool.tensor_tensor(full[x][:, v, :], cosd[x][:, :], sind[x][:, :], ALU.add).then_inc(done[f"{x}full"], 1)

            @block.vector
            def _(dve):
                dve.tensor_scalar(W[:, W_FQ:W_01], W[:, W_FQ:W_01], vec(V_LN1), None, ALU.mult).then_inc(done["ln1w"], 1)
                dve.tensor_scalar(W[:, W_FK:W_O], W[:, W_FK:W_O], vec(V_LN1), None, ALU.mult).then_inc(done["ln1w"], 1)
                dve.wait_ge(done["turn"], 16)
                for n, u, i in pipeline(dve, PAIRS, STAGES):
                    if live(n, 4, PAIRS):
                        m = n - 4
                        for x in "qk":
                            wait(dve, done[f"{x}lo"], m)
                            wait(dve, done[f"{x}hi"], m + 1)
                            dve.tensor_tensor(rest[x][:, :], full[x][:, u, :], part[x][:, u, 0, :], ALU.subtract).then_inc(done[f"{x}rest"], 1)
                    if live(n, 1, PAIRS):
                        m = n - 1
                        wait(dve, done["r"], m + 1)
                        dve.tensor_tensor(tile_of(XN, m), bk_c[1 - u][:, :], r[:, :], ALU.mult).then_inc(done["xn"], 1)
                    if live(n, 3, PAIRS):
                        m = n - 3
                        for x in "qk":
                            wait(dve, done[f"{x}full"], m)
                            for (source, name, table), term, to in zip(terms[x], ("cos", "sin"), (cosd, sind)):
                                wait(dve, done[name], m + 1)
                                dve.tensor_tensor(to[x][:, :], source, table, ALU.mult).then_inc(done[f"{x}{term}"], 1)
                    if live(n, 4, PAIRS):
                        m = n - 4
                        for x in "qk":
                            wait(dve, done[f"{x}mid"], m + 1)
                            dve.tensor_tensor(part[x][:, u, 2, :], rest[x][:, :], part[x][:, u, 1, :], ALU.subtract).then_inc(done[f"{x}lo"], 1)
                    if live(n, 2, PAIRS):
                        m = n - 2
                        wait(dve, done["r2"], m + 1)
                        wait(dve, done["V"], m - 1)
                        dve.tensor_tensor(hn[:, u, :], tile_of(XN, m), r2[:, :], ALU.mult).then_inc(done["hn"], 1)


def score_units(order):
    units = []
    for b in order:
        w = SEQ - P * b
        heads = min(HEADS, SEQ // w)
        units += [(b, h, heads, w) for h in range(0, HEADS, heads)]
    return units


def attend(nc, sem, banks, H, XN, W, VT, q_parts, k_parts, parts_stored, K, V, mask, eye, ident):
    RING = KEY_RING
    UNITS = score_units(range(BLK))
    NU = len(UNITS)
    SROWS = 6 * HD
    STAGES = 6
    with ExitStack() as ctx:
        def sb(name, shape, dt=F32):
            return ctx.enter_context(nc.sbuf_tensor(name, shape, dt))

        Q = sb("t_q", [KEY_ROWS, RING, HEADS, SEQ], BF16)
        negmax = sb("negmax", [P, 2, HEADS * BLK])
        nm = sb("nm", [HEADS * BLK, 2, 3, P], BF16)
        nraw = sb("nraw", [HEADS * BLK, P])
        nrest = sb("nrest", [HEADS * BLK, P])
        E = sb("t_e", [P, HEADS * TRAP])
        Y = sb("t_y", [P, SEQ])
        den = sb("den", [P, SEQ])
        lnd = sb("lnd", [P, SEQ])
        rd = sb("rd", [P, SEQ])
        yn = sb("yn", [P, 2, SEQ])
        names = ("sp_seen", "pool_seen", "dve_seen", "S", "max", "turned", "nraw", "nhi", "nrest", "nmid", "nlo", "T", "exp", "masked", "V",
                 "av", "Y", "den", "lnd", "rd", "yn", "wo", "xn", "h")
        done = {n: sem(f"att_{n}") for n in names}
        q_loaded = [sem(f"q_loaded{u}") for u in range(RING)]
        nm_loaded = [sem(f"nm_loaded{u}") for u in range(RING)]
        bk_s, bk_t, bk_av, bk_o = banks[0:3], banks[3:6], banks[6], banks[7]
        NS, NT = len(bk_s), len(bk_t)
        SLOTS = [(0, 0, 3), (1, 3, 2), (2, 5, 1)]
        LOADS = 2 * len(SLOTS)

        def e_block(b):
            return E[:, HEADS * START[b]:HEADS * (START[b] + WIDTH[b])].rearrange("p (h w) -> p h w", h=HEADS)

        with nc.Block() as block:
            @block.sync
            def _(sp):
                for n, u, i in pipeline(sp, ROWS, STAGES, RING):
                    if live(n, 0, ROWS):
                        pair, a = RING // 2 * i + u // 2, u % 2
                        sp.wait_ge(parts_stored[u // 2], (i + 1) * PART_STORES * 16)
                        sp.sem_inc(done["sp_seen"], 1)
                        wait(sp, done["T"], (n - RING + 1) * NU)
                        for j, slot, k in SLOTS:
                            there = slice(slot * HD, (slot + k) * HD)
                            sp.dma_start(Q[there, u].rearrange("p h s -> p (h s)"),
                                         q_parts[bass.ds(pair, 1), 0:k, a].rearrange("o t d h s -> (o t) d (h s)")).then_inc(q_loaded[u], 16)
                            sp.dma_start(K[there, u].rearrange("p h s -> p (h s)"),
                                         k_parts[bass.ds(pair, 1), j:j + 1, a].rearrange("o t d h s -> (o t) d (h s)").to_broadcast([k, HD, KV * SEQ])).then_inc(q_loaded[u], 16)
                    if live(n, 2, ROWS):
                        m, g = n - 2, (u - 2) % RING
                        wait(sp, done["nlo"], m + 1)
                        for part in range(3):
                            sp.dma_start(Q[SROWS + part:SROWS + part + 1, g].rearrange("o h s -> o (h s)"),
                                         nm[:, u % 2, part, :]).then_inc(nm_loaded[g], 16)

            @block.gpsimd
            def _(pool):
                def select(n, u, c):
                    m = n - 3
                    wait(pool, done["exp"], m * NU + sum(b <= c for b, *_ in UNITS))
                    pool.sem_inc(done["pool_seen"], 1)
                    pool.affine_select(e_block(c)[:, :, 0:P], e_block(c)[:, :, 0:P], [[0, HEADS], [1, P]],
                                       ALU.is_ge, 0.0, base=0, channel_multiplier=-1).then_inc(done["masked"], 1)

                def values(n, u, i):
                    m, a = n - 3, (u - 3) % 2
                    pair = RING // 2 * i + (u - 3) // 2
                    wait(pool, done["av"], (m - 1) * BLK)
                    pool.sem_inc(done["pool_seen"], 1)
                    src = tile_of(VT, pair).rearrange("p (q a k d) -> p q a k d", q=BLK, a=2, k=KV)[:, :, a]
                    pool.tensor_copy(V[:, a, :, :, 0:HD], src).then_inc(done["V"], 1)

                def split(n, u, i):
                    m = n - 2
                    wait(pool, done["nraw"], m + 1)
                    if live(n, 4, ROWS):
                        g = (u - 4) % RING
                        pool.wait_ge(nm_loaded[g], turns(i, u, 4, RING) * 48)
                    pool.sem_inc(done["pool_seen"], 1)
                    pool.tensor_copy(nm[:, u % 2, 0, :], nraw[:, :]).then_inc(done["nhi"], 1)
                    wait(pool, done["nhi"], m + 1)
                    pool.tensor_tensor(nrest[:, :], nraw[:, :], nm[:, u % 2, 0, :], ALU.subtract).then_inc(done["nrest"], 1)
                    wait(pool, done["nrest"], m + 1)
                    pool.sem_inc(done["pool_seen"], 1)
                    pool.tensor_copy(nm[:, u % 2, 1, :], nrest[:, :]).then_inc(done["nmid"], 1)
                    wait(pool, done["nmid"], m + 1)
                    pool.tensor_tensor(nm[:, u % 2, 2, :], nrest[:, :], nm[:, u % 2, 1, :], ALU.subtract).then_inc(done["nlo"], 1)

                def residual(n, u, i):
                    pair = RING // 2 * i + (u - 5) // 2
                    wait(pool, done["xn"], pair + 1)
                    pool.tensor_tensor(tile_of(H, pair), tile_of(H, pair), tile_of(XN, pair), ALU.add).then_inc(done["h"], 1)

                def normalise(n, u, i):
                    m, a = n - 4, u % 2
                    wait(pool, done["rd"], m + 1)
                    wait(pool, done["wo"], (m - a) // 2 if isinstance(m, int) else RING // 2 * i + (u - 4 - a) // 2)
                    pool.tensor_tensor(yn[:, a, :], Y[:, :], rd[:, :], ALU.mult).then_inc(done["yn"], 1)

                for n, u, i in pipeline(pool, ROWS, STAGES, RING):
                    for what in POOL_ORDER:
                        if what == "V" and live(n, 3, ROWS):
                            values(n, u, i)
                        if what == "split" and live(n, 2, ROWS):
                            split(n, u, i)
                        if what == "H" and live(n, 5, ROWS) and u % 2 == 0:
                            residual(n, u, i)
                        if what == "yn" and live(n, 4, ROWS):
                            normalise(n, u, i)
                        if isinstance(what, int) and live(n, 3, ROWS):
                            select(n, u, what)
                        if isinstance(what, tuple) and live(n, 4, ROWS):
                            select(n - 1, u, what[0])

            @block.vector
            def _(dve):
                for n, u, i in pipeline(dve, ROWS, STAGES, RING):
                    if live(n, 2, ROWS):
                        m = n - 2
                        wait(dve, done["turned"], m + 1)
                        wait(dve, done["nrest"], m)
                        dve.tensor_copy(nraw[:, :], bk_o[0:HEADS * BLK, 0:P]).then_inc(done["nraw"], 1)
                    for t, (c, h, heads, w) in enumerate(UNITS):
                        if live(n, 1, ROWS):
                            m = n - 1
                            wait(dve, done["S"], m * NU + t + 1)
                            if t == 0:
                                wait(dve, done["turned"], m - 1)
                            j = BLK - 1 - c
                            to = negmax[:, (u - 1) % 2, :].rearrange("p (h j) -> p h j", j=BLK)[:, h:h + heads, j]
                            dve.tensor_reduce(to, bk_s[t % NS][:, 0:heads * w].rearrange("p (h s) -> p h s", h=heads),
                                              AX_X, ALU.max, negate=True).then_inc(done["max"], 1)
                        if t == D_DEN and live(n, 4, ROWS):
                            m = n - 4
                            wait(dve, done["lnd"], m)
                            wait(dve, done["Y"], m + 1)
                            dve.sem_inc(done["dve_seen"], 1)
                            dve.stream_shuffle(den[:, :], Y[:, :], [HD] * 32).then_inc(done["den"], 1)
                        if t == D_XN and live(n, 5, ROWS) and u % 2 == 0:
                            pair = RING // 2 * i + (u - 5) // 2
                            wait(dve, done["wo"], pair + 1)
                            dve.tensor_tensor(tile_of(XN, pair), tile_of(XN, pair), bk_o[:, :], ALU.add).then_inc(done["xn"], 1)

            @block.tensor
            def _(pe):
                def last_turn(t, ring):
                    return (NU - 1 - t) % ring

                def s_unit(m, g, t):
                    c, h, heads, w = UNITS[t]
                    j = BLK - 1 - c
                    wait(pe, done["max"], m * NU + t - NS + 1 if t >= NS else m * NU - last_turn(t, NS))
                    for x in range(heads):
                        pe.matmul(bk_s[t % NS][:, x * w:(x + 1) * w], Q[0:SROWS, g, h + x, j * P:(j + 1) * P],
                                  K[0:SROWS, g, (h + x) // KV, 0:w], start=x == 0, stop=False, skip_group_check=True)
                    for x in range(heads):
                        mm = pe.matmul(bk_s[t % NS][:, (x + 1) * w - P:(x + 1) * w], mask[:, :], eye[:, :],
                                       start=False, stop=False, skip_group_check=True)
                    mm.then_inc(done["S"], 1)

                def t_unit(m, g, t):
                    c, h, heads, w = UNITS[t]
                    wait(pe, done["exp"], m * NU + t - NT + 1 if t >= NT else m * NU - last_turn(t, NT))
                    for x in range(heads):
                        mm = pe.matmul(bk_t[t % NT][:, x * w:(x + 1) * w], K[:, g, (h + x) // KV, c * P:(c + 1) * P],
                                       Q[:, g, h + x, c * P:], start=x == 0, stop=False, skip_group_check=True)
                    mm.then_inc(done["T"], 1)

                def values(m, a, c):
                    wait(pe, done["masked"], m * BLK + c + 1)
                    if c == 0:
                        wait(pe, done["V"], m + 1)
                        wait(pe, done["Y"], m)
                    for h in range(HEADS):
                        mm = pe.matmul(bk_av[32 * h:32 * h + 32, c * P:], V[:, a, c, h // KV, :], e_block(c)[:, h],
                                       start=c == 0, stop=False, skip_group_check=True)
                    mm.then_inc(done["av"], 1)

                for n, u, i in pipeline(pe, ROWS, STAGES, RING):
                    s_live, t_live, f_live = live(n, 1, ROWS), live(n, 3, ROWS), live(n, 4, ROWS)
                    if s_live:
                        g = (u - 1) % RING
                        pe.wait_ge(q_loaded[g], turns(i, u, 1, RING) * LOADS * 16)
                    if t_live:
                        g = (u - 3) % RING
                        pe.wait_ge(nm_loaded[g], turns(i, u, 3, RING) * 48)
                    for t in range(NU):
                        if s_live:
                            s_unit(n - 1, (u - 1) % RING, t)
                        if t_live:
                            t_unit(n - 3, (u - 3) % RING, t)
                        if t == 0 and live(n, 2, ROWS):
                            m = n - 2
                            wait(pe, done["max"], (m + 1) * NU)
                            wait(pe, done["xn"], (n - 5) // 2 if isinstance(n, int) else RING // 2 * i + (u - 5) // 2)
                            wait(pe, done["nraw"], m)
                            pe.transpose(bk_o[0:HEADS * BLK, 0:P], negmax[:, u % 2, :], ident).then_inc(done["turned"], 1)
                        if f_live:
                            m, a = n - 4, u % 2
                            for c in range(BLK):
                                if AV_AT[c] == t + NU:
                                    values(m, a, c)
                        if t == P_WO and live(n, 5, ROWS) and u % 2 == 0:
                            pair = RING // 2 * i + (u - 5) // 2
                            wait(pe, done["yn"], n - 5 + 1)
                            wait(pe, done["nraw"], min(n - 1, ROWS) if isinstance(n, int) else n - 1)
                            for a in range(2):
                                mm = pe.matmul(bk_o[a * D:(a + 1) * D, :], W[:, W_O:W_O + D], yn[:, a, :],
                                               start=True, stop=False, skip_group_check=True)
                            mm.then_inc(done["wo"], 1)
                        if t_live:
                            m, a = n - 3, (u - 3) % 2
                            for c in range(BLK):
                                if AV_AT[c] == t:
                                    values(m, a, c)

            @block.scalar
            def _(act):
                def run(name, to, source, func, **more):
                    act.activation(to, source, func, **more).then_inc(done[name], 1)

                for n, u, i in pipeline(act, ROWS, STAGES, RING):
                    for t, (c, h, heads, w) in enumerate(UNITS):
                        if live(n, 3, ROWS):
                            m = n - 3
                            wait(act, done["T"], m * NU + t + 1)
                            wait(act, done["av"], (m - 1) * BLK + c + 1)
                            at = HEADS * START[c] + h * w
                            run("exp", E[:, at:at + heads * w], bk_t[t % NT][:, 0:heads * w], ACT.Exp)
                        if live(n, 4, ROWS):
                            m = n - 4
                            if t == A_Y:
                                wait(act, done["av"], (m + 1) * BLK)
                                wait(act, done["yn"], m)
                                run("Y", Y[:, :], bk_av[:, :], ACT.Identity)
                            if t == A_RD:
                                wait(act, done["den"], m + 1)
                                wait(act, done["rd"], m)
                                run("lnd", lnd[:, :], den[:, :], ACT.Ln)
                                wait(act, done["lnd"], m + 1)
                                wait(act, done["yn"], m)
                                run("rd", rd[:, :], lnd[:, :], ACT.Exp, scale=-1.0)


X_SCALE, W_SCALE = 256.0, 64.0


def route(nc, sem, banks, XN, W, CST, FS, gates, w13, w2, whi, wlo, v2hi, v2lo, ident, mean, eps_rms, vec):
    TOKENS = PAIRS * BLK * 2
    with ExitStack() as ctx:
        def sb(name, shape, dt=F32):
            return ctx.enter_context(nc.sbuf_tensor(name, shape, dt))

        sq, lnv, r = (sb(f"g_{n}", [P, SEQ]) for n in ("sq", "ln", "r"))
        flat = sb("g_flat", [P, 2, SEQ])
        hi, lo = sb("g_hi", [P, 2, SEQ], F16), sb("g_lo", [P, 2, SEQ], F16)
        LG = sb("g_logits", [P, PAIRS, BLK * 2 * EXPERTS])
        done = {n: sem(f"route_{n}") for n in ("ln2w", "sq", "v", "ln", "r", "flat", "L", "logits", "hi", "lo")}
        stacked = [sem(f"stacked{u}") for u in range(2)]
        bk_v, bk_l = banks[0], banks[1]
        G8 = 2 * EXPERTS
        STAGES = 3

        with nc.Block() as block:
            @block.sync
            def _(sp):
                for n, u, i in pipeline(sp, PAIRS, STAGES):
                    if live(n, 2, PAIRS):
                        m = n - 2
                        wait(sp, done["hi"], m + 1)
                        wait(sp, done["lo"], m + 1)
                        for a in range(2):
                            for j, part in enumerate((hi, lo)):
                                sp.dma_start(FS[j * D:(j + 1) * D, bass.ds(2 * m + a, 1), :].rearrange("p a s -> p (a s)"),
                                             part[a * D:(a + 1) * D, u, :]).then_inc(stacked[u], 16)
                for u in range(2):
                    sp.wait_ge(stacked[u], PAIRS // 2 * 64)

            @block.tensor
            def _(pe):
                pe.wait_ge(done["ln2w"], 1)
                for n, u, i in pipeline(pe, PAIRS, STAGES):
                    if live(n, 0, PAIRS):
                        wait(pe, done["sq"], n + 1)
                        wait(pe, done["ln"], n)
                        pe.matmul(bk_v[:, :], mean, sq[:, :], start=True, stop=True).then_inc(done["v"], 1)
                    if live(n, 1, PAIRS):
                        m, v = n - 1, 1 - u
                        wait(pe, done["flat"], m + 1)
                        wait(pe, done["logits"], m)
                        for q in range(BLK):
                            mm = pe.matmul(bk_l[:, q * G8:(q + 1) * G8], flat[:, v, q * P:(q + 1) * P], W[:, W_ROUTE:W_ROUTE + G8],
                                           start=q == 0, stop=False, skip_group_check=True)
                        mm.then_inc(done["L"], 1)

            @block.scalar
            def _(act):
                def run(name, to, source, func, **more):
                    act.activation(to, source, func, **more).then_inc(done[name], 1)

                for n, u, i in pipeline(act, PAIRS, STAGES):
                    if live(n, 0, PAIRS):
                        wait(act, done["v"], n)
                        run("sq", sq[:, :], tile_of(XN, n), ACT.Square)
                    if live(n, 1, PAIRS):
                        m, v = n - 1, 1 - u
                        wait(act, done["flat"], m + 1)
                        if live(n, 3, PAIRS):
                            wait(act, stacked[v], turns(i, u, 3) * 64)
                        run("hi", hi[:, v, :], flat[:, v, :], ACT.Identity, scale=X_SCALE)
                        wait(act, done["L"], m + 1)
                        run("logits", tile_of(LG, m), bk_l[:, 0:BLK * G8], ACT.Identity)
                    if live(n, 0, PAIRS):
                        wait(act, done["v"], n + 1)
                        run("ln", lnv[:, :], bk_v[:, :], ACT.Ln, bias=eps_rms)
                        wait(act, done["ln"], n + 1)
                        wait(act, done["flat"], n)
                        run("r", r[:, :], lnv[:, :], ACT.Exp, scale=-0.5)

            @block.vector
            def _(dve):
                dve.tensor_scalar(W[:, W_ROUTE:W_ROUTE + G8], W[:, W_ROUTE:W_ROUTE + G8], vec(V_LN2), None, ALU.mult).then_inc(done["ln2w"], 1)
                for n, u, i in pipeline(dve, PAIRS, STAGES):
                    if live(n, 1, PAIRS):
                        m, v = n - 1, 1 - u
                        wait(dve, done["hi"], m + 1)
                        if live(n, 3, PAIRS):
                            wait(dve, stacked[v], turns(i, u, 3) * 64)
                        dve.scalar_tensor_tensor(lo[:, v, :], flat[:, v, :], X_SCALE, hi[:, v, :], ALU.mult, ALU.subtract).then_inc(done["lo"], 1)
                    if live(n, 0, PAIRS):
                        wait(dve, done["r"], n + 1)
                        wait(dve, done["L"], n - 1)
                        wait(dve, done["lo"], n - 1)
                        dve.tensor_tensor(flat[:, u, :], tile_of(XN, n), r[:, :], ALU.mult).then_inc(done["flat"], 1)

        prob, first, second, spare = (sb(f"g_{n}", [P, TOKENS, EXPERTS]) for n in ("prob", "first", "second", "spare"))
        most, total, top1, top2 = (sb(f"g_{n}", [P, TOKENS]) for n in ("most", "total", "top1", "top2"))
        gate = sb("g_gate", [P, PAIRS, 2, EXPERTS, BLK])
        gateT = sb("g_gateT", [P, 2, BLK, P])
        chain, less_ready, exp_ready, gate_ready = sem("chain_g"), sem("less_ready"), sem("exp_ready"), sem("gate_ready")
        gate_turned, gateT_ready, gates_stored = sem("gate_turned"), sem("gateT_ready"), sem("gates_stored")
        logits = LG[:, :, :].rearrange("p m (g e) -> p (m g) e", e=EXPERTS)

        def each(t):
            return t[:, :].unsqueeze(2).to_broadcast([P, TOKENS, EXPERTS])

        COLS = 2 * EXPERTS * HID
        raw = XN[:, :, :].rearrange("p m s -> p (m s)")
        w13raw, w2raw = raw[:, 0:COLS], raw[:, COLS:COLS + 2 * EXPERTS * D]
        v2hi_, v2lo_ = (v[:, :, :].rearrange("p j d -> p (j d)") for v in (v2hi, v2lo))
        w13_loaded, w2_loaded, scaled, high, low = (sem(n) for n in ("w13_loaded", "w2_loaded", "w_scaled", "w_high", "w_low"))

        with nc.Block() as block:
            @block.gpsimd
            def _(pool):
                pool.wait_ge(w13_loaded, 32)
                pool.tensor_scalar(w13raw, w13raw, vec(V_LN2), W_SCALE, ALU.mult, ALU.mult).then_inc(scaled, 1)
                pool.wait_ge(w2_loaded, 16)
                pool.tensor_scalar(w2raw, w2raw, W_SCALE, None, ALU.mult).then_inc(scaled, 1)
                pool.wait_ge(high, 1)
                pool.tensor_tensor(wlo[:, :], w13raw, whi[:, :], ALU.subtract).then_inc(low, 1)
                pool.wait_ge(high, 2)
                pool.tensor_tensor(v2lo_, w2raw, v2hi_, ALU.subtract).then_inc(low, 1)

            @block.vector
            def _(dve):
                count = [0]

                def then(ins):
                    count[0] += 1
                    ins.then_inc(chain, 1)
                    dve.wait_ge(chain, count[0])

                rank = CST[:, C_RANK:C_RANK + EXPERTS].unsqueeze(1).to_broadcast([P, TOKENS, EXPERTS])

                def pick(chosen, source, best):
                    then(dve.tensor_reduce(best[:, :], source[:, :, :], AX_X, ALU.max))
                    then(dve.tensor_tensor(chosen[:, :, :], source[:, :, :], each(best), ALU.is_equal))
                    then(dve.tensor_tensor(chosen[:, :, :], chosen[:, :, :], rank, ALU.mult))
                    then(dve.tensor_reduce(most[:, :], chosen[:, :, :], AX_X, ALU.max))
                    then(dve.tensor_tensor(chosen[:, :, :], chosen[:, :, :], each(most), ALU.is_equal))

                then(dve.tensor_reduce(most[:, :], logits, AX_X, ALU.max))
                dve.tensor_tensor(prob[:, :, :], logits, each(most), ALU.subtract).then_inc(less_ready, 1)
                dve.wait_ge(exp_ready, 1)
                then(dve.tensor_reduce(total[:, :], prob[:, :, :], AX_X, ALU.add))
                then(dve.reciprocal(total[:, :], total[:, :]))
                then(dve.tensor_tensor(prob[:, :, :], prob[:, :, :], each(total), ALU.mult))
                pick(first, prob, top1)
                then(dve.scalar_tensor_tensor(spare[:, :, :], first[:, :, :], -2.0, prob[:, :, :], ALU.mult, ALU.add))
                pick(second, spare, top2)
                then(dve.tensor_tensor(first[:, :, :], first[:, :, :], second[:, :, :], ALU.add))
                then(dve.tensor_tensor(first[:, :, :], first[:, :, :], prob[:, :, :], ALU.mult))
                then(dve.tensor_tensor(total[:, :], top1[:, :], top2[:, :], ALU.add))
                then(dve.tensor_scalar(total[:, :], total[:, :], 1e-9, None, ALU.add))
                then(dve.reciprocal(total[:, :], total[:, :]))
                for q in range(BLK):
                    chosen = first[:, :, :].rearrange("p (m q a) e -> p q m a e", q=BLK, a=2)[:, q]
                    by = each(total).rearrange("p (m q a) e -> p q m a e", q=BLK, a=2)[:, q]
                    for a in range(2):
                        dve.tensor_tensor(gate[:, :, a, :, q], chosen[:, :, a], by[:, :, a], ALU.mult).then_inc(gate_ready, 1)
                for half in range(2):
                    dve.wait_ge(gate_turned, (half + 1) * BLK)
                    dve.tensor_scalar(gateT[:, half].rearrange("p b t -> p (b t)"), banks[half][:, :],
                                      1.0 / (W_SCALE * HH_SCALE), None, ALU.mult).then_inc(gateT_ready, 1)

            @block.scalar
            def _(act):
                act.wait_ge(less_ready, 1)
                act.activation(prob[:, :, :], prob[:, :, :], ACT.Exp).then_inc(exp_ready, 1)
                act.wait_ge(scaled, 1)
                act.activation(whi[:, :], w13raw, ACT.Identity).then_inc(high, 1)
                act.wait_ge(scaled, 2)
                act.activation(v2hi_, w2raw, ACT.Identity).then_inc(high, 1)
                act.preload_act_table_set("silu_and_others")

            @block.tensor
            def _(pe):
                pe.wait_ge(gate_ready, 2 * BLK)
                cols = gate[:, :, :, :, :].rearrange("p m a e q -> p (m a e q)")
                for b in range(2 * BLK):
                    pe.transpose(banks[b // BLK][:, b % BLK * P:(b % BLK + 1) * P], cols[:, b * P:(b + 1) * P], ident).then_inc(gate_turned, 1)

            @block.sync
            def _(sp):
                for a in range(2):
                    sp.dma_start(w13raw[a * D:(a + 1) * D, :], w13.rearrange("d j h -> d (j h)")).then_inc(w13_loaded, 16)
                sp.dma_start(w2raw, w2.rearrange("p j d -> p (j d)")).then_inc(w2_loaded, 16)
                sp.wait_ge(gateT_ready, 2)
                flat_gates = gates.rearrange("m a e (q t) -> (m a e q) t", t=P)
                sp.dma_start(flat_gates.rearrange("(b r) t -> r b t", r=P), gateT[:, :, :, :].rearrange("p h b t -> p (h b) t")).then_inc(gates_stored, 16)
                sp.wait_ge(gates_stored, 16)


GROUPS = [(0, 3), (3, 3), (6, 2)]
CHUNKS = [[(c, min(P, k * HID - c)) for c in range(0, k * HID, P)] for _, k in GROUPS]
TILES = [2 * len(c) for c in CHUNKS]
TILE_AT = [sum(TILES[:x]) for x in range(len(GROUPS))]
PAIR_TILES = sum(TILES)
TILE_ROWS = [rows for c in CHUNKS for _, rows in c for a in range(2)]
EXPERTS_UPTO = [first + k for (first, k), tiles in zip(GROUPS, TILES) for t in range(tiles)]
BANK_BEFORE = [6, 7, 5, 0, 1, 2, 3, 4]
HH_SCALE = 4.0
MORE_POOL = ()
HI_LAG, LO_LAG = 1, 2
OUT_AT = [1, 3, 5]
GATE_AT = [3, 5, 7]
ACC_AT = [3, 5, 7]


def experts(nc, sem, banks, H, XN, FS, gates, whi, wlo, v2hi, v2lo, out, ident):
    RING = len(GROUPS)
    UNITS = PAIRS * RING
    DOWN = 1.0 / (X_SCALE * W_SCALE)
    SLOTS = PAIR_TILES // 2
    with ExitStack() as ctx:
        def sb(name, shape, dt=F32):
            return ctx.enter_context(nc.sbuf_tensor(name, shape, dt))

        gate = sb("x_gate", [P, EXPERTS, SEQ])
        s = sb("x_s", [P, 2, SEQ])
        hhi, hlo = sb("hhi", [P, PAIR_TILES, SEQ], F16), sb("hlo", [P, PAIR_TILES, SEQ], F16)
        part = sb("x_part", [P, 3, SEQ])
        acc = sb("x_acc", [P, SEQ])
        outsb = sb("outsb", [P, SEQ])
        names = ("H1", "H3", "s", "hh", "hi", "lo_d", "lo_p", "O", "part", "acc", "turned", "out")
        done = {n: sem(f"moe_{n}") for n in names}
        gate_loaded = [sem(f"gate_loaded{u}") for u in range(RING)]
        stored = sem("stored")
        bk_h1, bk_h3, bk_o, bk_t = banks[0:2], banks[2:4], banks[4:7], banks[7]
        out_v = out.rearrange("r (q p) f -> r p q f", p=P)
        by_pool = [t % 2 == 1 or t in MORE_POOL for t in range(PAIR_TILES)]
        engine_of = ["lo_p" if x else "lo_d" for x in by_pool]
        total = {n: engine_of.count(n) for n in ("lo_p", "lo_d")}

        def formed(name, pair, t):
            return pair * total[name] + engine_of[:t].count(name)

        STAGES = 3

        def unit(i, u, stage):
            return i + (u - stage) // RING, (u - stage) % RING

        def split_tile(pair, t):
            return (pair, t) if t >= 0 else (pair - 1, t + PAIR_TILES)

        def begun(pair, t):
            return not isinstance(pair, int) or pair * PAIR_TILES + t >= 0

        def low(eng, pair, t, name):
            if not begun(pair, t):
                return
            pair, t = split_tile(pair, t)
            if engine_of[t] != name:
                return
            rows = TILE_ROWS[t]
            wait(eng, done["hi"], pair * PAIR_TILES + t + 1)
            eng.tensor_tensor(hlo[0:rows, t, :], XN[0:rows, t % SLOTS, :], hhi[0:rows, t, :], ALU.subtract).then_inc(done[name], 1)

        with nc.Block() as block:
            @block.sync
            def _(sp):
                for n, u, i in pipeline(sp, UNITS, STAGES, RING, 2 * RING):
                    if live(n, 0, UNITS):
                        first, k = GROUPS[u]
                        wait(sp, done["part"], (i - 1) * EXPERTS + first + k)
                        for a in range(2):
                            src = gates[bass.ds(i, 1), a, first:first + k, :].rearrange("o e s -> (o e) s").partition_broadcast(D)
                            sp.dma_start(gate[a * D:(a + 1) * D, first:first + k], src).then_inc(gate_loaded[u], 16)
                    if live(n, 2, UNITS) and u == 1:
                        pair = i - 1
                        wait(sp, done["out"], pair + 1)
                        for a in range(2):
                            sp.dma_start(out_v[bass.ds(2 * pair + a, 1)].rearrange("o p q f -> (o p) q f"),
                                         outsb[:, :].rearrange("p (q a f) -> p q a f", q=BLK, a=2)[:, :, a]).then_inc(stored, 16)
                sp.wait_ge(stored, ROWS * 16)

            @block.tensor
            def _(pe):
                def hidden(i, u, t):
                    (at, rows), a = CHUNKS[u][t // 2], t % 2
                    k = i * PAIR_TILES + TILE_AT[u] + t
                    for bank, name, layer, reader in ((bk_h1, "H1", 0, "s"), (bk_h3, "H3", 1, "hh")):
                        wait(pe, done[reader], k - 1)
                        cols = slice((layer * EXPERTS + GROUPS[u][0]) * HID + at, (layer * EXPERTS + GROUPS[u][0]) * HID + at + rows)
                        x = tile_of(FS, 2 * i + a)
                        pe.matmul(bank[t % 2][0:rows, :], whi[:, cols], x, start=True, stop=False)
                        pe.matmul(bank[t % 2][0:rows, :], wlo[:, cols], x, start=False, stop=True).then_inc(done[name], 1)

                def output(pair, x, j):
                    last = TILE_AT[x] + 2 * (j + 2)
                    wait(pe, done["hi"], pair * PAIR_TILES + last)
                    wait(pe, done["lo_d"], formed("lo_d", pair, last))
                    wait(pe, done["lo_p"], formed("lo_p", pair, last))
                    e = GROUPS[x][0] + j
                    wait(pe, done["part"], (pair if x else pair - 1) * EXPERTS + (BANK_BEFORE[e] + 1))
                    for c in range(j, j + 2):
                        rows = CHUNKS[x][c][1]
                        for z, (w, h) in enumerate(((v2hi, hhi), (v2lo, hhi), (v2hi, hlo))):
                            for a in range(2):
                                mm = pe.matmul(bk_o[j][a * D:(a + 1) * D, :], w[0:rows, 2 * e + c - j, :],
                                               h[0:rows, TILE_AT[x] + 2 * c + a, :], start=c == j and z == 0,
                                               stop=c == j + 1 and z == 2, skip_group_check=True)
                    mm.then_inc(done["O"], 1)

                for n, u, i in pipeline(pe, UNITS, STAGES, RING, 2 * RING):
                    for t in range(max(TILES)):
                        if live(n, 0, UNITS) and t < TILES[u]:
                            hidden(i, u, t)
                        if live(n, 1, UNITS):
                            pair, x = unit(i, u, 1)
                            for j in range(GROUPS[x][1]):
                                if OUT_AT[j] == t:
                                    output(pair, x, j)
                        if live(n, 2, UNITS) and u == 1 and t == 3:
                            pair = i - 1
                            wait(pe, done["acc"], (pair + 1) * EXPERTS)
                            wait(pe, done["out"], pair)
                            for q in range(BLK):
                                mm = pe.transpose(bk_t[:, q * P:(q + 1) * P], acc[:, q * P:(q + 1) * P], ident)
                            mm.then_inc(done["turned"], 1)

            @block.scalar
            def _(act):
                def high(pair, t):
                    if not begun(pair, t):
                        return
                    pair, t = split_tile(pair, t)
                    rows = TILE_ROWS[t]
                    wait(act, done["hh"], pair * PAIR_TILES + t + 1)
                    wait(act, done["O"], (pair - 1) * EXPERTS + EXPERTS_UPTO[t])
                    act.activation(hhi[0:rows, t, :], XN[0:rows, t % SLOTS, :], ACT.Identity).then_inc(done["hi"], 1)

                for n, u, i in pipeline(act, UNITS, STAGES, RING, 2 * RING):
                    if live(n, 0, UNITS):
                        for t in range(TILES[u]):
                            at = TILE_AT[u] + t
                            wait(act, done["H1"], i * PAIR_TILES + at + 1)
                            wait(act, done["hh"], i * PAIR_TILES + at - 1)
                            rows = TILE_ROWS[at]
                            act.activation(s[0:rows, t % 2, :], bk_h1[t % 2][0:rows, :], ACT.Silu, scale=DOWN).then_inc(done["s"], 1)
                            high(i, at - HI_LAG)
                    if isinstance(n, int) and n == UNITS:
                        for t in range(PAIR_TILES - HI_LAG, PAIR_TILES):
                            high(PAIRS - 1, t)
                    if live(n, 2, UNITS) and u == 1:
                        pair = i - 1
                        wait(act, done["turned"], pair + 1)
                        wait(act, stored, pair * 32)
                        act.activation(outsb[:, :], bk_t[:, :], ACT.Identity).then_inc(done["out"], 1)

            @block.gpsimd
            def _(pool):
                for n, u, i in pipeline(pool, UNITS, STAGES, RING, 2 * RING):
                    for t in range(max(TILES)):
                        if live(n, 0, UNITS) and t < TILES[u]:
                            low(pool, i, TILE_AT[u] + t - LO_LAG, "lo_p")
                        if isinstance(n, int) and n == UNITS and t == 0:
                            for x in range(PAIR_TILES - LO_LAG, PAIR_TILES):
                                low(pool, PAIRS - 1, x, "lo_p")
                        if live(n, 1, UNITS):
                            pair, x = unit(i, u, 1)
                            for j in range(GROUPS[x][1]):
                                if ACC_AT[j] == t:
                                    e = GROUPS[x][0] + j
                                    wait(pool, done["part"], pair * EXPERTS + e + 1)
                                    if e == 0:
                                        wait(pool, done["turned"], pair)
                                    else:
                                        wait(pool, done["acc"], pair * EXPERTS + e)
                                    pool.tensor_tensor(acc[:, :], part[:, j, :], tile_of(H, pair) if e == 0 else acc[:, :], ALU.add).then_inc(done["acc"], 1)

            @block.vector
            def _(dve):
                def gating(i, u, j):
                    pair, x = unit(i, u, 1)
                    e = GROUPS[x][0] + j
                    wait(dve, gate_loaded[x], (pair + 1) * 32)
                    wait(dve, done["acc"], (pair if x else pair - 1) * EXPERTS + (BANK_BEFORE[e] + 1))
                    wait(dve, done["O"], pair * EXPERTS + e + 1)
                    dve.tensor_tensor(part[:, j, :], bk_o[j][:, :], gate[:, e, :], ALU.mult).then_inc(done["part"], 1)

                for n, u, i in pipeline(dve, UNITS, STAGES, RING, 2 * RING):
                    for t in range(max(TILES)):
                        if live(n, 0, UNITS) and t < TILES[u]:
                            at = TILE_AT[u] + t
                            rows = TILE_ROWS[at]
                            wait(dve, done["s"], i * PAIR_TILES + at + 1)
                            wait(dve, done["H3"], i * PAIR_TILES + at + 1)
                            old_pair, old = split_tile(i, at - SLOTS)
                            wait(dve, done["hi"], old_pair * PAIR_TILES + old + 1)
                            wait(dve, done[engine_of[old]], formed(engine_of[old], old_pair, old + 1))
                            dve.scalar_tensor_tensor(XN[0:rows, at % SLOTS, :], bk_h3[t % 2][0:rows, :], DOWN * HH_SCALE, s[0:rows, t % 2, :],
                                                     ALU.mult, ALU.mult).then_inc(done["hh"], 1)
                            low(dve, i, at - LO_LAG, "lo_d")
                        if isinstance(n, int) and n == UNITS and t == 0:
                            for x in range(PAIR_TILES - LO_LAG, PAIR_TILES):
                                low(dve, PAIRS - 1, x, "lo_d")
                        if live(n, 1, UNITS):
                            for j in range(GROUPS[unit(i, u, 1)[1]][1]):
                                if GATE_AT[j] == t:
                                    gating(i, u, j)


def lay_out(a):
    fixed = shape_constants()
    places = np.stack([a["L0_tok_instr_emb"][:SEQ], a["L0_tok_arg_emb"][:SEQ]])
    places = places.reshape(2 * BLK, P, D).transpose(1, 0, 2)
    w13 = np.stack([a["L0_ffn_w1"], a["L0_ffn_w3"]]).transpose(3, 0, 1, 2).reshape(D, 2, EXPERTS * HID)
    w2 = np.zeros((P, 2 * EXPERTS, D), np.float32)
    for (first, k), chunks in zip(GROUPS, CHUNKS):
        for j in range(k):
            w, at = a["L0_ffn_w2"][first + j].T, j * HID
            for half, (c, rows) in enumerate(chunks[j:j + 2]):
                low, high = max(c, at), min(c + rows, at + HID)
                w2[low - c:high - c, 2 * (first + j) + half] = w[low - at:high - at]
    return {"ids": a["x"], "token_emb": a["L0_tok_token_emb"], "place_emb": np.ascontiguousarray(places),
            "weights": pack_weights(a), "w13": np.ascontiguousarray(w13), "w2": w2, **fixed}


def kernel(**inputs):
    import concourse.bacc as bacc
    from concourse.bass_utils import run_bass_kernel_spmd

    nc = bacc.Bacc("TRN2", target_bir_lowering=False, num_devices=1)
    arrays, args = {}, []
    for name, a in lay_out({k: np.asarray(v) for k, v in inputs.items()}).items():
        arrays[f"in_{name}"] = a = np.ascontiguousarray(a)
        args.append(nc.dram_tensor(f"in_{name}", a.shape, mybir.dt.from_np(a.dtype), kind="ExternalInput").ap())
    out = nc.dram_tensor("out_0", [ROWS, SEQ, D], F32, kind="ExternalOutput").ap()
    tower(nc, *args, out)
    return run_bass_kernel_spmd(nc, [arrays], core_ids=[0]).results[0]["out_0"]
```

```python
from contextlib import ExitStack

import numpy as np
import concourse.bass as bass
from concourse import mybir

F32 = mybir.dt.float32
F16 = mybir.dt.float16
BF16 = mybir.dt.bfloat16
I32 = mybir.dt.int32
ALU = mybir.AluOpType
ACT = mybir.ActivationFunctionType
AX_X = mybir.AxisListType.X

P = 128
ROWS, SEQ, D = 32, 512, 64
PAIRS = ROWS // 2
BLK = SEQ // P
NEXT_ID = 5
EPS_LN, EPS_RMS = 1e-5, 1e-6
LR, WD, MAX_ALR, EPS_ADAM = 0.001, 0.01, 0.1, 1e-8
HEADS, KV, HD = 4, 2, 16
EXPERTS, HID = 8, 170
NEG = -1e30

WIDTH = [SEQ - P * c for c in range(BLK)]
START = [sum(WIDTH[:c]) for c in range(BLK)]
TRAP = sum(WIDTH)

C_ID, C_CENTRE, C_MEAN, C_FOLD = (P * j for j in range(4))
C_IOTA = 4 * P
C_EPS_LN, C_EPS_RMS = C_IOTA + BLK, C_IOTA + BLK + 1
C_EPS_BOTH = C_EPS_RMS + 1
C_RANK = C_EPS_BOTH + 1
C_COLS = C_RANK + EXPERTS


def shape_constants():
    p = np.arange(P)
    same_half = (p[:, None] // D == p[None, :] // D).astype(np.float32)
    c = np.zeros((P, C_COLS), np.float32)
    c[:, C_ID:C_ID + P] = np.eye(P)
    c[:, C_CENTRE:C_CENTRE + P] = np.eye(P) - same_half / D
    c[:, C_MEAN:C_MEAN + P] = same_half / D
    c[:, C_FOLD:C_FOLD + P] = p[:, None] % D == p[None, :] % D
    c[:, C_IOTA:C_IOTA + BLK] = p[:, None] + P * np.arange(BLK)[None, :]
    c[:, C_EPS_LN] = EPS_LN
    c[:, C_EPS_RMS] = EPS_RMS
    c[:, C_EPS_BOTH] = EPS_LN * EPS_RMS
    c[:, C_RANK:C_RANK + EXPERTS] = EXPERTS - np.arange(EXPERTS)
    position = np.tile(np.arange(SEQ, dtype=np.float32), (ROWS, 1))
    inv_freq = 1.0 / 10000.0 ** (np.arange(0, HD, 2, dtype=np.float32) / HD)
    angle = np.outer(np.arange(SEQ, dtype=np.float32), inv_freq)
    angle = np.concatenate([angle, angle], axis=-1)
    sign = np.where(np.arange(HD) < HD // 2, -1.0, 1.0).astype(np.float32)
    cos, sin = np.cos(angle).T, np.sin(angle).T * sign[:, None]
    scale = np.float32(HD ** -0.5)
    turn = [np.tile(np.repeat(t, heads, axis=0), (P // (HD * heads), 1))
            for t, heads in ((cos * scale, HEADS), (sin * scale, HEADS), (cos, KV), (sin, KV))]
    turn = np.stack(turn, axis=1).astype(np.float32)
    causal = np.where(p[:, None] <= p[None, :], 0.0, NEG).astype(np.float32)
    return {"consts": c, "position": position, "turn": np.ascontiguousarray(turn), "causal": causal}


def wait(eng, sem, count):
    if isinstance(count, int) and count <= 0:
        return
    eng.wait_ge(sem, count)


def live(n, stage, tiles):
    return not isinstance(n, int) or 0 <= n - stage < tiles


def pipeline(eng, tiles, stages, ring=2, first=0):
    first = first or (stages + ring) // ring * ring
    for n in range(first):
        yield n, n % ring, n // ring
    with eng.Fori(first // ring, tiles // ring) as i:
        for u in range(ring):
            yield ring * i + u, u, i
    for n in range(tiles, tiles + stages - 1):
        yield n, n % ring, n // ring


def turns(i, u, stage=0, ring=2):
    return i + (u - stage) // ring + 1



(W_K, W_Q, W_V, W_LR, W_0, W_1, W_1T, W_FQ, W_FQR) = (P * j for j in range(9))
W_01 = 9 * P
W_FK, W_FKR, W_FV, W_O = (W_01 + P + D * j for j in range(4))
W_ROUTE = W_O + D
V_GAMMA, V_BETA, V_B0, V_B1, V_BLR, V_LN1, V_LN2 = (W_ROUTE + 2 * EXPERTS + j for j in range(7))
W_COLS = V_LN2 + 1


def diagonal(w):
    k, m = w.shape
    out = np.zeros((2 * k, 2 * m), np.float32)
    out[:k, :m] = w
    out[k:, m:] = w
    return out


def twice(w):
    return np.concatenate([w, w], axis=0)


def pack_weights(a):
    ws, bs = a["L0_attn_Ws"], a["L0_attn_bs"]
    swap = np.arange(D).reshape(-1, 2, HD // 2)[:, ::-1].reshape(-1)
    by_dim = {n: np.arange(n * HD).reshape(n, HD).T.reshape(-1) for n in (HEADS, KV)}
    fq, fk, fv = a["L0_ffn_wq"].T, a["L0_ffn_wk"].T, a["L0_ffn_wv"].T
    wo = np.zeros((P, D), np.float32)
    for h in range(HEADS):
        wo[32 * h:32 * h + HD] = a["L0_ffn_wo"].T[HD * h:HD * (h + 1)]
    vectors = [a["L0_tok_gamma"], a["L0_tok_beta"], bs[0], bs[1], np.repeat(a["L0_attn_blr"], D),
               a["L0_ffn_ln1_w"], a["L0_ffn_ln2_w"]]
    parts = [diagonal(w) for w in (a["L0_attn_Wk"], a["L0_attn_Wq"], a["L0_attn_Wv"],
                                   np.repeat(a["L0_attn_Wlr"], D, axis=1), ws[0], ws[1], ws[1].T,
                                   fq[:, by_dim[HEADS]], fq[:, swap[by_dim[HEADS]]])]
    parts += [twice(ws[0]), twice(ws[1])]
    parts += [diagonal(w) for w in (fk[:, by_dim[KV]], fk[:, swap[by_dim[KV]]], fv)]
    parts += [wo, diagonal(a["L0_ffn_router_w"].T)]
    parts += [twice(v[:, None]) for v in vectors]
    return np.ascontiguousarray(np.concatenate(parts, axis=1))


def tower(nc, ids, ids_down, token_emb, place_emb, weights, w13, w2, consts, position, turn, causal, out):
    ctx = ExitStack()
    with ctx:
        def sb(name, shape, dt=F32):
            return ctx.enter_context(nc.sbuf_tensor(name, shape, dt))

        sems = []

        def sem(name):
            sems.append(nc.alloc_semaphore(name=name))
            return sems[-1]

        def recycle():
            nc.all_engine_barrier()
            nc.clear_and_free_semaphores(sems)
            sems.clear()
            nc.all_engine_barrier()

        banks = [ctx.enter_context(nc.psum_tensor(f"bank{j}", [P, SEQ], F32)) for j in range(8)]

        H = sb("H", [P, PAIRS, SEQ])
        XN = sb("XN", [P, PAIRS, SEQ])
        CST = sb("CST", [P, C_COLS])
        W = sb("W", [P, W_COLS])

        def wcols(at, cols=P):
            return W[:, at:at + cols]

        def vec(at):
            return W[:, at:at + 1]

        ident = CST[:, C_ID:C_ID + P]
        centre = CST[:, C_CENTRE:C_CENTRE + P]
        mean = CST[:, C_MEAN:C_MEAN + P]
        fold = CST[:, C_FOLD:C_FOLD + P]
        eps_ln = CST[:, C_EPS_LN:C_EPS_LN + 1]
        eps_rms = CST[:, C_EPS_RMS:C_EPS_RMS + 1]
        eps_both = CST[:, C_EPS_BOTH:C_EPS_BOTH + 1]

        with ExitStack() as inner:
            MK = inner.enter_context(nc.sbuf_tensor("MK", [P, PAIRS, SEQ], F32))
            embed(nc, sb, sem, banks, ids, ids_down, token_emb, place_emb, weights, consts, position,
                  H, XN, MK, CST, W, ident, mean, centre, eps_ln, wcols, vec)
            with ExitStack() as later:
                NW, NB = learn(nc, later, sem, banks, XN, MK, W, wcols, vec, ident, fold)
                retrieve(nc, later, sem, banks, XN, H, W, wcols, NW, NB)
        recycle()
        with ExitStack() as outer:
            FS = outer.enter_context(nc.sbuf_tensor("FS", [P, ROWS, SEQ], F16))
            LG = outer.enter_context(nc.sbuf_tensor("g_logits", [P, PAIRS, BLK * G8], F32))
            fhi, flo = (outer.enter_context(nc.sbuf_tensor(n, [P, 2, SEQ], F16)) for n in ("g_hi", "g_lo"))
            stacked = [sem(f"stacked{v}") for v in range(2)]
            with ExitStack() as inner:
                VT = inner.enter_context(nc.sbuf_tensor("VT", [P, PAIRS, BLK * 2 * KV * HD], F32))
                q_parts = nc.dram_tensor("q_parts", [PAIRS, 3, 2, HD, HEADS, SEQ], BF16, kind="Internal").ap()
                k_parts = nc.dram_tensor("k_parts", [PAIRS, 3, 2, HD, KV, SEQ], BF16, kind="Internal").ap()
                parts_stored = [sem(f"parts_stored{u}") for u in range(2)]
                K = inner.enter_context(nc.sbuf_tensor("t_k", [KEY_ROWS, KEY_RING, KV, SEQ], BF16))
                Q = inner.enter_context(nc.sbuf_tensor("t_q", [KEY_ROWS, KEY_RING, HEADS, SEQ], BF16))
                q_loaded = [sem(f"q_loaded{u}") for u in range(KEY_RING)]
                V = inner.enter_context(nc.sbuf_tensor("t_v", [P, 2, BLK, KV, 32], F32))
                mask, eye = (inner.enter_context(nc.sbuf_tensor(n, [P, P], BF16)) for n in ("mask", "eye"))
                project(nc, sem, banks, H, XN, W, VT, q_parts, k_parts, parts_stored, turn, causal, Q, K, q_loaded, V, mask, eye, LG,
                        ident, centre, mean, eps_ln, eps_both, vec)
                attend(nc, sem, banks, H, XN, W, VT, q_parts, k_parts, parts_stored, Q, K, q_loaded, V, mask, eye, FS, LG,
                       fhi, flo, stacked, ident, mean, eps_rms)
            gates = nc.dram_tensor("gates", [PAIRS, 2, EXPERTS, SEQ], F32, kind="Internal").ap()
            whi, wlo = (outer.enter_context(nc.sbuf_tensor(n, [P, 2 * EXPERTS * HID], F16)) for n in ("whi", "wlo"))
            v2hi, v2lo = (outer.enter_context(nc.sbuf_tensor(n, [P, 2 * EXPERTS, D], F16)) for n in ("v2hi", "v2lo"))
            gateT = outer.enter_context(nc.sbuf_tensor("g_gateT", [P, 2, BLK, P], F32))
            gates_stored = route(nc, sem, banks, XN, LG, CST, gates, gateT, w13, w2, whi, wlo, v2hi, v2lo, ident, vec)
            experts(nc, sem, banks, H, XN, FS, stacked, gates, gates_stored, whi, wlo, v2hi, v2lo, out, ident)


def embed(nc, sb_, sem, banks, ids, ids_down, token_emb, place_emb, weights, consts, position,
          H, XN, MK, CST, W, ident, mean, centre, eps_ln, wcols, vec):
    ids16 = nc.dram_tensor("ids16", [2, ROWS, SEQ], F16, kind="Internal").ap()
    with ExitStack() as ctx:
        def sb(name, shape, dt=F32):
            return ctx.enter_context(nc.sbuf_tensor(name, shape, dt))

        pos = sb("pos", [ROWS, SEQ])
        xi = sb("xi", [ROWS, SEQ], I32)
        xf = sb("xf", [ROWS, SEQ])
        starts = sb("starts", [ROWS, SEQ])
        ones = sb("ones", [ROWS, SEQ])
        seg = sb("seg", [ROWS, SEQ])
        place16 = sb("place16", [ROWS, 2, SEQ], F16)
        tokid = sb("tokid", [P, PAIRS, BLK * 2], I32)
        pemb = sb("pemb", [P, 2 * BLK, D])
        table = sb("table", [P, 3, 2 * BLK, D], BF16)
        tokcol = sb("tokcol", [P, 2, BLK * 2], I32)
        tok = sb("tok", [P, 2, BLK, 2, D])
        where = sb("where", [P, 2, 2, 2, SEQ], F16)
        onehot = sb("onehot", [P, 2, 2, 2 * TRAP], BF16)
        pmean = sb("pmean", [P, 2 * BLK])
        toksum = sb("toksum", [P, 2 * BLK])
        centred = sb("centred", [P, 2, BLK, 2, D])
        prest = centred[:, 0].rearrange("p q a f -> p (q a) f")
        sq1, sq2, ln1, ln2, r1, r2 = (sb(n, [P, SEQ]) for n in ("sq1", "sq2", "ln1", "ln2", "r1", "r2"))
        normed = sb("normed", [P, SEQ])

        loaded, xloaded, ploaded, cloaded = sem("loaded"), sem("xloaded"), sem("ploaded"), sem("cloaded")
        step, tok_ready, places_stored = sem("step"), sem("tok_ready"), sem("places_stored")
        places_ready, table_ready, table_step = sem("places_ready"), sem("table_ready"), sem("table_step")
        col_ready, col_seen, gathered = sem("col_ready"), sem("col_seen"), [sem(f"gathered{u}") for u in range(2)]
        where_loaded, onehot_ready, tok_summed, tok_centred, embedded = [sem(f"where_loaded{u}") for u in range(2)], sem("onehot_ready"), sem("tok_summed"), sem("tok_centred"), sem("embedded")
        sq1_done, v1_done, ln1_done, r1_done, n1_done, h_done = (sem(f"{n}_a") for n in ("sq", "v", "ln", "r", "n", "h"))
        c2_done, sq2_done, v2_done, ln2_done, r2_done, xn_done = (sem(f"{n}_b") for n in ("c", "sq", "v", "ln", "r", "xn"))

        ps_c1, ps_c2, ps_v1, ps_v2 = banks[1:3], banks[3:5], banks[5], banks[6]
        ps_k, keys_done, keys_kept = banks[0], sem("keys_done"), sem("keys_kept")
        STAGES = 5

        with nc.Block() as block:
            @block.sync
            def _(sp):
                sp.dma_start(xi[:, :], ids).then_inc(xloaded, 16)
                sp.dma_start(tokid[:, :, :], ids_down).then_inc(tok_ready, 16)
                sp.dma_start(pos[:, :], position).then_inc(xloaded, 16)
                sp.dma_start(CST[:, :], consts).then_inc(cloaded, 16)
                sp.dma_start(pemb[:, :, :], place_emb).then_inc(ploaded, 16)
                sp.dma_start(W[:, :], weights).then_inc(loaded, 16)
                sp.wait_ge(places_ready, 2)
                sp.dma_start(ids16.rearrange("t r s -> r t s"), place16[:, :, :]).then_inc(places_stored, 16)
                sp.wait_ge(places_stored, 16)
                for n, u, i in pipeline(sp, PAIRS, STAGES):
                    if live(n, 0, PAIRS):
                        wait(sp, onehot_ready, n - 1)
                        sp.dma_start(where[:, u], ids16[:, bass.ds(2 * n, 2), :].partition_broadcast(P)).then_inc(where_loaded[u], 16)

            @block.gpsimd
            def _(pool):
                pool.wait_ge(tok_ready, 16)
                for n, u, i in pipeline(pool, PAIRS, STAGES):
                    if live(n, 0, PAIRS):
                        wait(pool, tok_centred, n - 1)
                        pool.sem_inc(col_seen, 1)
                        pool.tensor_copy(tokcol[:, u, :], tokid[:, bass.ds(n, 1), :].rearrange("p a b -> p (a b)")).then_inc(col_ready, 1)
                        wait(pool, col_ready, n + 1)
                        pool.sem_inc(col_seen, 1)
                        for q in range(BLK):
                            for a in range(2):
                                pool.indirect_dma_start(
                                    out=tok[:, u, q, a, :], out_offset=None, in_=token_emb,
                                    in_offset=bass.IndirectOffsetOnAxis(ap=tokcol[:, u, 2 * q + a:2 * q + a + 1], axis=0),
                                ).then_inc(gathered[u], 16)

            @block.vector
            def _(dve):
                count = [0]

                def then(ins):
                    count[0] += 1
                    ins.then_inc(step, 1)
                    dve.wait_ge(step, count[0])

                then(dve.memset(ones[:, :], 1.0))
                then(dve.memset(starts[:, :], 0.0))
                dve.wait_ge(xloaded, 32)
                then(dve.tensor_copy(xf[:, :], xi[:, :]))
                then(dve.tensor_scalar(starts[:, 1:SEQ], xf[:, 0:SEQ - 1], float(NEXT_ID), None, ALU.is_equal))
                dve.tensor_tensor_scan(place16[:, 0, :], ones[:, :], starts[:, :], 0.0, ALU.mult, ALU.add).then_inc(places_ready, 1)
                then(dve.tensor_tensor(seg[:, :], starts[:, :], pos[:, :], ALU.mult))
                dve.wait_ge(places_ready, 1)
                last = ones
                then(dve.tensor_tensor_scan(last[:, :], seg[:, :], seg[:, :], 0.0, ALU.max, ALU.max))
                dve.tensor_tensor(place16[:, 1, :], pos[:, :], last[:, :], ALU.subtract).then_inc(places_ready, 1)
                dve.wait_ge(ploaded, 16)
                then(dve.tensor_reduce(pmean[:, :], pemb[:, :, :], AX_X, ALU.add))
                then(dve.tensor_scalar(pmean[:, :], pmean[:, :], 1.0 / D, None, ALU.mult))
                then(dve.tensor_tensor(pemb[:, :, :], pemb[:, :, :], pmean[:, :].unsqueeze(2).to_broadcast([P, 2 * BLK, D]), ALU.subtract))
                then(dve.tensor_copy(table[:, 0], pemb[:, :, :]))
                then(dve.tensor_tensor(prest, pemb[:, :, :], table[:, 0], ALU.subtract))
                then(dve.tensor_copy(table[:, 1], prest))
                dve.tensor_tensor(table[:, 2], prest, table[:, 1], ALU.subtract).then_inc(table_ready, 1)
                dve.wait_ge(cloaded, 16)
                dve.wait_ge(loaded, 16)
                for n, u, i in pipeline(dve, PAIRS, STAGES):
                    if live(n, 0, PAIRS):
                        dve.wait_ge(where_loaded[u], turns(i, u) * 16)
                        wait(dve, embedded, n - 1)
                        for t in range(2):
                            for c in range(BLK):
                                at, w = 2 * START[c], WIDTH[c]
                                mark = dve.tensor_scalar(
                                    onehot[:, u, t, at:at + 2 * w].rearrange("p (a s) -> p a s", a=2),
                                    where[:, u, t, :, SEQ - w:], CST[:, C_IOTA + c:C_IOTA + c + 1], None, ALU.is_equal)
                        mark.then_inc(onehot_ready, 1)
                    if live(n, 1, PAIRS):
                        m, v = n - 1, 1 - u
                        pieces = tok[:, v].rearrange("p q a f -> p (q a) f")
                        dve.wait_ge(gathered[v], turns(i, u, 1) * 2 * BLK * 16)
                        wait(dve, tok_centred, m)
                        dve.tensor_reduce(toksum[:, :], pieces, AX_X, ALU.add).then_inc(tok_summed, 1)
                        wait(dve, tok_summed, m + 1)
                        wait(dve, embedded, m - 1)
                        dve.scalar_tensor_tensor(centred[:, v].rearrange("p q a f -> p (q a) f"), toksum[:, :].unsqueeze(2).to_broadcast([P, 2 * BLK, D]),
                                                 -1.0 / D, pieces, ALU.mult, ALU.add).then_inc(tok_centred, 1)
                    if live(n, 2, PAIRS):
                        m = n - 2
                        dve.wait_ge(r1_done, m + 1)
                        wait(dve, h_done, m)
                        dve.tensor_tensor(normed[:, :], ps_c1[u][:, :], r1[:, :], ALU.mult).then_inc(n1_done, 1)
                        dve.wait_ge(n1_done, m + 1)
                        dve.tensor_scalar(H[:, bass.ds(m, 1), :].rearrange("p a s -> p (a s)"), normed[:, :], vec(V_GAMMA), vec(V_BETA), ALU.mult, ALU.add).then_inc(h_done, 1)
                    if live(n, 3, PAIRS):
                        m, v = n - 3, 1 - u
                        dve.wait_ge(r2_done, m + 1)
                        dve.tensor_tensor(XN[:, bass.ds(m, 1), :].rearrange("p a s -> p (a s)"), ps_c2[v][:, :], r2[:, :], ALU.mult).then_inc(xn_done, 1)

            @block.tensor
            def _(pe):
                pe.wait_ge(cloaded, 16)
                pe.wait_ge(table_ready, 1)
                pe.wait_ge(loaded, 16)
                for n, u, i in pipeline(pe, PAIRS, STAGES):
                    if live(n, 1, PAIRS):
                        m, v = n - 1, 1 - u
                        wait(pe, n1_done, m - 1)
                        pe.wait_ge(onehot_ready, m + 1)
                        for t in range(2):
                            for part in range(3):
                                for c in range(BLK):
                                    w = WIDTH[c]
                                    for a in range(2):
                                        at = 2 * START[c] + a * w
                                        pe.matmul(ps_c1[v][a * D:(a + 1) * D, SEQ - w:], table[:, part, t * BLK + c, :],
                                                  onehot[:, v, t, at:at + w], start=t + part + c == 0, stop=False, skip_group_check=True)
                    if live(n, 3, PAIRS):
                        m, v = n - 3, 1 - u
                        pe.wait_ge(h_done, m + 1)
                        wait(pe, xn_done, m - 1)
                        pe.matmul(ps_c2[v][:, :], centre, H[:, bass.ds(m, 1), :].rearrange("p a s -> p (a s)"), start=True, stop=True).then_inc(c2_done, 1)
                    if live(n, 2, PAIRS):
                        m = n - 2
                        pe.wait_ge(sq1_done, m + 1)
                        wait(pe, ln1_done, m)
                        pe.matmul(ps_v1[:, :], mean, sq1[:, :], start=True, stop=True).then_inc(v1_done, 1)
                    if live(n, 4, PAIRS):
                        m = n - 4
                        pe.wait_ge(xn_done, m + 1)
                        wait(pe, keys_kept, m)
                        pe.matmul(ps_k[:, :], wcols(W_K), tile_of(XN, m), start=True, stop=True).then_inc(keys_done, 1)
                    if live(n, 3, PAIRS):
                        m = n - 3
                        pe.wait_ge(sq2_done, m + 1)
                        wait(pe, ln2_done, m)
                        pe.matmul(ps_v2[:, :], mean, sq2[:, :], start=True, stop=True).then_inc(v2_done, 1)
                    if live(n, 1, PAIRS):
                        m, v = n - 1, 1 - u
                        pe.wait_ge(tok_centred, m + 1)
                        for q in range(BLK):
                            mm = pe.matmul(ps_c1[v][:, q * P:(q + 1) * P], centred[:, v, q].rearrange("p a f -> p (a f)"), ident,
                                           start=False, stop=False, skip_group_check=True)
                        mm.then_inc(embedded, 1)

            @block.scalar
            def _(act):
                act.preload_act_table_set("natural_log_exp_and_others")
                act.wait_ge(cloaded, 16)
                for n, u, i in pipeline(act, PAIRS, STAGES):
                    if live(n, 2, PAIRS):
                        m = n - 2
                        act.wait_ge(embedded, m + 1)
                        wait(act, v1_done, m)
                        act.activation(sq1[:, :], ps_c1[u][:, :], ACT.Square).then_inc(sq1_done, 1)
                    if live(n, 3, PAIRS):
                        m, v = n - 3, 1 - u
                        act.wait_ge(c2_done, m + 1)
                        wait(act, v2_done, m)
                        act.activation(sq2[:, :], ps_c2[v][:, :], ACT.Square).then_inc(sq2_done, 1)
                    if live(n, 2, PAIRS):
                        m = n - 2
                        act.wait_ge(v1_done, m + 1)
                        act.activation(ln1[:, :], ps_v1[:, :], ACT.Ln, bias=eps_ln).then_inc(ln1_done, 1)
                        act.wait_ge(ln1_done, m + 1)
                        wait(act, n1_done, m)
                        act.activation(r1[:, :], ln1[:, :], ACT.Exp, scale=-0.5).then_inc(r1_done, 1)
                    if live(n, 3, PAIRS):
                        m = n - 3
                        act.wait_ge(v2_done, m + 1)
                        act.activation(ln2[:, :], ps_v2[:, :], ACT.Ln, bias=eps_ln).then_inc(ln2_done, 1)
                        act.wait_ge(ln2_done, m + 1)
                        wait(act, xn_done, m)
                        act.activation(r2[:, :], ln2[:, :], ACT.Exp, scale=-0.5).then_inc(r2_done, 1)
                    if live(n, 4, PAIRS):
                        m = n - 4
                        act.wait_ge(keys_done, m + 1)
                        act.activation(tile_of(MK, m), ps_k[:, :], ACT.Identity).then_inc(keys_kept, 1)

def tile_of(big, m):
    return big[:, bass.ds(m, 1), :].rearrange("p a s -> p (a s)")


def learn(nc, outer, sem, banks, XN, MK, W, wcols, vec, ident, fold):
    NW = outer.enter_context(nc.sbuf_tensor("NW", [P, 2, P], F32))
    NB = outer.enter_context(nc.sbuf_tensor("NB", [P, 2], F32))
    with ExitStack() as ctx:
        def sb(name, shape, dt=F32):
            return ctx.enter_context(nc.sbuf_tensor(name, shape, dt))

        k, tlr, s0, x1, w0, s1, t1 = (sb(f"m_{n}", [P, 2, SEQ]) for n in ("k", "tlr", "s0", "x1", "w0", "s1", "t1"))
        t0, u0, x2, e, g, u1, w1, dz1, dx1, dz0, kT, x1T, dz1T, dz0T = (
            sb(f"m_{n}", [P, SEQ]) for n in ("t0", "u0", "x2", "e", "g", "u1", "w1", "dz1", "dx1", "dz0", "kT", "x1T", "dz1T", "dz0T"))
        gbs = sb("gbs", [P, 2, PAIRS])
        half_b = sb("half_b", [P, 3])
        names = ("L", "k", "tlr", "Z0", "s0", "t0", "x1", "u0", "w0", "Z1", "V", "s1", "t1", "x2", "e", "g", "u1", "w1",
                 "dz1", "B", "dx1", "dz0", "Tk", "Tx1", "Tdz1", "Tdz0", "kT", "x1T", "dz1T", "dz0T", "grads")
        done = {n: sem(f"learn_{n}") for n in names}
        half_ready, updated = sem("half_ready"), sem("updated")
        bk_z0, bk_z1, bk_v, bk_b, bk_t0, bk_t1, bk_t2, bk_grad = banks
        STAGES = 3

        with nc.Block() as block:
            @block.tensor
            def _(pe):
                def turn(bank, source, name):
                    for q in range(BLK):
                        mm = pe.transpose(bank[:, q * P:(q + 1) * P], source[:, q * P:(q + 1) * P], ident)
                    mm.then_inc(done[name], 1)

                for n, u, i in pipeline(pe, PAIRS, STAGES):
                    v, m = 1 - u, n - 1
                    front, back, last = live(n, 0, PAIRS), live(n, 1, PAIRS), live(n, 2, PAIRS)
                    if front:
                        wait(pe, done["s1"], n)
                        wait(pe, done["t1"], n)
                        pe.matmul(bk_z1[:, :], wcols(W_LR), tile_of(XN, n), start=True, stop=True).then_inc(done["L"], 1)
                    if last:
                        wait(pe, done["dz0"], m)
                        wait(pe, done["kT"], m)
                        turn(bk_t0, dz0, "Tdz0")
                    if front:
                        wait(pe, done["s0"], n)
                        wait(pe, done["t0"], n)
                        wait(pe, done["k"], n + 1)
                        pe.matmul(bk_z0[:, :], wcols(W_0), k[:, u, :], start=True, stop=True).then_inc(done["Z0"], 1)
                    if last:
                        wait(pe, done["x1T"], m)
                        wait(pe, done["dz1T"], m)
                        for q in range(BLK):
                            pe.matmul(bk_grad[:, P:2 * P], x1T[:, q * P:(q + 1) * P], dz1T[:, q * P:(q + 1) * P],
                                      start=isinstance(n, int) and m == 1 and q == 0, stop=False, skip_group_check=True)
                        wait(pe, done["dz0T"], m)
                        for q in range(BLK):
                            mm = pe.matmul(bk_grad[:, 0:P], kT[:, q * P:(q + 1) * P], dz0T[:, q * P:(q + 1) * P],
                                           start=False, stop=False, skip_group_check=True)
                        mm.then_inc(done["grads"], 1)
                    if back:
                        wait(pe, done["dz1"], m + 1)
                        wait(pe, done["dx1"], m)
                        pe.matmul(bk_b[:, :], wcols(W_1T), dz1[:, :], start=True, stop=True).then_inc(done["B"], 1)
                    if front:
                        wait(pe, done["x1"], n + 1)
                        wait(pe, done["tlr"], n + 1)
                        pe.matmul(bk_z1[:, :], wcols(W_1), x1[:, u, :], start=True, stop=True).then_inc(done["Z1"], 1)
                    if back:
                        wait(pe, done["dz0T"], m)
                        turn(bk_t0, k[:, v, :], "Tk")
                        wait(pe, done["x1T"], m)
                        turn(bk_t1, x1[:, v, :], "Tx1")
                        wait(pe, done["dz1T"], m)
                        turn(bk_t2, dz1, "Tdz1")
                    if front:
                        wait(pe, done["e"], n)
                        pe.matmul(bk_v[:, :], wcols(W_V), tile_of(XN, n), start=True, stop=True).then_inc(done["V"], 1)

            @block.scalar
            def _(act):
                act.preload_act_table_set("silu_and_others")
                act.wait_ge(half_ready, 1)

                def run(name, to, source, func, **more):
                    act.activation(to, source, func, **more).then_inc(done[name], 1)

                for n, u, i in pipeline(act, PAIRS, STAGES):
                    m = n - 1
                    front, back = live(n, 0, PAIRS), live(n, 1, PAIRS)
                    if front:
                        wait(act, done["Tk"], n - 1)
                        run("k", k[:, u, :], tile_of(MK, n), ACT.Identity)
                        wait(act, done["L"], n + 1)
                        wait(act, done["g"], n - 1)
                        run("tlr", tlr[:, u, :], bk_z1[:, :], ACT.Tanh, bias=half_b[:, 2:3], scale=0.5)
                    if live(n, 2, PAIRS):
                        wait(act, done["grads"], n - 2)
                        wait(act, done["Tdz0"], m)
                        run("dz0T", dz0T[:, :], bk_t0[:, :], ACT.Identity)
                    if front:
                        wait(act, done["Z0"], n + 1)
                        wait(act, done["w0"], n - 1)
                        run("s0", s0[:, u, :], bk_z0[:, :], ACT.Silu, bias=vec(V_B0))
                        wait(act, done["u0"], n)
                        run("t0", t0[:, :], bk_z0[:, :], ACT.Tanh, bias=half_b[:, 0:1], scale=0.5)
                    if front:
                        wait(act, done["Z1"], n + 1)
                        wait(act, done["x2"], n - 1)
                        wait(act, done["w1"], n - 1)
                        run("s1", s1[:, u, :], bk_z1[:, :], ACT.Silu, bias=vec(V_B1))
                        run("t1", t1[:, u, :], bk_z1[:, :], ACT.Tanh, bias=half_b[:, 1:2], scale=0.5)
                    if back:
                        wait(act, done["grads"], m)
                        wait(act, done["Tk"], m + 1)
                        run("kT", kT[:, :], bk_t0[:, :], ACT.Identity)
                        wait(act, done["Tx1"], m + 1)
                        run("x1T", x1T[:, :], bk_t1[:, :], ACT.Identity)

            @block.gpsimd
            def _(pool):
                for n, u, i in pipeline(pool, PAIRS, STAGES):
                    if live(n, 1, PAIRS):
                        m, v = n - 1, 1 - u
                        wait(pool, done["s1"], m + 1)
                        wait(pool, done["e"], m)
                        pool.tensor_tensor(x2[:, :], x1[:, v, :], s1[:, v, :], ALU.add).then_inc(done["x2"], 1)

            @block.vector
            def _(dve):
                dve.tensor_scalar(half_b[:, 0:2], W[:, V_B0:V_B1 + 1], 0.5, None, ALU.mult)
                dve.tensor_scalar(half_b[:, 2:3], vec(V_BLR), 0.5, None, ALU.mult).then_inc(half_ready, 1)
                for n, u, i in pipeline(dve, PAIRS, STAGES):
                    v, m = 1 - u, n - 1
                    front, back = live(n, 0, PAIRS), live(n, 1, PAIRS)
                    if back:
                        wait(dve, done["x2"], m + 1)
                        wait(dve, done["V"], m + 1)
                        dve.tensor_tensor(e[:, :], x2[:, :], bk_v[:, :], ALU.subtract).then_inc(done["e"], 1)
                        wait(dve, done["t1"], m + 1)
                        dve.tensor_scalar(u1[:, :], t1[:, v, :], 1.0, None, ALU.subtract).then_inc(done["u1"], 1)
                        wait(dve, done["e"], m + 1)
                        dve.scalar_tensor_tensor(g[:, :], tlr[:, v, :], 1.0, e[:, :], ALU.add, ALU.mult).then_inc(done["g"], 1)
                        wait(dve, done["u1"], m + 1)
                        dve.scalar_tensor_tensor(w1[:, :], s1[:, v, :], 1.0, u1[:, :], ALU.subtract, ALU.mult).then_inc(done["w1"], 1)
                        wait(dve, done["w1"], m + 1)
                        wait(dve, done["Tdz1"], m)
                        dve.scalar_tensor_tensor(dz1[:, :], w1[:, :], 2.0, g[:, :], ALU.subtract, ALU.mult,
                                                 accum_out=gbs[:, 1, bass.ds(m, 1)]).then_inc(done["dz1"], 1)
                    if front:
                        wait(dve, done["s0"], n + 1)
                        wait(dve, done["Tx1"], n - 1)
                        dve.tensor_tensor(x1[:, u, :], k[:, u, :], s0[:, u, :], ALU.add).then_inc(done["x1"], 1)
                        wait(dve, done["t0"], n + 1)
                        dve.tensor_scalar(u0[:, :], t0[:, :], 1.0, None, ALU.subtract).then_inc(done["u0"], 1)
                        wait(dve, done["u0"], n + 1)
                        dve.scalar_tensor_tensor(w0[:, u, :], s0[:, u, :], 1.0, u0[:, :], ALU.subtract, ALU.mult).then_inc(done["w0"], 1)
                    if back:
                        wait(dve, done["B"], m + 1)
                        dve.scalar_tensor_tensor(dx1[:, :], bk_b[:, :], -0.5, g[:, :], ALU.mult, ALU.add).then_inc(done["dx1"], 1)
                        wait(dve, done["dx1"], m + 1)
                        wait(dve, done["Tdz0"], m)
                        dve.scalar_tensor_tensor(dz0[:, :], w0[:, v, :], 2.0, dx1[:, :], ALU.subtract, ALU.mult,
                                                 accum_out=gbs[:, 0, bass.ds(m, 1)]).then_inc(done["dz0"], 1)
                        wait(dve, done["grads"], m)
                        wait(dve, done["Tdz1"], m + 1)
                        dve.tensor_copy(dz1T[:, :], bk_t2[:, :]).then_inc(done["dz1T"], 1)

        gd = sb("gd", [P, 2, D])
        gb = sb("gb", [P, 2])
        grad = sb("grad", [P, 2 * D + 2])
        size = sb("size", [P, 2 * D + 2])
        param = sb("param", [P, 2 * D + 2])
        folded, gathered_g, chain = sem("folded"), sem("gathered_g"), sem("chain")
        with nc.Block() as block:
            @block.vector
            def _(dve):
                count = [0]

                def then(ins):
                    count[0] += 1
                    ins.then_inc(chain, 1)
                    dve.wait_ge(chain, count[0])

                dve.tensor_reduce(gb[:, :], gbs[:, :, :], AX_X, ALU.add).then_inc(gathered_g, 1)
                dve.memset(NW[:, :, :], 0.0).then_inc(gathered_g, 1)
                dve.tensor_copy(param[:, 2 * D:], W[:, V_B0:V_B1 + 1])
                for layer in range(2):
                    for a in range(2):
                        half = slice(a * D, (a + 1) * D)
                        dve.tensor_copy(gd[half, layer, :], bk_grad[half, layer * P + a * D:layer * P + (a + 1) * D]).then_inc(gathered_g, 1)
                then(dve.tensor_copy(param[:, 0:2 * D], W[:, W_01:W_01 + 2 * D]))
                dve.wait_ge(folded, 2)
                then(dve.tensor_scalar(grad[:, :], bk_v[:, 0:2 * D + 2], -0.5 * 2.0 / D * MAX_ALR * 0.5, None, ALU.mult))
                then(dve.scalar_tensor_tensor(size[:, :], grad[:, :], -1.0, grad[:, :], ALU.mult, ALU.max))
                then(dve.tensor_scalar(size[:, :], size[:, :], EPS_ADAM, None, ALU.add))
                then(dve.reciprocal(size[:, :], size[:, :]))
                then(dve.scalar_tensor_tensor(grad[:, :], grad[:, :], -LR, size[:, :], ALU.mult, ALU.mult))
                then(dve.scalar_tensor_tensor(param[:, :], param[:, :], 1.0 - LR * WD, grad[:, :], ALU.mult, ALU.add))
                for layer in range(2):
                    for a in range(2):
                        half = slice(a * D, (a + 1) * D)
                        then(dve.tensor_copy(NW[half, layer, a * D:(a + 1) * D], param[half, layer * D:(layer + 1) * D]))
                then(dve.tensor_copy(NB[:, :], param[:, 2 * D:]))

            @block.tensor
            def _(pe):
                pe.wait_ge(gathered_g, 6)
                pe.matmul(bk_v[:, 0:2 * D], fold, gd[:, :, :].rearrange("p l d -> p (l d)"), start=True, stop=True).then_inc(folded, 1)
                pe.matmul(bk_v[:, 2 * D:2 * D + 2], fold, gb[:, :], start=False, stop=True, skip_group_check=True).then_inc(folded, 1)
    return NW, NB


def retrieve(nc, ctx, sem, banks, XN, H, W, wcols, NW, NB):
    q, s0, x1, s1 = (ctx.enter_context(nc.sbuf_tensor(f"r_{n}", [P, 2, SEQ], F32)) for n in ("q", "s0", "x1", "s1"))
    done = {n: sem(f"read_{n}") for n in ("Q", "q", "Z0", "s0", "x1", "Z1", "s1", "x2", "h")}
    STAGES = 3
    with nc.Block() as block:
        @block.tensor
        def _(pe):
            for n, u, i in pipeline(pe, PAIRS, STAGES):
                if live(n, 0, PAIRS):
                    wait(pe, done["q"], n - 1)
                    pe.matmul(banks[u][:, :], wcols(W_Q), tile_of(XN, n), start=True, stop=True).then_inc(done["Q"], 1)
                if live(n, 1, PAIRS):
                    wait(pe, done["q"], n)
                    wait(pe, done["s0"], n - 2)
                    pe.matmul(banks[3 - u][:, :], NW[:, 0, :], q[:, 1 - u, :], start=True, stop=True).then_inc(done["Z0"], 1)
                if live(n, 2, PAIRS):
                    wait(pe, done["x1"], n - 1)
                    wait(pe, done["s1"], n - 3)
                    pe.matmul(banks[4 + u][:, :], NW[:, 1, :], x1[:, u, :], start=True, stop=True).then_inc(done["Z1"], 1)

        @block.scalar
        def _(act):
            for n, u, i in pipeline(act, PAIRS, STAGES):
                if live(n, 0, PAIRS):
                    wait(act, done["Q"], n + 1)
                    wait(act, done["x1"], n - 1)
                    act.activation(q[:, u, :], banks[u][:, :], ACT.Identity).then_inc(done["q"], 1)
                if live(n, 1, PAIRS):
                    wait(act, done["Z0"], n)
                    wait(act, done["x1"], n - 2)
                    act.activation(s0[:, 1 - u, :], banks[3 - u][:, :], ACT.Silu, bias=NB[:, 0:1]).then_inc(done["s0"], 1)
                if live(n, 2, PAIRS):
                    wait(act, done["Z1"], n - 1)
                    wait(act, done["h"], n - 3)
                    act.activation(s1[:, u, :], banks[4 + u][:, :], ACT.Silu, bias=NB[:, 1:2]).then_inc(done["s1"], 1)

        @block.vector
        def _(dve):
            for n, u, i in pipeline(dve, PAIRS, STAGES):
                if live(n, 1, PAIRS):
                    wait(dve, done["s0"], n)
                    wait(dve, done["x2"], n - 2)
                    wait(dve, done["Z1"], n - 2)
                    dve.tensor_tensor(x1[:, 1 - u, :], q[:, 1 - u, :], s0[:, 1 - u, :], ALU.add).then_inc(done["x1"], 1)
                if live(n, 2, PAIRS):
                    wait(dve, done["s1"], n - 1)
                    dve.tensor_tensor(s1[:, u, :], x1[:, u, :], s1[:, u, :], ALU.add).then_inc(done["x2"], 1)
                    wait(dve, done["x2"], n - 1)
                    dve.tensor_tensor(tile_of(H, n - 2), tile_of(H, n - 2), s1[:, u, :], ALU.add).then_inc(done["h"], 1)


X_SCALE, W_SCALE = 256.0, 64.0
G8 = 2 * EXPERTS
KEY_ROWS, KEY_RING = 6 * HD + 3, 4
PART_STORES = 2
SLOTS = [(0, 0, 3), (1, 3, 2), (2, 5, 1)]
LOADED_BEFORE = 2
AV_AT = [7, 11, 13, 14]
P_WO, P_VAR, P_LOGITS = 2, 5, 5
A_Y, A_RD = 3, 7
A_SQ, A_LN, A_HI, A_LOGITS = 1, 9, 3, 9
D_DEN, D_XN = 5, 2
D_FLAT, D_LO = 2, 6


def load_sequence(sp, Q, K, q_parts, k_parts, pair, a, u, loaded):
    for j, slot, k in SLOTS:
        there = slice(slot * HD, (slot + k) * HD)
        sp.dma_start(Q[there, u].rearrange("p h s -> p (h s)"),
                     q_parts[bass.ds(pair, 1), 0:k, a].rearrange("o t d h s -> (o t) d (h s)")).then_inc(loaded, 16)
        sp.dma_start(K[there, u].rearrange("p h s -> p (h s)"),
                     k_parts[bass.ds(pair, 1), j:j + 1, a].rearrange("o t d h s -> (o t) d (h s)").to_broadcast([k, HD, KV * SEQ])).then_inc(loaded, 16)


def project(nc, sem, banks, H, XN, W, VT, q_parts, k_parts, parts_stored, turn, causal, Q, K, q_loaded, V, mask, eye, LG,
            ident, centre, mean, eps_ln, eps_both, vec):
    KR = 2 * KV * HD
    with ExitStack() as ctx:
        def sb(name, shape, dt=F32):
            return ctx.enter_context(nc.sbuf_tensor(name, shape, dt))

        TURN = sb("TURN", [P, 4, SEQ])
        sq, hn = (sb(f"j_{n}", [P, 2, SEQ]) for n in ("sq", "hn"))
        r, r2 = (LG[:, :, :].rearrange("p m g -> p (m g)")[:, k * SEQ:(k + 1) * SEQ] for k in range(2))
        rows = {"q": P, "k": KR}
        cosd = {x: sb(f"j_{x}cos", [rows[x], SEQ]) for x in "qk"}
        sind = {x: sb(f"j_{x}sin", [rows[x], SEQ]) for x in "qk"}
        full = {x: sb(f"j_{x}", [rows[x], 2, SEQ]) for x in "qk"}
        rest = {x: sb(f"j_{x}rest", [rows[x], 2, SEQ]) for x in "qk"}
        part = {x: sb(f"j_{x}part", [rows[x], 2, 3, SEQ], BF16) for x in "qk"}
        names = ["turn", "causal", "setup", "ln1w", "c", "sq", "v", "ln", "r", "xn", "ln2", "r2", "hn", "V", "VT", "qP", "qR", "kPR"]
        names += [f"{x}{n}" for x in "qk" for n in ("cos", "sin", "full", "hi", "rest", "mid", "lo")]
        done = {n: sem(f"proj_{n}") for n in names}
        causal32 = sb("causal32", [P, P])
        bk_c, bk_v, bk_vt, bk_q, bk_qr, bk_k = banks[0:2], banks[2:4], banks[4], banks[5], banks[6], banks[7]
        terms = {"q": ((bk_q[:, :], "qP", TURN[:, 0, :]), (bk_qr[:, :], "qR", TURN[:, 1, :])),
                 "k": ((bk_k[0:KR, :], "kPR", TURN[0:KR, 2, :]), (bk_k[KR:2 * KR, :], "kPR", TURN[KR:2 * KR, 3, :]))}
        parts = {"q": q_parts, "k": k_parts}
        STAGES = 5

        with nc.Block() as block:
            @block.sync
            def _(sp):
                sp.dma_start(TURN[:, :, :], turn).then_inc(done["turn"], 16)
                sp.dma_start(causal32[:, :], causal).then_inc(done["causal"], 16)
                for n, u, i in pipeline(sp, PAIRS, STAGES):
                    if live(n, 4, PAIRS):
                        m = n - 4
                        for x in "qk":
                            to = parts[x]
                            wait(sp, done[f"{x}lo"], m + 1)
                            sp.dma_start(to[bass.ds(m, 1)].rearrange("o t a d h s -> (o a d h) t s"),
                                         part[x][:, u]).then_inc(parts_stored[u], 16)
                    if isinstance(n, int) and n == PAIRS:
                        sp.wait_ge(parts_stored[0], PART_STORES * 16)
                        for a in range(LOADED_BEFORE):
                            load_sequence(sp, Q, K, q_parts, k_parts, 0, a, a, q_loaded[a])

            @block.tensor
            def _(pe):
                pe.wait_ge(done["ln1w"], 3)
                for n, u, i in pipeline(pe, PAIRS, STAGES):
                    if live(n, 1, PAIRS):
                        m, v = n - 1, 1 - u
                        wait(pe, done["sq"], m + 1)
                        wait(pe, done["ln2"], m - 1)
                        pe.matmul(bk_v[v][:, :], mean, sq[:, v, :], start=True, stop=True).then_inc(done["v"], 1)
                    if live(n, 0, PAIRS):
                        wait(pe, done["hn"], n - 1)
                        pe.matmul(bk_c[u][:, :], centre, tile_of(H, n), start=True, stop=True).then_inc(done["c"], 1)
                    if live(n, 2, PAIRS):
                        m = n - 2
                        wait(pe, done["hn"], m + 1)
                        wait(pe, done["qcos"], m)
                        pe.matmul(bk_q[:, :], W[:, W_FQ:W_FQ + P], hn[:, u, :], start=True, stop=True).then_inc(done["qP"], 1)
                        wait(pe, done["qsin"], m)
                        pe.matmul(bk_qr[:, :], W[:, W_FQR:W_FQR + P], hn[:, u, :], start=True, stop=True).then_inc(done["qR"], 1)
                    if live(n, 2, PAIRS):
                        m = n - 2
                        wait(pe, done["ksin"], m)
                        pe.matmul(bk_k[:, :], W[:, W_FK:W_FK + 2 * KR], hn[:, u, :], start=True, stop=True).then_inc(done["kPR"], 1)
                        wait(pe, done["VT"], m)
                        for q in range(BLK):
                            mm = pe.matmul(bk_vt[:, q * KR:(q + 1) * KR], hn[:, u, q * P:(q + 1) * P], W[:, W_FV:W_FV + KR],
                                           start=q == 0, stop=False, skip_group_check=True)
                        mm.then_inc(done["V"], 1)

            @block.scalar
            def _(act):
                act.preload_act_table_set("natural_log_exp_and_others")

                def run(name, to, source, func, **more):
                    act.activation(to, source, func, **more).then_inc(done[name], 1)

                for n, u, i in pipeline(act, PAIRS, STAGES):
                    if live(n, 1, PAIRS):
                        m, v = n - 1, 1 - u
                        wait(act, done["v"], m + 1)
                        wait(act, done["xn"], m)
                        run("ln", r, bk_v[v][:, :], ACT.Ln, bias=eps_ln)
                        wait(act, done["hn"], m)
                        run("ln2", r2, bk_v[v][:, :], ACT.Ln, bias=eps_both, scale=1.0 + EPS_RMS)
                        wait(act, done["ln"], m + 1)
                        run("r", r, r, ACT.Exp, scale=-0.5)
                        wait(act, done["ln2"], m + 1)
                        run("r2", r2, r2, ACT.Exp, scale=-0.5)
                    if live(n, 0, PAIRS):
                        wait(act, done["c"], n + 1)
                        wait(act, done["v"], n - 1)
                        run("sq", sq[:, u, :], bk_c[u][:, :], ACT.Square)
                    if live(n, 4, PAIRS):
                        m = n - 4
                        for x in "qk":
                            wait(act, done[f"{x}rest"], m + 1)
                            run(f"{x}mid", part[x][:, u, 1, :], rest[x][:, u, :], ACT.Identity)
                    if live(n, 3, PAIRS):
                        m, v = n - 3, 1 - u
                        for x in "qk":
                            wait(act, done[f"{x}full"], m + 1)
                            if live(n, 5, PAIRS):
                                wait(act, parts_stored[v], turns(i, u, 5) * PART_STORES * 16)
                            run(f"{x}hi", part[x][:, v, 0, :], full[x][:, v, :], ACT.Identity)
                    if live(n, 2, PAIRS):
                        m = n - 2
                        wait(act, done["V"], m + 1)
                        run("VT", tile_of(VT, m), bk_vt[:, 0:BLK * KR], ACT.Identity)

            @block.gpsimd
            def _(pool):
                pool.memset(V[:, :, :, :, :], 0.0).then_inc(done["setup"], 1)
                pool.wait_ge(done["setup"], 1)
                pool.memset(K[KEY_ROWS - 3:KEY_ROWS, :, :, :], 1.0).then_inc(done["setup"], 1)
                pool.wait_ge(done["setup"], 2)
                pool.memset(V[:, :, :, :, HD:HD + 1], 1.0).then_inc(done["setup"], 1)
                pool.tensor_copy(eye[:, :], ident).then_inc(done["setup"], 1)
                pool.wait_ge(done["causal"], 16)
                pool.tensor_copy(mask[:, :], causal32[:, :]).then_inc(done["setup"], 1)
                for n, u, i in pipeline(pool, PAIRS, STAGES):
                    for x in "qk":
                        if live(n, 4, PAIRS):
                            m = n - 4
                            wait(pool, done[f"{x}mid"], m + 1)
                            pool.tensor_tensor(part[x][:, u, 2, :], rest[x][:, u, :], part[x][:, u, 1, :], ALU.subtract).then_inc(done[f"{x}lo"], 1)
                    for x in "qk":
                        if live(n, 2, PAIRS):
                            m = n - 2
                            wait(pool, done[f"{x}sin"], m + 1)
                            wait(pool, done[f"{x}cos"], m + 1)
                            wait(pool, done[f"{x}rest"], m - 1)
                            pool.tensor_tensor(full[x][:, u, :], cosd[x][:, :], sind[x][:, :], ALU.add).then_inc(done[f"{x}full"], 1)

            @block.vector
            def _(dve):
                dve.tensor_scalar(W[:, W_FQ:W_01], W[:, W_FQ:W_01], vec(V_LN1), None, ALU.mult).then_inc(done["ln1w"], 1)
                dve.tensor_scalar(W[:, W_FK:W_O], W[:, W_FK:W_O], vec(V_LN1), None, ALU.mult).then_inc(done["ln1w"], 1)
                dve.tensor_scalar(W[:, W_ROUTE:W_ROUTE + G8], W[:, W_ROUTE:W_ROUTE + G8], vec(V_LN2), None, ALU.mult).then_inc(done["ln1w"], 1)
                dve.wait_ge(done["turn"], 16)
                for n, u, i in pipeline(dve, PAIRS, STAGES):
                    if live(n, 1, PAIRS):
                        m, v = n - 1, 1 - u
                        wait(dve, done["r"], m + 1)
                        dve.tensor_tensor(tile_of(XN, m), bk_c[v][:, :], r, ALU.mult).then_inc(done["xn"], 1)
                        wait(dve, done["r2"], m + 1)
                        wait(dve, done["V"], m - 1)
                        dve.tensor_tensor(hn[:, v, :], bk_c[v][:, :], r2, ALU.mult).then_inc(done["hn"], 1)
                    if live(n, 2, PAIRS):
                        m = n - 2
                        for x in "qk":
                            wait(dve, done[f"{x}full"], m)
                            for (source, name, table), term, to in zip(terms[x], ("cos", "sin"), (cosd, sind)):
                                wait(dve, done[name], m + 1)
                                dve.tensor_tensor(to[x][:, :], source, table, ALU.mult).then_inc(done[f"{x}{term}"], 1)
                    if live(n, 3, PAIRS):
                        m, v = n - 3, 1 - u
                        for x in "qk":
                            wait(dve, done[f"{x}lo"], m - 1)
                            wait(dve, done[f"{x}hi"], m + 1)
                            dve.tensor_tensor(rest[x][:, v, :], full[x][:, v, :], part[x][:, v, 0, :], ALU.subtract).then_inc(done[f"{x}rest"], 1)


def score_units(order):
    units = []
    for b in order:
        w = SEQ - P * b
        heads = min(HEADS, SEQ // w)
        units += [(b, h, heads, w) for h in range(0, HEADS, heads)]
    return units


def attend(nc, sem, banks, H, XN, W, VT, q_parts, k_parts, parts_stored, Q, K, q_loaded, V, mask, eye, FS, LG, fhi, flo, stacked,
           ident, mean, eps_rms):
    RING = KEY_RING
    UNITS = score_units(range(BLK))
    NU = len(UNITS)
    SROWS = 6 * HD
    STAGES = 10
    with ExitStack() as ctx:
        def sb(name, shape, dt=F32):
            return ctx.enter_context(nc.sbuf_tensor(name, shape, dt))

        negmax = sb("negmax", [P, 2, HEADS * BLK])
        nm = sb("nm", [HEADS * BLK, 2, 3, P], BF16)
        nraw = sb("nraw", [HEADS * BLK, P])
        nrest = sb("nrest", [HEADS * BLK, P])
        E = sb("t_e", [P, HEADS * TRAP])
        Y = sb("t_y", [P, SEQ])
        den = sb("den", [P, SEQ])
        lnd = sb("lnd", [P, SEQ])
        rd = sb("rd", [P, SEQ])
        yn = sb("yn", [P, 2, SEQ])
        names = ("sp_seen", "pool_seen", "dve_seen", "S", "max", "turned", "nraw", "nhi", "nrest", "nmid", "nlo", "T", "exp", "masked", "V",
                 "av", "Y", "den", "lnd", "rd", "yn", "wo", "xn", "h", "sq", "v", "ln", "r", "flat", "L", "logits", "fhi", "flo")
        done = {n: sem(f"att_{n}") for n in names}
        sq, ln2, r2, flat = (sb(f"g_{n}", [P, SEQ]) for n in ("sq", "ln", "r", "flat"))
        nm_loaded = [sem(f"nm_loaded{u}") for u in range(RING)]
        bk_s, bk_t, bk_av, bk_o = banks[0:3], banks[3:6], banks[6], banks[7]
        NS, NT = len(bk_s), len(bk_t)

        def pair_of(i, u, stage):
            return RING // 2 * i + (u - stage) // 2

        def routing(n, u, stage):
            return live(n, stage, ROWS) and (u - stage) % 2 == 0

        def e_block(b):
            return E[:, HEADS * START[b]:HEADS * (START[b] + WIDTH[b])].rearrange("p (h w) -> p h w", h=HEADS)

        with nc.Block() as block:
            @block.sync
            def _(sp):
                for n, u, i in pipeline(sp, ROWS, STAGES, RING):
                    if live(n, 0, ROWS) and not (isinstance(n, int) and n < LOADED_BEFORE):
                        pair, a = RING // 2 * i + u // 2, u % 2
                        sp.wait_ge(parts_stored[u // 2], (i + 1) * PART_STORES * 16)
                        sp.sem_inc(done["sp_seen"], 1)
                        wait(sp, done["T"], (n - RING + 1) * NU)
                        load_sequence(sp, Q, K, q_parts, k_parts, pair, a, u, q_loaded[u])
                    if live(n, 2, ROWS):
                        m, g = n - 2, (u - 2) % RING
                        wait(sp, done["nlo"], m + 1)
                        for part in range(3):
                            sp.dma_start(Q[SROWS + part:SROWS + part + 1, g].rearrange("o h s -> o (h s)"),
                                         nm[:, u % 2, part, :]).then_inc(nm_loaded[g], 16)
                    if routing(n, u, 9):
                        p, v = pair_of(i, u, 9), (u - 9) // 2 % 2
                        wait(sp, done["flo"], p + 1)
                        for a in range(2):
                            for j, piece in enumerate((fhi, flo)):
                                sp.dma_start(FS[j * D:(j + 1) * D, bass.ds(2 * p + a, 1), :].rearrange("p a s -> p (a s)"),
                                             piece[a * D:(a + 1) * D, v, :]).then_inc(stacked[v], 16)

            @block.gpsimd
            def _(pool):
                def select(n, u, c):
                    m = n - 3
                    wait(pool, done["exp"], m * NU + sum(b <= c for b, *_ in UNITS))
                    pool.sem_inc(done["pool_seen"], 1)
                    pool.affine_select(e_block(c)[:, :, 0:P], e_block(c)[:, :, 0:P], [[0, HEADS], [1, P]],
                                       ALU.is_ge, 0.0, base=0, channel_multiplier=-1).then_inc(done["masked"], 1)

                def values(n, u, i):
                    m, a = n - 3, (u - 3) % 2
                    pair = RING // 2 * i + (u - 3) // 2
                    wait(pool, done["av"], (m - 1) * BLK)
                    pool.sem_inc(done["pool_seen"], 1)
                    src = tile_of(VT, pair).rearrange("p (q a k d) -> p q a k d", q=BLK, a=2, k=KV)[:, :, a]
                    pool.tensor_copy(V[:, a, :, :, 0:HD], src).then_inc(done["V"], 1)

                def split(n, u, i):
                    m = n - 2
                    wait(pool, done["nraw"], m + 1)
                    if live(n, 4, ROWS):
                        g = (u - 4) % RING
                        pool.wait_ge(nm_loaded[g], turns(i, u, 4, RING) * 48)
                    pool.sem_inc(done["pool_seen"], 1)
                    pool.tensor_copy(nm[:, u % 2, 0, :], nraw[:, :]).then_inc(done["nhi"], 1)
                    wait(pool, done["nhi"], m + 1)
                    pool.tensor_tensor(nrest[:, :], nraw[:, :], nm[:, u % 2, 0, :], ALU.subtract).then_inc(done["nrest"], 1)
                    wait(pool, done["nrest"], m + 1)
                    pool.sem_inc(done["pool_seen"], 1)
                    pool.tensor_copy(nm[:, u % 2, 1, :], nrest[:, :]).then_inc(done["nmid"], 1)
                    wait(pool, done["nmid"], m + 1)
                    pool.tensor_tensor(nm[:, u % 2, 2, :], nrest[:, :], nm[:, u % 2, 1, :], ALU.subtract).then_inc(done["nlo"], 1)

                def residual(n, u, i):
                    pair = RING // 2 * i + (u - 5) // 2
                    wait(pool, done["xn"], pair + 1)
                    pool.tensor_tensor(tile_of(H, pair), tile_of(H, pair), tile_of(XN, pair), ALU.add).then_inc(done["h"], 1)

                def normalise(n, u, i):
                    m, a = n - 4, u % 2
                    wait(pool, done["rd"], m + 1)
                    wait(pool, done["wo"], (m - a) // 2 if isinstance(m, int) else RING // 2 * i + (u - 4 - a) // 2)
                    pool.tensor_tensor(yn[:, a, :], Y[:, :], rd[:, :], ALU.mult).then_inc(done["yn"], 1)

                for n, u, i in pipeline(pool, ROWS, STAGES, RING):
                    three, four = live(n, 3, ROWS), live(n, 4, ROWS)
                    if three:
                        values(n, u, i)
                    if live(n, 2, ROWS):
                        split(n, u, i)
                    if three:
                        select(n, u, 0)
                    if live(n, 5, ROWS) and u % 2 == 0:
                        residual(n, u, i)
                    if three:
                        select(n, u, 1)
                    if four:
                        normalise(n, u, i)
                    if three:
                        select(n, u, 2)
                        select(n, u, 3)

            @block.vector
            def _(dve):
                for n, u, i in pipeline(dve, ROWS, STAGES, RING):
                    if live(n, 2, ROWS):
                        m = n - 2
                        wait(dve, done["turned"], m + 1)
                        wait(dve, done["nrest"], m)
                        dve.tensor_copy(nraw[:, :], bk_o[0:HEADS * BLK, 0:P]).then_inc(done["nraw"], 1)
                    for t, (c, h, heads, w) in enumerate(UNITS):
                        if live(n, 1, ROWS):
                            m = n - 1
                            wait(dve, done["S"], m * NU + t + 1)
                            if t == 0:
                                wait(dve, done["turned"], m - 1)
                            j = BLK - 1 - c
                            to = negmax[:, (u - 1) % 2, :].rearrange("p (h j) -> p h j", j=BLK)[:, h:h + heads, j]
                            dve.tensor_reduce(to, bk_s[t % NS][:, 0:heads * w].rearrange("p (h s) -> p h s", h=heads),
                                              AX_X, ALU.max, negate=True).then_inc(done["max"], 1)
                        if t == D_FLAT and routing(n, u, 8):
                            p = pair_of(i, u, 8)
                            wait(dve, done["r"], p + 1)
                            wait(dve, done["L"], p)
                            wait(dve, done["flo"], p)
                            dve.tensor_tensor(flat[:, :], tile_of(XN, p), r2[:, :], ALU.mult).then_inc(done["flat"], 1)
                        if t == D_LO and routing(n, u, 8):
                            p, v = pair_of(i, u, 8), (u - 8) // 2 % 2
                            wait(dve, done["fhi"], p + 1)
                            dve.scalar_tensor_tensor(flo[:, v, :], flat[:, :], X_SCALE, fhi[:, v, :], ALU.mult, ALU.subtract).then_inc(done["flo"], 1)
                        if t == D_DEN and live(n, 4, ROWS):
                            m = n - 4
                            wait(dve, done["lnd"], m)
                            wait(dve, done["Y"], m + 1)
                            dve.sem_inc(done["dve_seen"], 1)
                            dve.stream_shuffle(den[:, :], Y[:, :], [HD] * 32).then_inc(done["den"], 1)
                        if t == D_XN and live(n, 5, ROWS) and u % 2 == 0:
                            pair = RING // 2 * i + (u - 5) // 2
                            wait(dve, done["wo"], pair + 1)
                            dve.tensor_tensor(tile_of(XN, pair), tile_of(XN, pair), bk_o[:, :], ALU.add).then_inc(done["xn"], 1)

            @block.tensor
            def _(pe):
                def last_turn(t, ring):
                    return (NU - 1 - t) % ring

                def s_unit(m, g, t):
                    c, h, heads, w = UNITS[t]
                    j = BLK - 1 - c
                    wait(pe, done["max"], m * NU + t - NS + 1 if t >= NS else m * NU - last_turn(t, NS))
                    for x in range(heads):
                        pe.matmul(bk_s[t % NS][:, x * w:(x + 1) * w], Q[0:SROWS, g, h + x, j * P:(j + 1) * P],
                                  K[0:SROWS, g, (h + x) // KV, 0:w], start=x == 0, stop=False, skip_group_check=True)
                    for x in range(heads):
                        mm = pe.matmul(bk_s[t % NS][:, (x + 1) * w - P:(x + 1) * w], mask[:, :], eye[:, :],
                                       start=False, stop=False, skip_group_check=True)
                    mm.then_inc(done["S"], 1)

                def t_unit(m, g, t):
                    c, h, heads, w = UNITS[t]
                    wait(pe, done["exp"], m * NU + t - NT + 1 if t >= NT else m * NU - last_turn(t, NT))
                    for x in range(heads):
                        mm = pe.matmul(bk_t[t % NT][:, x * w:(x + 1) * w], K[:, g, (h + x) // KV, c * P:(c + 1) * P],
                                       Q[:, g, h + x, c * P:], start=x == 0, stop=False, skip_group_check=True)
                    mm.then_inc(done["T"], 1)

                def values(m, a, c):
                    wait(pe, done["masked"], m * BLK + c + 1)
                    if c == 0:
                        wait(pe, done["V"], m + 1)
                        wait(pe, done["Y"], m)
                    for h in range(HEADS):
                        mm = pe.matmul(bk_av[32 * h:32 * h + 32, c * P:], V[:, a, c, h // KV, :], e_block(c)[:, h],
                                       start=c == 0, stop=False, skip_group_check=True)
                    mm.then_inc(done["av"], 1)

                for n, u, i in pipeline(pe, ROWS, STAGES, RING):
                    s_live, t_live, f_live = live(n, 1, ROWS), live(n, 3, ROWS), live(n, 4, ROWS)
                    if s_live:
                        g = (u - 1) % RING
                        pe.wait_ge(q_loaded[g], turns(i, u, 1, RING) * 2 * len(SLOTS) * 16)
                    if t_live:
                        g = (u - 3) % RING
                        pe.wait_ge(nm_loaded[g], turns(i, u, 3, RING) * 48)
                    for t in range(NU):
                        if s_live:
                            s_unit(n - 1, (u - 1) % RING, t)
                        if t_live:
                            t_unit(n - 3, (u - 3) % RING, t)
                        if t == 0 and live(n, 2, ROWS):
                            m = n - 2
                            wait(pe, done["max"], (m + 1) * NU)
                            wait(pe, done["xn"], (n - 5) // 2 if isinstance(n, int) else RING // 2 * i + (u - 5) // 2)
                            wait(pe, done["nraw"], m)
                            wait(pe, done["ln"], (n - 6) // 2 if isinstance(n, int) else pair_of(i, u, 6))
                            wait(pe, done["logits"], (n - 7) // 2 if isinstance(n, int) else pair_of(i, u, 7))
                            pe.transpose(bk_o[0:HEADS * BLK, 0:P], negmax[:, u % 2, :], ident).then_inc(done["turned"], 1)
                        if f_live:
                            m, a = n - 4, u % 2
                            for c in range(BLK):
                                if AV_AT[c] == t + NU:
                                    values(m, a, c)
                        if t == P_WO and live(n, 5, ROWS) and u % 2 == 0:
                            pair = RING // 2 * i + (u - 5) // 2
                            wait(pe, done["yn"], n - 5 + 1)
                            wait(pe, done["nraw"], min(n - 1, ROWS) if isinstance(n, int) else n - 1)
                            wait(pe, done["ln"], pair)
                            wait(pe, done["logits"], pair - 1)
                            for a in range(2):
                                mm = pe.matmul(bk_o[a * D:(a + 1) * D, :], W[:, W_O:W_O + D], yn[:, a, :],
                                               start=True, stop=False, skip_group_check=True)
                            mm.then_inc(done["wo"], 1)
                        if t == P_VAR and routing(n, u, 7):
                            p = pair_of(i, u, 7)
                            wait(pe, done["sq"], p + 1)
                            wait(pe, done["nraw"], min(n - 1, ROWS) if isinstance(n, int) else n - 1)
                            wait(pe, done["logits"], p)
                            pe.matmul(bk_o[:, :], mean, sq[:, :], start=True, stop=True).then_inc(done["v"], 1)
                        if t == P_LOGITS and routing(n, u, 8):
                            p = pair_of(i, u, 8)
                            wait(pe, done["flat"], p + 1)
                            wait(pe, done["xn"], min(p + 2, PAIRS) if isinstance(n, int) else p + 2)
                            for q in range(BLK):
                                mm = pe.matmul(bk_o[:, q * G8:(q + 1) * G8], flat[:, q * P:(q + 1) * P], W[:, W_ROUTE:W_ROUTE + G8],
                                               start=q == 0, stop=False, skip_group_check=True)
                            mm.then_inc(done["L"], 1)
                        if t_live:
                            m, a = n - 3, (u - 3) % 2
                            for c in range(BLK):
                                if AV_AT[c] == t:
                                    values(m, a, c)

            @block.scalar
            def _(act):
                def run(name, to, source, func, **more):
                    act.activation(to, source, func, **more).then_inc(done[name], 1)

                for n, u, i in pipeline(act, ROWS, STAGES, RING):
                    for t, (c, h, heads, w) in enumerate(UNITS):
                        if live(n, 3, ROWS):
                            m = n - 3
                            wait(act, done["T"], m * NU + t + 1)
                            wait(act, done["av"], (m - 1) * BLK + c + 1)
                            at = HEADS * START[c] + h * w
                            run("exp", E[:, at:at + heads * w], bk_t[t % NT][:, 0:heads * w], ACT.Exp)
                        if live(n, 4, ROWS):
                            m = n - 4
                            if t == A_Y:
                                wait(act, done["av"], (m + 1) * BLK)
                                wait(act, done["yn"], m)
                                run("Y", Y[:, :], bk_av[:, :], ACT.Identity)
                            if t == A_RD:
                                wait(act, done["den"], m + 1)
                                wait(act, done["rd"], m)
                                run("lnd", lnd[:, :], den[:, :], ACT.Ln)
                                wait(act, done["lnd"], m + 1)
                                wait(act, done["yn"], m)
                                run("rd", rd[:, :], lnd[:, :], ACT.Exp, scale=-1.0)
                        if t == A_SQ and routing(n, u, 7):
                            p = pair_of(i, u, 7)
                            wait(act, done["xn"], p + 1)
                            wait(act, done["v"], p)
                            run("sq", sq[:, :], tile_of(XN, p), ACT.Square)
                        if t == A_LN and routing(n, u, 7):
                            p = pair_of(i, u, 7)
                            wait(act, done["v"], p + 1)
                            wait(act, done["r"], p)
                            run("ln", ln2[:, :], bk_o[:, :], ACT.Ln, bias=eps_rms)
                            wait(act, done["ln"], p + 1)
                            wait(act, done["flat"], p)
                            run("r", r2[:, :], ln2[:, :], ACT.Exp, scale=-0.5)
                        if t == A_HI and routing(n, u, 8):
                            p, v = pair_of(i, u, 8), (u - 8) // 2 % 2
                            wait(act, done["flat"], p + 1)
                            if live(n, 12, ROWS):
                                act.wait_ge(stacked[v], (p // 2 if isinstance(n, int) else i + (u - 8) // 4) * 64)
                            run("fhi", fhi[:, v, :], flat[:, :], ACT.Identity, scale=X_SCALE)
                        if t == A_LOGITS and routing(n, u, 8):
                            p = pair_of(i, u, 8)
                            wait(act, done["L"], p + 1)
                            run("logits", tile_of(LG, p), bk_o[:, 0:BLK * G8], ACT.Identity)


def route(nc, sem, banks, XN, LG, CST, gates, gateT, w13, w2, whi, wlo, v2hi, v2lo, ident, vec):
    TOKENS = PAIRS * BLK * 2
    with ExitStack() as ctx:
        def sb(name, shape, dt=F32):
            return ctx.enter_context(nc.sbuf_tensor(name, shape, dt))

        prob, first, second, spare = (sb(f"g_{n}", [P, TOKENS, EXPERTS]) for n in ("prob", "first", "second", "spare"))
        most, total, top1, top2 = (sb(f"g_{n}", [P, TOKENS]) for n in ("most", "total", "top1", "top2"))
        gate = sb("g_gate", [P, PAIRS, 2, EXPERTS, BLK])
        chain = [sem(f"chain_g{h}") for h in range(2)]
        less_ready, exp_ready, gate_ready = sem("less_ready"), sem("exp_ready"), sem("gate_ready")
        gate_turned, gateT_ready, gates_stored = sem("gate_turned"), sem("gateT_ready"), sem("gates_stored")
        logits = LG[:, :, :].rearrange("p m (g e) -> p (m g) e", e=EXPERTS)
        HALF = TOKENS // 2
        halves = [slice(h * HALF, (h + 1) * HALF) for h in range(2)]

        def each(t, h):
            return t[:, halves[h]].unsqueeze(2).to_broadcast([P, HALF, EXPERTS])

        COLS = 2 * EXPERTS * HID
        raw = XN[:, :, :].rearrange("p m s -> p (m s)")
        w13raw, w2raw = raw[:, 0:COLS], raw[:, COLS:COLS + 2 * EXPERTS * D]
        v2hi_, v2lo_ = (v[:, :, :].rearrange("p j d -> p (j d)") for v in (v2hi, v2lo))
        w13_loaded, w2_loaded, scaled, high, low = (sem(n) for n in ("w13_loaded", "w2_loaded", "w_scaled", "w_high", "w_low"))

        with nc.Block() as block:
            @block.gpsimd
            def _(pool):
                pool.wait_ge(w13_loaded, 32)
                pool.tensor_scalar(w13raw, w13raw, vec(V_LN2), W_SCALE, ALU.mult, ALU.mult).then_inc(scaled, 1)
                pool.wait_ge(w2_loaded, 16)
                pool.tensor_scalar(w2raw, w2raw, W_SCALE, None, ALU.mult).then_inc(scaled, 1)
                pool.wait_ge(high, 1)
                pool.tensor_tensor(wlo[:, :], w13raw, whi[:, :], ALU.subtract).then_inc(low, 1)
                pool.wait_ge(high, 2)
                pool.tensor_tensor(v2lo_, w2raw, v2hi_, ALU.subtract).then_inc(low, 1)

            @block.vector
            def _(dve):
                count = [0]

                def both(step):
                    for h, half in enumerate(halves):
                        if count[0]:
                            dve.wait_ge(chain[h], count[0])
                        step(h, half).then_inc(chain[h], 1)
                    count[0] += 1

                rank = CST[:, C_RANK:C_RANK + EXPERTS].unsqueeze(1).to_broadcast([P, HALF, EXPERTS])

                def reduce(to, source, op):
                    both(lambda h, half: dve.tensor_reduce(to[:, half], source[:, half], AX_X, op))

                def combine(to, one, two, op):
                    both(lambda h, half: dve.tensor_tensor(to[:, half], one[:, half], two(h, half), op))

                def pick(chosen, source, best):
                    reduce(best, source, ALU.max)
                    combine(chosen, source, lambda h, half: each(best, h), ALU.is_equal)
                    combine(chosen, chosen, lambda h, half: rank, ALU.mult)
                    reduce(most, chosen, ALU.max)
                    combine(chosen, chosen, lambda h, half: each(most, h), ALU.is_equal)

                reduce(most, logits, ALU.max)
                for h, half in enumerate(halves):
                    dve.wait_ge(chain[h], count[0])
                    dve.tensor_tensor(prob[:, half], logits[:, half], each(most, h), ALU.subtract).then_inc(less_ready, 1)
                for h, half in enumerate(halves):
                    dve.wait_ge(exp_ready, h + 1)
                    dve.tensor_reduce(total[:, half], prob[:, half], AX_X, ALU.add).then_inc(chain[h], 1)
                count[0] += 1
                both(lambda h, half: dve.reciprocal(total[:, half], total[:, half]))
                combine(prob, prob, lambda h, half: each(total, h), ALU.mult)
                pick(first, prob, top1)
                both(lambda h, half: dve.scalar_tensor_tensor(spare[:, half], first[:, half], -2.0, prob[:, half], ALU.mult, ALU.add))
                pick(second, spare, top2)
                combine(first, first, lambda h, half: second[:, half], ALU.add)
                combine(first, first, lambda h, half: prob[:, half], ALU.mult)
                combine(total, top1, lambda h, half: top2[:, half], ALU.add)
                both(lambda h, half: dve.tensor_scalar(total[:, half], total[:, half], 1e-9, None, ALU.add))
                both(lambda h, half: dve.reciprocal(total[:, half], total[:, half]))
                for h in range(2):
                    dve.wait_ge(chain[h], count[0])
                whole = total[:, :].unsqueeze(2).to_broadcast([P, TOKENS, EXPERTS])
                for q in range(BLK):
                    chosen = first[:, :, :].rearrange("p (m q a) e -> p q m a e", q=BLK, a=2)[:, q]
                    by = whole.rearrange("p (m q a) e -> p q m a e", q=BLK, a=2)[:, q]
                    for a in range(2):
                        dve.tensor_tensor(gate[:, :, a, :, q], chosen[:, :, a], by[:, :, a], ALU.mult).then_inc(gate_ready, 1)
                for half in range(2):
                    dve.wait_ge(gate_turned, (half + 1) * BLK)
                    dve.tensor_scalar(gateT[:, half].rearrange("p b t -> p (b t)"), banks[half][:, :],
                                      1.0 / (W_SCALE * HH_SCALE), None, ALU.mult).then_inc(gateT_ready, 1)

            @block.scalar
            def _(act):
                for h, half in enumerate(halves):
                    act.wait_ge(less_ready, h + 1)
                    act.activation(prob[:, half], prob[:, half], ACT.Exp).then_inc(exp_ready, 1)
                act.wait_ge(scaled, 1)
                act.activation(whi[:, :], w13raw, ACT.Identity).then_inc(high, 1)
                act.wait_ge(scaled, 2)
                act.activation(v2hi_, w2raw, ACT.Identity).then_inc(high, 1)
                act.preload_act_table_set("silu_and_others")

            @block.tensor
            def _(pe):
                pe.wait_ge(gate_ready, 2 * BLK)
                cols = gate[:, :, :, :, :].rearrange("p m a e q -> p (m a e q)")
                for b in range(2 * BLK):
                    pe.transpose(banks[b // BLK][:, b % BLK * P:(b % BLK + 1) * P], cols[:, b * P:(b + 1) * P], ident).then_inc(gate_turned, 1)

            @block.sync
            def _(sp):
                for a in range(2):
                    sp.dma_start(w13raw[a * D:(a + 1) * D, :], w13.rearrange("d j h -> d (j h)")).then_inc(w13_loaded, 16)
                sp.dma_start(w2raw, w2.rearrange("p j d -> p (j d)")).then_inc(w2_loaded, 16)
                sp.wait_ge(gateT_ready, 2)
                flat_gates = gates.rearrange("m a e (q t) -> (m a e q) t", t=P)
                sp.dma_start(flat_gates.rearrange("(b r) t -> r b t", r=P), gateT[:, :, :, :].rearrange("p h b t -> p (h b) t")).then_inc(gates_stored, 16)
    return gates_stored


GROUPS = [(0, 3), (3, 3), (6, 2)]
CHUNKS = [[(c, min(P, k * HID - c)) for c in range(0, k * HID, P)] for _, k in GROUPS]
TILES = [2 * len(c) for c in CHUNKS]
TILE_AT = [sum(TILES[:x]) for x in range(len(GROUPS))]
PAIR_TILES = sum(TILES)
TILE_ROWS = [rows for c in CHUNKS for _, rows in c for a in range(2)]
EXPERTS_UPTO = [first + k for (first, k), tiles in zip(GROUPS, TILES) for t in range(tiles)]
BANK_BEFORE = [6, 7, 5, 0, 1, 2, 3, 4]
HH_SCALE = 4.0
MORE_POOL = (6, 10)
HI_LAG, LO_LAG = 1, 1
OUT_AT = [1, 4, 5]
GATE_AT = [3, 4, 7]
ACC_AT = [4, 5, 7]


def experts(nc, sem, banks, H, XN, FS, stacked, gates, gates_stored, whi, wlo, v2hi, v2lo, out, ident):
    RING = len(GROUPS)
    UNITS = PAIRS * RING
    DOWN = 1.0 / (X_SCALE * W_SCALE)
    SLOTS = PAIR_TILES // 2
    with ExitStack() as ctx:
        def sb(name, shape, dt=F32):
            return ctx.enter_context(nc.sbuf_tensor(name, shape, dt))

        gate = sb("x_gate", [P, EXPERTS, SEQ])
        s = sb("x_s", [P, 2, SEQ])
        hhi, hlo = sb("hhi", [P, PAIR_TILES, SEQ], F16), sb("hlo", [P, PAIR_TILES, SEQ], F16)
        part = sb("x_part", [P, 3, SEQ])
        acc = sb("x_acc", [P, SEQ])
        outsb = sb("outsb", [P, SEQ])
        names = ("H1", "H3", "s", "hh", "hi", "lo_d", "lo_p", "O", "part", "acc", "turned", "out")
        done = {n: sem(f"moe_{n}") for n in names}
        gate_loaded = [sem(f"gate_loaded{u}") for u in range(RING)]
        stored = sem("stored")
        bk_h1, bk_h3, bk_o, bk_t = banks[0:2], banks[2:4], banks[4:7], banks[7]
        out_v = out.rearrange("r (q p) f -> r p q f", p=P)
        by_pool = [t % 2 == 1 or t in MORE_POOL for t in range(PAIR_TILES)]
        engine_of = ["lo_p" if x else "lo_d" for x in by_pool]
        total = {n: engine_of.count(n) for n in ("lo_p", "lo_d")}

        def formed(name, pair, t):
            return pair * total[name] + engine_of[:t].count(name)

        STAGES = 3

        def unit(i, u, stage):
            return i + (u - stage) // RING, (u - stage) % RING

        def split_tile(pair, t):
            return (pair, t) if t >= 0 else (pair - 1, t + PAIR_TILES)

        def begun(pair, t):
            return not isinstance(pair, int) or pair * PAIR_TILES + t >= 0

        def low(eng, pair, t, name):
            if not begun(pair, t):
                return
            pair, t = split_tile(pair, t)
            if engine_of[t] != name:
                return
            rows = TILE_ROWS[t]
            wait(eng, done["hi"], pair * PAIR_TILES + t + 1)
            eng.tensor_tensor(hlo[0:rows, t, :], XN[0:rows, t % SLOTS, :], hhi[0:rows, t, :], ALU.subtract).then_inc(done[name], 1)

        with nc.Block() as block:
            @block.sync
            def _(sp):
                sp.wait_ge(gates_stored, 16)
                for n, u, i in pipeline(sp, UNITS, STAGES, RING, 2 * RING):
                    if live(n, 0, UNITS):
                        first, k = GROUPS[u]
                        wait(sp, done["part"], (i - 1) * EXPERTS + first + k)
                        for a in range(2):
                            src = gates[bass.ds(i, 1), a, first:first + k, :].rearrange("o e s -> (o e) s").partition_broadcast(D)
                            sp.dma_start(gate[a * D:(a + 1) * D, first:first + k], src).then_inc(gate_loaded[u], 16)
                    if live(n, 2, UNITS) and u == 1:
                        pair = i - 1
                        wait(sp, done["out"], pair + 1)
                        for a in range(2):
                            sp.dma_start(out_v[bass.ds(2 * pair + a, 1)].rearrange("o p q f -> (o p) q f"),
                                         outsb[:, :].rearrange("p (q a f) -> p q a f", q=BLK, a=2)[:, :, a]).then_inc(stored, 16)
                sp.wait_ge(stored, ROWS * 16)

            @block.tensor
            def _(pe):
                for v in range(2):
                    pe.wait_ge(stacked[v], PAIRS // 2 * 64)

                def hidden(i, u, t):
                    (at, rows), a = CHUNKS[u][t // 2], t % 2
                    k = i * PAIR_TILES + TILE_AT[u] + t
                    for bank, name, layer, reader in ((bk_h1, "H1", 0, "s"), (bk_h3, "H3", 1, "hh")):
                        wait(pe, done[reader], k - 1)
                        cols = slice((layer * EXPERTS + GROUPS[u][0]) * HID + at, (layer * EXPERTS + GROUPS[u][0]) * HID + at + rows)
                        x = tile_of(FS, 2 * i + a)
                        pe.matmul(bank[t % 2][0:rows, :], whi[:, cols], x, start=True, stop=False)
                        pe.matmul(bank[t % 2][0:rows, :], wlo[:, cols], x, start=False, stop=True).then_inc(done[name], 1)

                def output(pair, x, j):
                    last = TILE_AT[x] + 2 * (j + 2)
                    wait(pe, done["hi"], pair * PAIR_TILES + last)
                    wait(pe, done["lo_d"], formed("lo_d", pair, last))
                    wait(pe, done["lo_p"], formed("lo_p", pair, last))
                    e = GROUPS[x][0] + j
                    wait(pe, done["part"], (pair if x else pair - 1) * EXPERTS + (BANK_BEFORE[e] + 1))
                    for c in range(j, j + 2):
                        rows = CHUNKS[x][c][1]
                        for z, (w, h) in enumerate(((v2hi, hhi), (v2lo, hhi), (v2hi, hlo))):
                            for a in range(2):
                                mm = pe.matmul(bk_o[j][a * D:(a + 1) * D, :], w[0:rows, 2 * e + c - j, :],
                                               h[0:rows, TILE_AT[x] + 2 * c + a, :], start=c == j and z == 0,
                                               stop=c == j + 1 and z == 2, skip_group_check=True)
                    mm.then_inc(done["O"], 1)

                for n, u, i in pipeline(pe, UNITS, STAGES, RING, 2 * RING):
                    for t in range(max(TILES)):
                        if live(n, 0, UNITS) and t < TILES[u]:
                            hidden(i, u, t)
                        if live(n, 1, UNITS):
                            pair, x = unit(i, u, 1)
                            for j in range(GROUPS[x][1]):
                                if OUT_AT[j] == t:
                                    output(pair, x, j)
                        if live(n, 2, UNITS) and u == 1 and t == 3:
                            pair = i - 1
                            wait(pe, done["acc"], (pair + 1) * EXPERTS)
                            wait(pe, done["out"], pair)
                            for q in range(BLK):
                                mm = pe.transpose(bk_t[:, q * P:(q + 1) * P], acc[:, q * P:(q + 1) * P], ident)
                            mm.then_inc(done["turned"], 1)

            @block.scalar
            def _(act):
                def high(pair, t):
                    if not begun(pair, t):
                        return
                    pair, t = split_tile(pair, t)
                    rows = TILE_ROWS[t]
                    wait(act, done["hh"], pair * PAIR_TILES + t + 1)
                    wait(act, done["O"], (pair - 1) * EXPERTS + EXPERTS_UPTO[t])
                    act.activation(hhi[0:rows, t, :], XN[0:rows, t % SLOTS, :], ACT.Identity).then_inc(done["hi"], 1)

                for n, u, i in pipeline(act, UNITS, STAGES, RING, 2 * RING):
                    if live(n, 0, UNITS):
                        for t in range(TILES[u]):
                            at = TILE_AT[u] + t
                            wait(act, done["H1"], i * PAIR_TILES + at + 1)
                            wait(act, done["hh"], i * PAIR_TILES + at - 1)
                            rows = TILE_ROWS[at]
                            act.activation(s[0:rows, t % 2, :], bk_h1[t % 2][0:rows, :], ACT.Silu, scale=DOWN).then_inc(done["s"], 1)
                            high(i, at - HI_LAG)
                    if isinstance(n, int) and n == UNITS:
                        for t in range(PAIR_TILES - HI_LAG, PAIR_TILES):
                            high(PAIRS - 1, t)
                    if live(n, 2, UNITS) and u == 1:
                        pair = i - 1
                        wait(act, done["turned"], pair + 1)
                        wait(act, stored, pair * 32)
                        act.activation(outsb[:, :], bk_t[:, :], ACT.Identity).then_inc(done["out"], 1)

            @block.gpsimd
            def _(pool):
                for n, u, i in pipeline(pool, UNITS, STAGES, RING, 2 * RING):
                    for t in range(max(TILES)):
                        if live(n, 0, UNITS) and t < TILES[u]:
                            low(pool, i, TILE_AT[u] + t - LO_LAG, "lo_p")
                        if isinstance(n, int) and n == UNITS and t == 0:
                            for x in range(PAIR_TILES - LO_LAG, PAIR_TILES):
                                low(pool, PAIRS - 1, x, "lo_p")
                        if live(n, 1, UNITS):
                            pair, x = unit(i, u, 1)
                            for j in range(GROUPS[x][1]):
                                if ACC_AT[j] == t:
                                    e = GROUPS[x][0] + j
                                    wait(pool, done["part"], pair * EXPERTS + e + 1)
                                    if e == 0:
                                        wait(pool, done["turned"], pair)
                                    else:
                                        wait(pool, done["acc"], pair * EXPERTS + e)
                                    pool.tensor_tensor(acc[:, :], part[:, j, :], tile_of(H, pair) if e == 0 else acc[:, :], ALU.add).then_inc(done["acc"], 1)

            @block.vector
            def _(dve):
                def gating(i, u, j):
                    pair, x = unit(i, u, 1)
                    e = GROUPS[x][0] + j
                    wait(dve, gate_loaded[x], (pair + 1) * 32)
                    wait(dve, done["acc"], (pair if x else pair - 1) * EXPERTS + (BANK_BEFORE[e] + 1))
                    wait(dve, done["O"], pair * EXPERTS + e + 1)
                    dve.tensor_tensor(part[:, j, :], bk_o[j][:, :], gate[:, e, :], ALU.mult).then_inc(done["part"], 1)

                for n, u, i in pipeline(dve, UNITS, STAGES, RING, 2 * RING):
                    for t in range(max(TILES)):
                        if live(n, 0, UNITS) and t < TILES[u]:
                            at = TILE_AT[u] + t
                            rows = TILE_ROWS[at]
                            wait(dve, done["s"], i * PAIR_TILES + at + 1)
                            wait(dve, done["H3"], i * PAIR_TILES + at + 1)
                            old_pair, old = split_tile(i, at - SLOTS)
                            wait(dve, done["hi"], old_pair * PAIR_TILES + old + 1)
                            wait(dve, done[engine_of[old]], formed(engine_of[old], old_pair, old + 1))
                            dve.scalar_tensor_tensor(XN[0:rows, at % SLOTS, :], bk_h3[t % 2][0:rows, :], DOWN * HH_SCALE, s[0:rows, t % 2, :],
                                                     ALU.mult, ALU.mult).then_inc(done["hh"], 1)
                            low(dve, i, at - LO_LAG, "lo_d")
                        if isinstance(n, int) and n == UNITS and t == 0:
                            for x in range(PAIR_TILES - LO_LAG, PAIR_TILES):
                                low(dve, PAIRS - 1, x, "lo_d")
                        if live(n, 1, UNITS):
                            for j in range(GROUPS[unit(i, u, 1)[1]][1]):
                                if GATE_AT[j] == t:
                                    gating(i, u, j)


def lay_out(a):
    fixed = shape_constants()
    places = np.stack([a["L0_tok_instr_emb"][:SEQ], a["L0_tok_arg_emb"][:SEQ]])
    places = places.reshape(2 * BLK, P, D).transpose(1, 0, 2)
    w13 = np.stack([a["L0_ffn_w1"], a["L0_ffn_w3"]]).transpose(3, 0, 1, 2).reshape(D, 2, EXPERTS * HID)
    w2 = np.zeros((P, 2 * EXPERTS, D), np.float32)
    for (first, k), chunks in zip(GROUPS, CHUNKS):
        for j in range(k):
            w, at = a["L0_ffn_w2"][first + j].T, j * HID
            for half, (c, rows) in enumerate(chunks[j:j + 2]):
                low, high = max(c, at), min(c + rows, at + HID)
                w2[low - c:high - c, 2 * (first + j) + half] = w[low - at:high - at]
    ids_down = a["x"].reshape(PAIRS, 2, BLK, P).transpose(3, 0, 2, 1).reshape(P, PAIRS, BLK * 2)
    return {"ids": a["x"], "ids_down": np.ascontiguousarray(ids_down), "token_emb": a["L0_tok_token_emb"], "place_emb": np.ascontiguousarray(places),
            "weights": pack_weights(a), "w13": np.ascontiguousarray(w13), "w2": w2, **fixed}


def kernel(**inputs):
    import concourse.bacc as bacc
    from concourse.bass_utils import run_bass_kernel_spmd

    nc = bacc.Bacc("TRN2", target_bir_lowering=False, num_devices=1)
    arrays, args = {}, []
    for name, a in lay_out({k: np.asarray(v) for k, v in inputs.items()}).items():
        arrays[f"in_{name}"] = a = np.ascontiguousarray(a)
        args.append(nc.dram_tensor(f"in_{name}", a.shape, mybir.dt.from_np(a.dtype), kind="ExternalInput").ap())
    out = nc.dram_tensor("out_0", [ROWS, SEQ, D], F32, kind="ExternalOutput").ap()
    tower(nc, *args, out)
    return run_bass_kernel_spmd(nc, [arrays], core_ids=[0]).results[0]["out_0"]
```
